# Optimizing a Trainium2 kernel written in Bass

```python
import numpy as np
import jax
import jax.numpy as jnp

def _softmax(x, axis=-1):
    return jax.nn.softmax(x, axis=axis)

def _gelu(x):
    return jax.nn.gelu(x, approximate=True)

def _silu(x):
    return jax.nn.silu(x)

def _sigmoid(x):
    return jax.nn.sigmoid(x)

def _layernorm(x, axis=-1, eps=1e-05):
    m = jnp.mean(x, axis=axis, keepdims=True)
    v = jnp.var(x, axis=axis, keepdims=True)
    return (x - m) / jnp.sqrt(v + eps)

def _scatter_add(tgt, idx, src, axis=0):
    return tgt.at[idx].add(src)

def _segment_sum(src, seg, n):
    return jax.ops.segment_sum(src, seg, n)
kernel_name = 'mk_xattn_seq_d2_seqx_r4_8bc5f0'

def setup_inputs(seed: int=0):
    np.random.seed(seed)
    _w = jnp.asarray

    def _rec_inputs():
        import jax
        import jax.numpy as jnp
        _rk = jax.random.key(seed)
        x = -0.0002928 + 1 * jax.random.normal(jax.random.fold_in(_rk, 1), (16, 112, 256), jnp.float32)
        _lenS = 112 - jax.random.randint(jax.random.fold_in(_rk, 7), (16,), 0, max(1, 112 // 4) + 1, jnp.int32)
        _lenS2 = 375 - jax.random.randint(jax.random.fold_in(_rk, 8), (16,), 0, max(1, 375 // 4) + 1, jnp.int32)
        _ctx_768P = jax.random.normal(jax.random.fold_in(_rk, 11), (16, 16, 192), jnp.float32)
        _ctx_768c = jax.random.dirichlet(jax.random.fold_in(_rk, 511), 0.3 * jnp.ones((16,), jnp.float32), (16, 375))
        _ctx_768t = jnp.einsum('bsk,bkd->bsd', _ctx_768c, _ctx_768P)
        _ctx_768t = _ctx_768t * jax.lax.rsqrt(jnp.mean(jnp.square(_ctx_768t)) + 1e-12) * 0.953939
        ctx_768 = -0.00055796 + 0.999787 * (_ctx_768t + 0.3 * jax.random.normal(jax.random.fold_in(_rk, 611), (16, 375, 192), jnp.float32))
        return (x, ctx_768)
    x, ctx_768 = _rec_inputs()

    def _L0_xattn_setup():
        import jax, jax.numpy as jnp
        import numpy as np
        DEPTH = 4
        DIM = 256
        HEADS = 16
        DIM_HEAD = 64
        INNER = HEADS * DIM_HEAD
        MLP = 1024
        CTX = 192
        SCALE = DIM_HEAD ** (-0.5)
        EPS = 1e-05

        def _ln(x, g, b):
            mu = jnp.mean(x, axis=-1, keepdims=True)
            var = jnp.mean(jnp.square(x - mu), axis=-1, keepdims=True)
            return (x - mu) * jax.lax.rsqrt(var + EPS) * g + b

        def _heads(t):
            b, n, _ = t.shape
            return t.reshape(b, n, HEADS, DIM_HEAD).transpose(0, 2, 1, 3)

        def _mha(q, k, v):
            attn = jax.nn.softmax(jnp.einsum('bhqd,bhkd->bhqk', q, k) * SCALE, axis=-1)
            out = jnp.einsum('bhqk,bhkd->bhqd', attn, v)
            b, h, n, d = out.shape
            return out.transpose(0, 2, 1, 3).reshape(b, n, h * d)
        key = jax.random.key(seed)
        ks = jax.random.split(key, 12)

        def rn(k, shape, s=0.02):
            return jax.random.normal(k, shape, jnp.float32) * s
        return {'x': jax.random.normal(ks[0], (2, 512, DIM), jnp.float32), 'context': jax.random.normal(ks[1], (2, 256, CTX), jnp.float32), 'ln1_g': jnp.ones((DEPTH, DIM), jnp.float32), 'ln1_b': jnp.zeros((DEPTH, DIM), jnp.float32), 'w_qkv': rn(ks[2], (DEPTH, DIM, 3 * INNER)), 'w_sa_o': rn(ks[3], (DEPTH, INNER, DIM)), 'b_sa_o': jnp.zeros((DEPTH, DIM), jnp.float32), 'ln2_g': jnp.ones((DEPTH, DIM), jnp.float32), 'ln2_b': jnp.zeros((DEPTH, DIM), jnp.float32), 'w_q': rn(ks[4], (DEPTH, DIM, INNER)), 'w_kv': rn(ks[5], (DEPTH, CTX, 2 * INNER)), 'w_ca_o': rn(ks[6], (DEPTH, INNER, DIM)), 'b_ca_o': jnp.zeros((DEPTH, DIM), jnp.float32), 'ln3_g': jnp.ones((DEPTH, DIM), jnp.float32), 'ln3_b': jnp.zeros((DEPTH, DIM), jnp.float32), 'w_ff1': rn(ks[7], (DEPTH, DIM, MLP)), 'b_ff1': jnp.zeros((DEPTH, MLP), jnp.float32), 'w_ff2': rn(ks[8], (DEPTH, MLP, DIM)), 'b_ff2': jnp.zeros((DEPTH, DIM), jnp.float32)}
    _L0_xattn_all = _L0_xattn_setup()
    _L0_xattn_in = {k: v for k, v in _L0_xattn_all.items() if k in ('ln1_g', 'ln1_b', 'w_qkv', 'w_sa_o', 'b_sa_o', 'ln2_g', 'ln2_b', 'w_q', 'w_kv', 'w_ca_o', 'b_ca_o', 'ln3_g', 'ln3_b', 'w_ff1', 'b_ff1', 'w_ff2', 'b_ff2')}
    del _L0_xattn_all

    def _L1_xattn_setup():
        import jax, jax.numpy as jnp
        import numpy as np
        LN_EPS = 1e-05

        def _ln(x, g, b):
            m = jnp.mean(x, axis=-1, keepdims=True)
            v = jnp.mean((x - m) ** 2, axis=-1, keepdims=True)
            return (x - m) / jnp.sqrt(v + LN_EPS) * g + b
        key = jax.random.key(seed)
        ks = jax.random.split(key, 8)
        B, N, S, D, T = (16, 64, 512, 256, 192)

        def xavier(k, shape):
            fan_in, fan_out = shape
            lim = (6.0 / (fan_in + fan_out)) ** 0.5
            return jax.random.uniform(k, shape, minval=-lim, maxval=lim, dtype=jnp.float32)
        return {'prev_states': jax.random.normal(ks[0], (B, N, D), dtype=jnp.float32), 'input_tokens': jax.random.normal(ks[1], (B, S, T), dtype=jnp.float32), 'W_proj': xavier(ks[2], (T, D)), 'b_proj': jnp.zeros((D,), jnp.float32), 'g_state': jnp.ones((D,), jnp.float32), 'beta_state': jnp.zeros((D,), jnp.float32), 'g_input': jnp.ones((D,), jnp.float32), 'beta_input': jnp.zeros((D,), jnp.float32), 'g_out': jnp.ones((D,), jnp.float32), 'beta_out': jnp.zeros((D,), jnp.float32), 'W_u': xavier(ks[3], (2 * D, D)), 'b_u': jnp.full((D,), -1.0, jnp.float32), 'W_r': xavier(ks[4], (2 * D, D)), 'b_r': jnp.zeros((D,), jnp.float32), 'W_n': xavier(ks[5], (2 * D, D)), 'b_n': jnp.zeros((D,), jnp.float32)}
    _L1_xattn_all = _L1_xattn_setup()
    _L1_xattn_in = {k: v for k, v in _L1_xattn_all.items() if k in ('W_proj', 'b_proj', 'g_state', 'beta_state', 'g_input', 'beta_input', 'g_out', 'beta_out', 'W_u', 'b_u', 'W_r', 'b_r', 'W_n', 'b_n')}
    del _L1_xattn_all
    return {'x': x, 'ctx_768': ctx_768, 'L0_xattn_ln1_g': _L0_xattn_in['ln1_g'], 'L0_xattn_ln1_b': _L0_xattn_in['ln1_b'], 'L0_xattn_w_qkv': _L0_xattn_in['w_qkv'], 'L0_xattn_w_sa_o': _L0_xattn_in['w_sa_o'], 'L0_xattn_b_sa_o': _L0_xattn_in['b_sa_o'], 'L0_xattn_ln2_g': _L0_xattn_in['ln2_g'], 'L0_xattn_ln2_b': _L0_xattn_in['ln2_b'], 'L0_xattn_w_q': _L0_xattn_in['w_q'], 'L0_xattn_w_kv': _L0_xattn_in['w_kv'], 'L0_xattn_w_ca_o': _L0_xattn_in['w_ca_o'], 'L0_xattn_b_ca_o': _L0_xattn_in['b_ca_o'], 'L0_xattn_ln3_g': _L0_xattn_in['ln3_g'], 'L0_xattn_ln3_b': _L0_xattn_in['ln3_b'], 'L0_xattn_w_ff1': _L0_xattn_in['w_ff1'], 'L0_xattn_b_ff1': _L0_xattn_in['b_ff1'], 'L0_xattn_w_ff2': _L0_xattn_in['w_ff2'], 'L0_xattn_b_ff2': _L0_xattn_in['b_ff2'], 'L1_xattn_W_proj': _L1_xattn_in['W_proj'], 'L1_xattn_b_proj': _L1_xattn_in['b_proj'], 'L1_xattn_g_state': _L1_xattn_in['g_state'], 'L1_xattn_beta_state': _L1_xattn_in['beta_state'], 'L1_xattn_g_input': _L1_xattn_in['g_input'], 'L1_xattn_beta_input': _L1_xattn_in['beta_input'], 'L1_xattn_g_out': _L1_xattn_in['g_out'], 'L1_xattn_beta_out': _L1_xattn_in['beta_out'], 'L1_xattn_W_u': _L1_xattn_in['W_u'], 'L1_xattn_b_u': _L1_xattn_in['b_u'], 'L1_xattn_W_r': _L1_xattn_in['W_r'], 'L1_xattn_b_r': _L1_xattn_in['b_r'], 'L1_xattn_W_n': _L1_xattn_in['W_n'], 'L1_xattn_b_n': _L1_xattn_in['b_n']}

def reference(x, ctx_768, L0_xattn_ln1_g, L0_xattn_ln1_b, L0_xattn_w_qkv, L0_xattn_w_sa_o, L0_xattn_b_sa_o, L0_xattn_ln2_g, L0_xattn_ln2_b, L0_xattn_w_q, L0_xattn_w_kv, L0_xattn_w_ca_o, L0_xattn_b_ca_o, L0_xattn_ln3_g, L0_xattn_ln3_b, L0_xattn_w_ff1, L0_xattn_b_ff1, L0_xattn_w_ff2, L0_xattn_b_ff2, L1_xattn_W_proj, L1_xattn_b_proj, L1_xattn_g_state, L1_xattn_beta_state, L1_xattn_g_input, L1_xattn_beta_input, L1_xattn_g_out, L1_xattn_beta_out, L1_xattn_W_u, L1_xattn_b_u, L1_xattn_W_r, L1_xattn_b_r, L1_xattn_W_n, L1_xattn_b_n):
    import jax
    import jax.numpy as jnp

    def _L0_xattn_ref(x, context, ln1_g, ln1_b, w_qkv, w_sa_o, b_sa_o, ln2_g, ln2_b, w_q, w_kv, w_ca_o, b_ca_o, ln3_g, ln3_b, w_ff1, b_ff1, w_ff2, b_ff2):
        import jax, jax.numpy as jnp
        import numpy as np
        DEPTH = 4
        DIM = 256
        HEADS = 16
        DIM_HEAD = 64
        INNER = HEADS * DIM_HEAD
        MLP = 1024
        CTX = 192
        SCALE = DIM_HEAD ** (-0.5)
        EPS = 1e-05

        def _ln(x, g, b):
            mu = jnp.mean(x, axis=-1, keepdims=True)
            var = jnp.mean(jnp.square(x - mu), axis=-1, keepdims=True)
            return (x - mu) * jax.lax.rsqrt(var + EPS) * g + b

        def _heads(t):
            b, n, _ = t.shape
            return t.reshape(b, n, HEADS, DIM_HEAD).transpose(0, 2, 1, 3)

        def _mha(q, k, v):
            attn = jax.nn.softmax(jnp.einsum('bhqd,bhkd->bhqk', q, k) * SCALE, axis=-1)
            out = jnp.einsum('bhqk,bhkd->bhqd', attn, v)
            b, h, n, d = out.shape
            return out.transpose(0, 2, 1, 3).reshape(b, n, h * d)
        for i in range(DEPTH):
            h = _ln(x, ln1_g[i], ln1_b[i])
            qkv = h @ w_qkv[i]
            q, k, v = jnp.split(qkv, 3, axis=-1)
            sa = _mha(_heads(q), _heads(k), _heads(v)) @ w_sa_o[i] + b_sa_o[i]
            x = sa + x
            h = _ln(x, ln2_g[i], ln2_b[i])
            q = h @ w_q[i]
            kv = context @ w_kv[i]
            k, v = jnp.split(kv, 2, axis=-1)
            ca = _mha(_heads(q), _heads(k), _heads(v)) @ w_ca_o[i] + b_ca_o[i]
            x = ca + x
            h = _ln(x, ln3_g[i], ln3_b[i])
            ff = jax.nn.gelu(h @ w_ff1[i] + b_ff1[i], approximate=False) @ w_ff2[i] + b_ff2[i]
            x = ff + x
        return x

    def _L1_xattn_ref(prev_states, input_tokens, W_proj, b_proj, g_state, beta_state, g_input, beta_input, g_out, beta_out, W_u, b_u, W_r, b_r, W_n, b_n):
        import jax, jax.numpy as jnp
        import numpy as np
        LN_EPS = 1e-05

        def _ln(x, g, b):
            m = jnp.mean(x, axis=-1, keepdims=True)
            v = jnp.mean((x - m) ** 2, axis=-1, keepdims=True)
            return (x - m) / jnp.sqrt(v + LN_EPS) * g + b
        D = prev_states.shape[-1]
        tok = input_tokens @ W_proj + b_proj
        scores = jnp.einsum('bnd,bsd->bns', prev_states, tok) / jnp.sqrt(jnp.float32(D))
        attn = jax.nn.softmax(scores, axis=-1)
        routed = jnp.einsum('bns,bsd->bnd', attn, tok)
        ps_n = _ln(prev_states, g_state, beta_state)
        in_n = _ln(routed, g_input, beta_input)
        concat = jnp.concatenate([ps_n, in_n], axis=-1)
        u = jax.nn.sigmoid(concat @ W_u + b_u)
        r = jax.nn.sigmoid(concat @ W_r + b_r)
        reset_in = jnp.concatenate([r * ps_n, in_n], axis=-1)
        cand = jnp.tanh(reset_in @ W_n + b_n)
        new_state = (1.0 - u) * prev_states + u * cand
        return _ln(new_state, g_out, beta_out)
    x = _L0_xattn_ref(x, ctx_768, L0_xattn_ln1_g, L0_xattn_ln1_b, L0_xattn_w_qkv, L0_xattn_w_sa_o, L0_xattn_b_sa_o, L0_xattn_ln2_g, L0_xattn_ln2_b, L0_xattn_w_q, L0_xattn_w_kv, L0_xattn_w_ca_o, L0_xattn_b_ca_o, L0_xattn_ln3_g, L0_xattn_ln3_b, L0_xattn_w_ff1, L0_xattn_b_ff1, L0_xattn_w_ff2, L0_xattn_b_ff2)
    x = _L1_xattn_ref(x, ctx_768, L1_xattn_W_proj, L1_xattn_b_proj, L1_xattn_g_state, L1_xattn_beta_state, L1_xattn_g_input, L1_xattn_beta_input, L1_xattn_g_out, L1_xattn_beta_out, L1_xattn_W_u, L1_xattn_b_u, L1_xattn_W_r, L1_xattn_b_r, L1_xattn_W_n, L1_xattn_b_n)
    return x

_drawn_inputs = setup_inputs


def setup_inputs(seed=0):
    import zlib

    import numpy as np

    out = dict(_drawn_inputs(seed))
    spreads = {'L0_xattn_ln1_g': (1.0, 0.6),
     'L0_xattn_ln1_b': (0.0, 0.1),
     'L0_xattn_b_sa_o': (0.0, 0.1),
     'L0_xattn_ln2_g': (1.0, 0.6),
     'L0_xattn_ln2_b': (0.0, 0.8),
     'L0_xattn_b_ca_o': (0.0, 0.1),
     'L0_xattn_ln3_g': (1.0, 0.2),
     'L0_xattn_ln3_b': (0.0, 0.37),
     'L0_xattn_b_ff1': (0.0, 0.1),
     'L0_xattn_b_ff2': (0.0, 0.1),
     'L1_xattn_b_proj': (0.0, 0.1),
     'L1_xattn_g_state': (1.0, 0.2),
     'L1_xattn_beta_state': (0.0, 0.295),
     'L1_xattn_g_input': (1.0, 0.2),
     'L1_xattn_beta_input': (0.0, 0.1),
     'L1_xattn_g_out': (1.0, 0.2),
     'L1_xattn_beta_out': (0.0, 0.1),
     'L1_xattn_b_u': (-1.0, 0.2),
     'L1_xattn_b_r': (0.0, 0.8),
     'L1_xattn_b_n': (0.0, 0.1)}
    factors = {'L0_xattn_w_q': 8.0}
    for name, (base, spread) in spreads.items():
        noise = np.random.default_rng([zlib.crc32(name.encode()), seed]).standard_normal(out[name].shape)
        drawn = base * np.exp(spread * noise) if base else spread * noise
        out[name] = jnp.asarray(drawn.astype(out[name].dtype))
    for name, factor in factors.items():
        out[name] = (out[name] * factor).astype(out[name].dtype)
    return out
```

```python
import concourse.bass as bass
from concourse import mybir
from contextlib import ExitStack

INPUTS = ['x', 'ctx_768',
          'L0_xattn_ln1_g', 'L0_xattn_ln1_b', 'L0_xattn_w_qkv', 'L0_xattn_w_sa_o', 'L0_xattn_b_sa_o',
          'L0_xattn_ln2_g', 'L0_xattn_ln2_b', 'L0_xattn_w_q', 'L0_xattn_w_kv', 'L0_xattn_w_ca_o', 'L0_xattn_b_ca_o',
          'L0_xattn_ln3_g', 'L0_xattn_ln3_b', 'L0_xattn_w_ff1', 'L0_xattn_b_ff1', 'L0_xattn_w_ff2', 'L0_xattn_b_ff2',
          'L1_xattn_W_proj', 'L1_xattn_b_proj', 'L1_xattn_g_state', 'L1_xattn_beta_state',
          'L1_xattn_g_input', 'L1_xattn_beta_input', 'L1_xattn_g_out', 'L1_xattn_beta_out',
          'L1_xattn_W_u', 'L1_xattn_b_u', 'L1_xattn_W_r', 'L1_xattn_b_r', 'L1_xattn_W_n', 'L1_xattn_b_n']


def xattn_stack_kernel(nc, x, ctx_768, ln1_g, ln1_b, w_qkv, w_sa_o, b_sa_o, ln2_g, ln2_b, w_q, w_kv, w_ca_o, b_ca_o,
                       ln3_g, ln3_b, w_ff1, b_ff1, w_ff2, b_ff2, W_proj, b_proj, g_state, beta_state,
                       g_input, beta_input, g_out, beta_out, W_u, b_u, W_r, b_r, W_n, b_n, out):
    f32 = mybir.dt.float32
    f32r = mybir.dt.float32r
    ALU = mybir.AluOpType
    ACT = mybir.ActivationFunctionType
    AX = mybir.AxisListType
    ds = bass.ds

    B, T, D = x.shape
    S, C = ctx_768.shape[1:]
    L = w_qkv.shape[0]
    INNER = w_q.shape[2]
    DH = 64
    H = INNER // DH
    HP = H // 2
    SP = S + S % 2
    KT = 3
    KC = S // KT
    CL = C - 128
    PAIRS = B // 2
    T2 = 2 * T
    BLK = 1024
    SCALE = DH ** -0.5
    SCALE_OUT = float(D) ** -0.5
    EPS = 1e-5
    PHASES = 3

    SA_J, CA_J, FF_J, L1_J = 20, 40, 8, 18

    ctx = ExitStack()
    with ctx:
        def sb(name, shape, dt=f32):
            return ctx.enter_context(nc.sbuf_tensor(name, shape, dt))

        def sem(name):
            return ctx.enter_context(nc.semaphore(name))

        X = sb("X", [T, B, D])
        WH = sb("WH", [128, 8 * BLK], f32r)
        WL = sb("WL", [128, 8 * BLK], f32r)
        stage = sb("stage", [128, 2, BLK])
        zeros = sb("zeros", [128, BLK // 2])
        hTf = sb("hTf", [128, 2, T2])
        hTh = sb("hTh", [128, 2, T2], f32r)
        hTl = sb("hTl", [128, 2, T2], f32r)
        xn = sb("xn", [T, 2, D])
        bst = sb("bst", [T, 2, 6])
        mv = sb("mv", [T, 2, 2])
        vare = sb("vare", [T, 2])
        rstd = sb("rstd", [T, 2])
        mhalf = sb("mhalf", [128, 2])
        qT = sb("qT", [128, HP, T2])
        kz = sb("kz", [128, HP, 2, T2])
        V = sb("V", [128, 2, KT * INNER])
        qzh = sb("qzh", [128, 2, 2, T], f32r)
        qzl = sb("qzl", [128, 2, 2, T], f32r)
        Kh = sb("Kh", [128, 2, SP], f32r)
        Kl = sb("Kl", [128, 2, SP], f32r)
        CT = sb("CT", [128, 2, 3, SP], f32r)
        P = sb("P", [T, 2, 4 * T])
        PT = sb("PT", [128, 2, 4 * T])
        rs = sb("rs", [T, 2, H])
        rinv = sb("rinv", [T, 2, HP])
        mx = sb("mx", [T, 2, 4])
        spare = sb("spare", [T, 1])
        nb = sb("nb", [T, 2, 4])
        O = sb("O", [T, 2, 8 * DH])
        Gh = sb("Gh", [128, 8, T2], f32r)
        Gl = sb("Gl", [128, 8, T2], f32r)
        ident = sb("ident", [128, 128])
        prow = sb("prow", [128, 128])
        pcol = sb("pcol", [128, 128])
        OB = sb("OB", [T, L * PHASES, D])
        hcols = sb("hcols", [128, 4])
        BP = sb("BP", [KC, D])
        GO = sb("GO", [T, 2, D])

        LNV = 2 * L + 2
        FF_V = 6 * LNV
        L1_V = FF_V + 8 * L
        cols = pcol[:, L1_V:L1_V + 12]

        OTh = Gh[:, 0:4, :].rearrange("p f (a t) -> p (f a) t", a=2)
        OTl = Gl[:, 0:4, :].rearrange("p f (a t) -> p (f a) t", a=2)
        Gf = V[:, 0, 0:8 * T2].rearrange("p (f t) -> p f t", f=8)
        craw = V[0:KC, :, 0:KT * C].rearrange("p b (t c) -> p b t c", t=KT)
        tokT = kz[:, 0:4, :, :].rearrange("p a b c -> p (a b c)")[:, 0:2 * SP].rearrange("p (m s) -> p m s", m=2)
        tok = V[0:KC, 0, 0:KT * D].rearrange("p (t d) -> p t d", t=KT)
        xT = qT[:, 0:2, :]
        uT = qT[:, 2:4, :]
        rT = qT[:, 4:6, :]
        cT = qT[:, 6:8, :]
        inT = kz[:, 4:5, :, :].rearrange("p a m t -> p (a m) t")
        nsT = kz[:, 5:6, :, :].rearrange("p a m t -> p (a m) t")
        rp = kz[:, 6:7, :, :].rearrange("p a m t -> p (a m) t")
        inTh, inTl = Gh[:, 0:2, :], Gl[:, 0:2, :]
        rph, rpl = Gh[:, 2:4, :], Gl[:, 2:4, :]
        xs = V[0:T, 0, 1024:1024 + 2 * D].rearrange("p (b d) -> p b d", b=2)
        routed = V[0:T, 0, 2048:2048 + 2 * D].rearrange("p (b d) -> p b d", b=2)
        y = V[0:T, 1, 0:2 * D].rearrange("p (b d) -> p b d", b=2)
        yn = V[0:T, 1, 1024:1024 + 2 * D].rearrange("p (b d) -> p b d", b=2)

        def bank(name):
            return ctx.enter_context(nc.psum_tensor(name, [128, 512], f32))

        PJ = [bank(f"proj{i}") for i in range(2)]
        SC = [bank(f"scores{i}") for i in range(2)]
        TR = [bank(f"probsT{i}") for i in range(2)]
        OA = [bank(f"attn{i}") for i in range(2)]

        ctxT = nc.dram_tensor("ctxT_scratch", (B, 128, 3 * SP), f32).ap()

        consts_set = sem("consts_set")
        params_in = sem("params_in")
        params_turned = sem("params_turned")
        stage_in = [sem(f"stage_in{i}") for i in range(2)]
        w_split = [sem(f"w_split{i}") for i in range(2)]
        w_high = sem("w_high")
        ctx_raw_in = [sem(f"ctx_raw_in{i}") for i in range(2)]
        ctx_turned = sem("ctx_turned")
        ctx_high = sem("ctx_high")
        ctx_split = [sem(f"ctx_split{i}") for i in range(2)]
        ctx_stored = [sem(f"ctx_stored{i}") for i in range(2)]
        ctx_in = [sem(f"ctx_in{i}") for i in range(2)]
        ln_var = sem("ln_var")
        ln_rstd = sem("ln_rstd")
        ln_xn = sem("ln_xn")
        ln_turned = sem("ln_turned")
        first_affine = sem("first_affine")
        ln_high = sem("ln_high")
        ln_low = sem("ln_low")

        def group(prefix, names, pairs=()):
            return {**{n: sem(f"{prefix}_{n}") for n in names},
                    **{n: [sem(f"{prefix}_{n}{i}") for i in range(2)] for n in pairs}}

        sa = group("sa", ["qk_ready", "v_ready", "s_ready", "nb_ready", "exp_done", "t_ready", "o_ready",
                          "ot_ready", "ot_high", "y_ready", "dve_step"], ["pj_done", "pt_done", "o_done"])
        ca = group("ca", ["q_ready", "v_ready", "k_high", "s_ready", "nb_ready", "exp_done", "t_ready", "o_ready",
                          "ot_ready", "ot_high", "y_ready", "dve_step", "qz_done"],
                   ["pj_done", "pt_done", "o_done", "k_ready"])
        ff = group("ff", ["f_ready", "g_split", "y_ready", "dve_step"], ["pj_done"])
        l1 = group("l1", ["xs_done", "x_ready", "tok_ready", "s_ready", "nb_ready", "exp_done", "t_ready", "o_ready",
                          "norm", "var", "rstd", "in_ready", "in_high", "in_low", "g_ready", 
                          "rp_split", "ns_done", "out_ready", "y_done", "y_stored", "dve_step"],
                   ["pj_done", "pt_done"])
        first_step = sem("first_step")

        PRIME = 1
        primed = [*w_split, ctx_turned, *ctx_split, *ctx_stored, *ca["k_ready"], ca["y_ready"], ff["y_ready"], ff["f_ready"],
                  sa["y_ready"], sa["v_ready"], ca["q_ready"], ca["v_ready"], ca["qz_done"], *sa["pj_done"], *sa["pt_done"], *sa["o_done"],
                  sa["exp_done"], *ca["pj_done"], *ca["pt_done"], *ca["o_done"], ca["exp_done"], *ff["pj_done"], *l1["pj_done"],
                  *l1["pt_done"], l1["y_stored"]]

        class Steps:

            def __init__(self, eng, s, base, per):
                self.eng, self.s, self.base, self.per, self.n = eng, s, base, per, 0

            def __call__(self, ins, before_aggr=False):
                self.n += 1
                ins.then_inc(self.s, 1)
                self.eng.wait_ge(self.s, self.base + self.n)
                if before_aggr:
                    nc.vector.tensor_copy(spare[:, :], mhalf[0:T, 0:1])

            def close(self):
                assert self.n == self.per, (self.n, self.per)

        def rows_of(w, k, c0, n):
            return lambda lay, h: w[ds(lay, 1), k * 128 + 64 * h:k * 128 + 64 * h + 64, c0:c0 + n].rearrange(
                "l p n -> (l p) n")

        def tiles_of(w, k0, n=4):
            return lambda lay, h: w[ds(lay, 1), k0 * 128:(k0 + n) * 128, :].rearrange(
                "l (k p) n -> p (l k) n", p=128)[64 * h:64 * h + 64]

        def last_rows_of(w, c0, n):
            return lambda lay, h: w[ds(lay, 1), 128:128 + CL, c0:c0 + n].rearrange("l p n -> (l p) n")

        SA_BLOCKS = [(2, rows_of(w_qkv, 0, INNER, BLK)), (4, rows_of(w_qkv, 0, 2 * INNER, BLK)),
                     (6, tiles_of(w_sa_o, 0)), (7, tiles_of(w_sa_o, 4)),
                     (0, rows_of(w_qkv, 0, 0, BLK)), (1, rows_of(w_qkv, 1, 0, BLK)),
                     (3, rows_of(w_qkv, 1, INNER, BLK)), (5, rows_of(w_qkv, 1, 2 * INNER, BLK))]
        CA_BLOCKS = [(0, rows_of(w_q, 0, 0, BLK)), (1, rows_of(w_q, 1, 0, BLK)),
                     (3, rows_of(w_kv, 0, INNER, BLK)), (5, last_rows_of(w_kv, INNER, BLK)),
                     (2, rows_of(w_kv, 0, 0, BLK)), (4, last_rows_of(w_kv, 0, BLK)),
                     (6, tiles_of(w_ca_o, 0)), (7, tiles_of(w_ca_o, 4))]
        FF_BLOCKS = [(0, rows_of(w_ff1, 0, 0, BLK)), (1, rows_of(w_ff1, 1, 0, BLK)),
                     (3, tiles_of(w_ff2, 0)), (5, tiles_of(w_ff2, 4))]
        flat = lambda w: w.rearrange("(k p) n -> p k n", p=128)
        L1_BLOCKS = [(2, BLK, lambda h: flat(W_u)[64 * h:64 * h + 64]), (4, BLK, lambda h: flat(W_r)[64 * h:64 * h + 64]),
                     (6, BLK, lambda h: flat(W_n)[64 * h:64 * h + 64]),
                     (7, D, lambda h: W_proj[64 * h:64 * h + 64, :]), (0, D, lambda h: W_proj[128:128 + CL, :])]
        PER_LAYER = len(SA_BLOCKS) + len(CA_BLOCKS) + len(FF_BLOCKS)

        def wcol(blk, off, n):
            return slice(blk * BLK + off, blk * BLK + off + n)

        def split_at(count):
            return count % 2, count // 2 + 1

        block = ctx.enter_context(nc.Block())

        @block.sync
        def _(sp):
            def load_block(n, cols_n, src, done_before):
                sp.wait_ge(w_split[n % 2], PRIME + done_before)
                for h in (1, 0):
                    dst = stage[64 * h:64 * h + 64, n % 2, 0:cols_n]
                    a = src(h)
                    if len(a.shape) == 3:
                        dst = dst.rearrange("p (k n) -> p k n", k=a.shape[1])
                    sp.dma_start(dst, a).then_inc(stage_in[n % 2], 16)

            sp.wait_ge(consts_set, 9)
            sp.dma_start(X[:, :, :], x.rearrange("b t d -> t b d")).then_inc(params_in, 16)
            for n, v in enumerate((ln1_g, ln1_b, ln2_g, ln2_b, ln3_g, ln3_b)):
                sp.dma_start(prow[n * LNV:n * LNV + 2 * L, :], v.rearrange("l (k p) -> (l k) p", p=128)) \
                    .then_inc(params_in, 16)
            for n, v in enumerate((g_state, beta_state)):
                sp.dma_start(prow[n * LNV + 2 * L:n * LNV + 2 * L + 2, :], v.rearrange("(k p) -> k p", p=128)) \
                    .then_inc(params_in, 16)
            sp.dma_start(prow[FF_V:FF_V + L * 8, :], b_ff1.rearrange("l (f p) -> (l f) p", p=128)) \
                .then_inc(params_in, 16)
            for n, v in enumerate((g_input, beta_input, b_proj, b_u, b_r, b_n)):
                sp.dma_start(prow[L1_V + 2 * n:L1_V + 2 * n + 2, :], v.rearrange("(k p) -> k p", p=128)) \
                    .then_inc(params_in, 16)
            for ph, b in enumerate((b_sa_o, b_ca_o, b_ff2)):
                sp.dma_start(OB[:, ph:(L - 1) * PHASES + ph + 1:PHASES, :], b.partition_broadcast(T)) \
                    .then_inc(params_in, 16)
            sp.dma_start(BP[:, :], b_proj.partition_broadcast(KC)).then_inc(params_in, 16)
            sp.dma_start(GO[:, 0, :], g_out.partition_broadcast(T)).then_inc(params_in, 16)
            sp.dma_start(GO[:, 1, :], beta_out.partition_broadcast(T)).then_inc(params_in, 16)

            for s in primed:
                sp.sem_inc(s, PRIME)

            with sp.Fori(0, PAIRS) as i:
                for b in range(2):
                    sp.wait_ge(ctx_turned, PRIME + 2 * i + b)
                    sp.dma_start(craw[:, b, :, :], ctx_768[ds(2 * i + b, 1), :, :].rearrange(
                        "o (t p) c -> p (o t) c", p=KC)).then_inc(ctx_raw_in[b], 16)
                for b in range(2):
                    sp.wait_ge(ctx_split[b], PRIME + i + 1)
                    sp.dma_start(ctxT[ds(2 * i + b, 1), :, :].rearrange("o p n -> p (o n)"),
                                 CT[:, b, :, :].rearrange("p a s -> p (a s)").bitcast(f32)).then_inc(ctx_stored[b], 16)

            def load_ctx(pair, b):
                sp.dma_start(CT[:, b, :, :].rearrange("p a s -> p (a s)").bitcast(f32),
                             ctxT[ds(2 * pair + b, 1), :, :].rearrange("o p n -> p (o n)")).then_inc(ctx_in[b], 16)

            for b in range(2):
                sp.wait_ge(ctx_stored[0], PRIME + 16 * PAIRS)
                sp.wait_ge(ctx_stored[1], PRIME + 16 * PAIRS)
                load_ctx(0, b)

            with sp.Fori(0, L) as lay:
                n = 0
                for blocks in (SA_BLOCKS, CA_BLOCKS):
                    for blk, src in blocks:
                        load_block(n, BLK, lambda h: src(lay, h), lay * (PER_LAYER // 2) + n // 2)
                        n += 1
                with sp.Fori(0, PAIRS) as pair:
                    it = lay * PAIRS + pair
                    for b in range(2):
                        sp.wait_ge(ca["k_ready"][b], PRIME + (it + 1) * HP)
                        load_ctx((pair + 1) % PAIRS, b)
                for blk, src in FF_BLOCKS:
                    load_block(n, BLK, lambda h: src(lay, h), lay * (PER_LAYER // 2) + n // 2)
                    n += 1
            for m, (blk, cn, src) in enumerate(L1_BLOCKS):
                load_block(m, cn, src, L * PER_LAYER // 2 + m // 2)
            with sp.Fori(0, PAIRS) as pair:
                for b in range(2):
                    sp.wait_ge(l1["tok_ready"], pair * 8 + 4 * b + 4)
                    load_ctx((pair + 1) % PAIRS, b)
                for b in range(2):
                    sp.wait_ge(l1["y_done"], pair * 2 + b + 1)
                    sp.dma_start(out[ds(2 * pair + b, 1), :, :].rearrange("o t d -> t (o d)"), y[:, b, :]) \
                        .then_inc(l1["y_stored"], 16)
            sp.wait_ge(l1["y_stored"], PRIME + 16 * B)
            for b in range(2):
                sp.wait_ge(ctx_in[b], 16 * (1 + (L + 1) * PAIRS))

        @block.gpsimd
        def _(pool):
            nc.gpsimd.memset(zeros[:, :], 0.0).then_inc(consts_set, 1)
            nc.gpsimd.memset(mhalf[:, :], -0.5).then_inc(consts_set, 1)
            nc.gpsimd.memset(prow[:, :], 0.0).then_inc(consts_set, 1)
            nc.gpsimd.memset(kz[:, :, :, :], 0.0).then_inc(consts_set, 1)
            nc.gpsimd.memset(qzh[:, :, :, :].bitcast(f32), 0.0).then_inc(consts_set, 1)
            nc.gpsimd.memset(qzl[:, :, :, :].bitcast(f32), 0.0).then_inc(consts_set, 1)
            nc.gpsimd.memset(CT[:, :, :, S:SP].bitcast(f32), 0.0).then_inc(consts_set, 1)
            nc.gpsimd.memset(ident[:, :], 0.0).then_inc(consts_set, 1)
            pool.wait_ge(consts_set, 8)
            nc.gpsimd.affine_select(out=ident[:, :], in_=ident[:, :], compare_op=ALU.not_equal, fill=1.0,
                                    base=0, pattern=[[-1, 128]], channel_multiplier=1).then_inc(consts_set, 1)
            pool.wait_ge(consts_set, 9)

            def split_block(n, blk, cols_n, loaded, high, before):
                pool.wait_ge(stage_in[n % 2], loaded)
                pool.wait_ge(w_split[(n + 1) % 2], PRIME + before)
                half = min(cols_n, BLK // 2)
                for c in range(0, cols_n, half):
                    nc.gpsimd.tensor_tensor(WH[:, wcol(blk, c, half)], stage[:, n % 2, c:c + half],
                                            zeros[:, 0:half], ALU.add).then_inc(w_high, 1)
                pool.wait_ge(w_high, high)
                nc.gpsimd.tensor_tensor(WL[:, wcol(blk, 0, cols_n)], stage[:, n % 2, 0:cols_n],
                                        WH[:, wcol(blk, 0, cols_n)].bitcast(f32), ALU.subtract) \
                    .then_inc(w_split[n % 2], 1)

            def layer_blocks(blocks, n0, lay, free, powers):
                pool.wait_ge(ln_rstd, powers)
                for m, (blk, _) in enumerate(blocks):
                    n = n0 + m
                    for s, v in free(blk):
                        pool.wait_ge(s, PRIME + v)
                    split_block(n, blk, BLK, 32 * (lay * (PER_LAYER // 2) + n // 2 + 1),
                                2 * (lay * PER_LAYER + n + 1), lay * (PER_LAYER // 2) + (n + 1) // 2)

            def power(event, src, dst, ready, done, per=1):
                pool.wait_ge(ready, event)
                nc.gpsimd.tensor_tensor(dst, src, mhalf[0:T, 0:2], ALU.pow).then_inc(done, 1)

            power(1, vare[:, :], rstd[:, :], ln_var, ln_rstd)
            with pool.Fori(0, L) as lay:
                def sa_free(blk):
                    if blk in (2, 4):
                        return [(ca["k_ready"][1], lay * (PAIRS * HP))]
                    if blk in (6, 7):
                        return [(ca["y_ready"], lay * (PAIRS * 2))]
                    if blk in (0, 1):
                        return [(ff["f_ready"], lay * (PAIRS * 4))]
                    return [(ff["y_ready"], lay * (PAIRS * 2))]

                def ca_free(blk):
                    if blk in (6, 7):
                        return [(sa["y_ready"], (lay + 1) * (PAIRS * 2))]
                    return [(sa["v_ready"], (lay + 1) * (PAIRS * 4))]

                def ff_free(blk):
                    return [(ca["q_ready"], (lay + 1) * (PAIRS * 4)) if blk < 2 else
                            (ca["v_ready"], (lay + 1) * (PAIRS * 12))]

                layer_blocks(SA_BLOCKS, 0, lay, sa_free, lay * (PHASES * PAIRS) + 1)
                with pool.Fori(0, PAIRS) as pair:
                    pool.wait_ge(w_split[1], PRIME + lay * (PER_LAYER // 2) + 4)
                    pool.wait_ge(ln_rstd, lay * (PHASES * PAIRS) + pair + 1)
                    power(lay * (PHASES * PAIRS) + pair + 2, vare[:, :], rstd[:, :], ln_var, ln_rstd)
                layer_blocks(CA_BLOCKS, 8, lay, ca_free, lay * (PHASES * PAIRS) + PAIRS + 1)
                with pool.Fori(0, PAIRS) as pair:
                    pool.wait_ge(w_split[1], PRIME + lay * (PER_LAYER // 2) + 8)
                    it = lay * PAIRS + pair
                    for hp in range(2 * HP):
                        b, h2 = hp // HP, hp % HP
                        if hp == 0:
                            for i in range(2):
                                pool.wait_ge(ca["pj_done"][i], PRIME + it * (CA_J // 2) + 2)
                        if hp >= 2:
                            pool.wait_ge(ca["s_ready"], it * (2 * H) + 2 * hp - 2)
                        pool.wait_ge(ca["qz_done"], PRIME + it * (8 * HP) + 4 * hp)
                        for a in range(2):
                            src = qT[64 * a:64 * a + 64, h2, b * T:(b + 1) * T]
                            nc.gpsimd.tensor_tensor(qzh[64 * a:64 * a + 64, hp % 2, a, :], src,
                                                    zeros[64 * a:64 * a + 64, 0:T], ALU.add).then_inc(ca["qz_done"], 1)
                        pool.wait_ge(ca["qz_done"], PRIME + it * (8 * HP) + 4 * hp + 2)
                        for a in range(2):
                            src = qT[64 * a:64 * a + 64, h2, b * T:(b + 1) * T]
                            nc.gpsimd.tensor_tensor(qzl[64 * a:64 * a + 64, hp % 2, a, :], src,
                                                    qzh[64 * a:64 * a + 64, hp % 2, a, :].bitcast(f32),
                                                    ALU.subtract).then_inc(ca["qz_done"], 1)
                        if hp == 10:
                            pool.wait_ge(ca["qz_done"], PRIME + it * (8 * HP) + 4 * hp + 4)
                            power(lay * (PHASES * PAIRS) + PAIRS + pair + 2, vare[:, :], rstd[:, :], ln_var, ln_rstd)
                            pool.wait_ge(ln_rstd, lay * (PHASES * PAIRS) + PAIRS + pair + 2)
                pool.wait_ge(ca["qz_done"], PRIME + (lay + 1) * (PAIRS * 8 * HP))
                layer_blocks(FF_BLOCKS, 16, lay, ff_free, lay * (PHASES * PAIRS) + 2 * PAIRS + 1)
                with pool.Fori(0, PAIRS) as pair:
                    pool.wait_ge(w_split[1], PRIME + lay * (PER_LAYER // 2) + 10)
                    pool.wait_ge(ln_rstd, lay * (PHASES * PAIRS) + 2 * PAIRS + pair + 1)
                    power(lay * (PHASES * PAIRS) + 2 * PAIRS + pair + 2, vare[:, :], rstd[:, :], ln_var, ln_rstd)
            for m, (blk, cn, src) in enumerate(L1_BLOCKS):
                if m == 0:
                    pool.wait_ge(ln_rstd, L * (PHASES * PAIRS) + 1)
                    pool.wait_ge(ff["y_ready"], PRIME + L * PAIRS * 2)
                base = L * PER_LAYER
                split_block(m, blk, cn, 32 * (base // 2 + m // 2 + 1), 2 * (base + m + 1) - (1 if m == 3 else 2 if m == 4 else 0),
                            base // 2 + (m + 1) // 2)
            with pool.Fori(0, PAIRS) as pair:
                pool.wait_ge(w_split[0], PRIME + (L * PER_LAYER + len(L1_BLOCKS) + 1) // 2)
                pool.wait_ge(ln_rstd, L * (PHASES * PAIRS) + pair + 1)
                power(pair * 2 + 1, vare[:, :], rstd[:, :], l1["var"], l1["rstd"])
                pool.wait_ge(l1["rstd"], pair * 2 + 1)
                power(pair * 2 + 2, vare[:, :], rstd[:, :], l1["var"], l1["rstd"])
                pool.wait_ge(l1["rstd"], pair * 2 + 2)
                power(L * (PHASES * PAIRS) + pair + 2, vare[:, :], rstd[:, :], ln_var, ln_rstd)

        @block.tensor
        def _(pe):
            def three(o, sh, sl, mh, ml, start, stop):
                nc.tensor.matmul(o, sh, mh, start=start, stop=False)
                nc.tensor.matmul(o, sh, ml, start=False, stop=False)
                return nc.tensor.matmul(o, sl, mh, start=False, stop=stop)

            def turn(o, src, n):
                return nc.tensor.transpose(o, src, ident[0:n, 0:n])

            def ln_turn(j, pj_done, base, event):
                for b in range(2):
                    bk = (j + b) % 2
                    pe.wait_ge(pj_done[bk], PRIME + base + (j + b) // 2)
                    pe.wait_ge(ln_xn, event * 2 + b + 1)
                    turn(PJ[bk][:, 0:T], xn[:, b, 0:128], T)
                    turn(PJ[bk][:, T:T2], xn[:, b, 128:256], T).then_inc(ln_turned, 1)

            pe.wait_ge(consts_set, 9)
            with pe.Fori(0, PAIRS) as i:
                for b in range(2):
                    pe.wait_ge(ctx_raw_in[b], 16 * (i + 1))
                    pe.wait_ge(ctx_split[b], PRIME + i)
                    for t in range(KT):
                        turn(SC[b][:, t * KC:(t + 1) * KC], craw[:, b, t, 0:128], KC)
                    for t in range(KT):
                        last = turn(TR[b][0:CL, t * KC:(t + 1) * KC], craw[:, b, t, 128:C], KC)
                    last.then_inc(ctx_turned, 1)
            for b in range(2):
                pe.wait_ge(ctx_split[b], PRIME + PAIRS)
            pe.wait_ge(params_in, 16 * PARAM_DMAS)
            turn(OA[0][:, 0:128], prow[:, :], 128).then_inc(params_turned, 1)
            for b in range(2):
                pe.wait_ge(ln_xn, b + 1)
                turn(PJ[b][:, 0:T], xn[:, b, 0:128], T)
                turn(PJ[b][:, T:T2], xn[:, b, 128:256], T).then_inc(ln_turned, 1)

            with pe.Fori(0, L) as lay:
                w0 = lay * (PER_LAYER // 2)
                git0 = lay * (PHASES * PAIRS)
                with pe.Fori(0, PAIRS) as pair:
                    pe.wait_ge(ff["pj_done"][0], PRIME + lay * (PAIRS * FF_J // 2))
                    pe.wait_ge(ff["pj_done"][1], PRIME + lay * (PAIRS * FF_J // 2))
                    for k in range(2):
                        pe.wait_ge(w_split[k], PRIME + w0 + 4)
                    for i in range(2):
                        pe.wait_ge(ca["exp_done"], PRIME + lay * (PAIRS * 2 * H))
                        pe.wait_ge(ca["pt_done"][i], PRIME + lay * (PAIRS * H))
                        pe.wait_ge(ca["o_done"][i], PRIME + lay * (PAIRS * 2))
                    it = lay * PAIRS + pair
                    pb = it * (SA_J // 2)

                    def pj(j):
                        pe.wait_ge(sa["pj_done"][j % 2], PRIME + pb + j // 2)
                        return PJ[j % 2]

                    def pj_out(j):
                        pe.wait_ge(sa["pj_done"][j % 2], PRIME + pb + j // 2 + 1)

                    pe.wait_ge(ln_low, git0 + pair + 1)
                    for hp in range(HP):
                        o = pj(hp)
                        for a in range(2):
                            for k in range(2):
                                w = wcol(2 * a + k, hp * 128, 128)
                                last = three(o[:, a * T2:(a + 1) * T2], WH[:, w], WL[:, w], hTh[:, k, :], hTl[:, k, :],
                                             k == 0, k == 1)
                        last.then_inc(sa["qk_ready"], 1)
                    for b in range(2):
                        for n in range(2):
                            o = pj(8 + 2 * b + n)
                            for k in range(2):
                                w = wcol(4 + k, n * 512, 512)
                                tt = slice(b * T, (b + 1) * T)
                                last = three(o[0:T, :], hTh[:, k, tt], hTl[:, k, tt], WH[:, w], WL[:, w], k == 0, k == 1)
                            last.then_inc(sa["v_ready"], 1)
                    pj_out(6)
                    pj_out(7)

                    def turn_out(i, j):
                        o = pj(j)
                        pe.wait_ge(sa["o_done"][i % 2], PRIME + it * 2 + i // 2 + 1)
                        for c in range(4):
                            last = turn(o[:, c * T:(c + 1) * T], O[:, i % 2, c * 128:(c + 1) * 128], T)
                        last.then_inc(sa["ot_ready"], 1)

                    def project(j, ja, jb):
                        o = pj(j)
                        pj_out(ja)
                        pj_out(jb)
                        for c in range(HP):
                            w = wcol(6, c * D, D)
                            last = three(o[0:T, 0:D], OTh[:, c, :], OTl[:, c, :], WH[:, w], WL[:, w], c == 0, c == HP - 1)
                        last.then_inc(sa["y_ready"], 1)

                    for s in range(13):
                        g = s - 2
                        if 0 <= g < 8:
                            pe.wait_ge(sa["exp_done"], PRIME + it * 8 + g + 1)
                            pe.wait_ge(sa["pt_done"][g % 2], PRIME + it * 4 + g // 2)
                            for c in range(4):
                                last = turn(TR[g % 2][0:T, c * T:(c + 1) * T], P[:, g % 2, c * T:(c + 1) * T], T)
                            last.then_inc(sa["t_ready"], 1)
                        if s < 8:
                            if s < 2:
                                pe.wait_ge(sa["exp_done"], PRIME + it * 8)
                            b = s // 4
                            for c in range(2):
                                hp = 2 * (s % 4) + c
                                last = nc.tensor.matmul(SC[s % 2][0:T, c * T2:(c + 1) * T2], qT[:, hp, b * T:(b + 1) * T],
                                                        kz[:, hp, :, b * T:(b + 1) * T], start=True, stop=True)
                            last.then_inc(sa["s_ready"], 1)
                        g = s - 3
                        if 0 <= g < 8:
                            i = g // 2
                            pe.wait_ge(sa["pt_done"][g % 2], PRIME + it * 4 + g // 2 + 1)
                            if g % 2 == 0:
                                pe.wait_ge(sa["o_done"][i % 2], PRIME + it * 2 + i // 2)
                            if g % 4 == 0:
                                pj_out(8 + 2 * (g // 4))
                                pj_out(9 + 2 * (g // 4))
                            for c in range(4):
                                h = 4 * (g % 4) + c
                                oc = (4 * (g % 2) + c) * DH
                                last = nc.tensor.matmul(OA[i % 2][0:T, oc:oc + DH], PT[0:T, g % 2, c * T:(c + 1) * T],
                                                        V[0:T, g // 4, h * DH:(h + 1) * DH], start=True, stop=True)
                            if g % 2 == 1:
                                last.then_inc(sa["o_ready"], 1)
                        if s == 4:
                            ln_turn(12, sa["pj_done"], pb, git0 + pair + 1)
                        if s == 5:
                            turn_out(0, 14)
                        if s == 7:
                            turn_out(1, 15)
                        if s == 9:
                            project(16, 14, 15)
                            turn_out(2, 17)
                        if s == 11:
                            turn_out(3, 18)
                        if s == 12:
                            project(19, 17, 18)

                with pe.Fori(0, PAIRS) as pair:
                    for i in range(2):
                        pe.wait_ge(sa["pj_done"][i], PRIME + (lay + 1) * (PAIRS * SA_J // 2))
                        pe.wait_ge(sa["pt_done"][i], PRIME + (lay + 1) * (PAIRS * 4))
                        pe.wait_ge(sa["o_done"][i], PRIME + (lay + 1) * (PAIRS * 2))
                        pe.wait_ge(w_split[i], PRIME + w0 + 8)
                    pe.wait_ge(sa["exp_done"], PRIME + (lay + 1) * (PAIRS * 8))
                    it = lay * PAIRS + pair
                    pb = it * (CA_J // 2)
                    jn = [0]

                    def pj(j):
                        assert j == jn[0]
                        jn[0] += 1
                        pe.wait_ge(ca["pj_done"][j % 2], PRIME + pb + j // 2)
                        return PJ[j % 2]

                    def pj_out(j):
                        pe.wait_ge(ca["pj_done"][j % 2], PRIME + pb + j // 2 + 1)

                    pe.wait_ge(ln_low, git0 + PAIRS + pair + 1)
                    for q in range(4):
                        o = pj(q)
                        for a in range(2):
                            for k in range(2):
                                w = wcol(k, (2 * q + a) * 128, 128)
                                last = three(o[:, a * T2:(a + 1) * T2], WH[:, w], WL[:, w], hTh[:, k, :], hTl[:, k, :],
                                             k == 0, k == 1)
                        last.then_inc(ca["q_ready"], 1)

                    def values(b, n):
                        t, c = n // 2, n % 2
                        tt = slice(t * KC, (t + 1) * KC)
                        o = pj(CA_JOBS[("v", b, n)])
                        w, wl = wcol(3, c * 512, 512), wcol(5, c * 512, 512)
                        three(o[0:KC, :], CT[:, b, 0, tt], CT[:, b, 1, tt], WH[:, w], WL[:, w], True, False)
                        nc.tensor.matmul(o[0:KC, :], CT[:, b, 2, tt], WH[:, wl], start=False, stop=False)
                        nc.tensor.matmul(o[0:KC, :], CT[:, b, 2, tt], WL[:, wl], start=False, stop=True) \
                            .then_inc(ca["v_ready"], 1)

                    def keys(hp):
                        b, h2 = hp // HP, hp % HP
                        o = pj(CA_JOBS[("k", hp)])
                        w, wl = wcol(2, h2 * 128, 128), wcol(4, h2 * 128, 128)
                        three(o[:, 0:SP], WH[:, w], WL[:, w], CT[:, b, 0, :], CT[:, b, 1, :], True, False)
                        nc.tensor.matmul(o[:, 0:SP], WH[:, wl], CT[:, b, 2, :], start=False, stop=False)
                        nc.tensor.matmul(o[:, 0:SP], WL[:, wl], CT[:, b, 2, :], start=False, stop=True) \
                            .then_inc(ca["k_ready"][b], 1)

                    def turn_out(i):
                        o = pj(CA_JOBS[("ot", i)])
                        pe.wait_ge(ca["o_done"][i % 2], PRIME + it * 2 + i // 2 + 1)
                        for c in range(4):
                            last = turn(o[:, c * T:(c + 1) * T], O[:, i % 2, c * 128:(c + 1) * 128], T)
                        last.then_inc(ca["ot_ready"], 1)

                    def project(b):
                        o = pj(CA_JOBS[("y", b)])
                        pj_out(CA_JOBS[("ot", 2 * b)])
                        pj_out(CA_JOBS[("ot", 2 * b + 1)])
                        for c in range(HP):
                            w = wcol(6, c * D, D)
                            last = three(o[0:T, 0:D], OTh[:, c, :], OTl[:, c, :], WH[:, w], WL[:, w], c == 0, c == HP - 1)
                        last.then_inc(ca["y_ready"], 1)

                    def scores(h):
                        hp, a = h // 2, h % 2
                        if h < 2:
                            pe.wait_ge(ca["exp_done"], PRIME + it * (2 * H))
                        if a == 0:
                            pe.wait_ge(ca["qz_done"], PRIME + it * (8 * HP) + 4 * hp + 4)
                            pj_out(CA_JOBS[("k", hp)])
                        three(SC[h % 2][0:T, 0:SP], qzh[:, hp % 2, a, :], qzl[:, hp % 2, a, :], Kh[:, hp % 2, :],
                              Kl[:, hp % 2, :], True, True).then_inc(ca["s_ready"], 1)

                    def turn_probs(h):
                        pe.wait_ge(ca["exp_done"], PRIME + it * (2 * H) + h + 1)
                        pe.wait_ge(ca["pt_done"][h % 2], PRIME + it * H + h // 2)
                        for t in range(KT):
                            last = turn(TR[h % 2][0:KC, t * T:(t + 1) * T], P[:, h % 2, t * KC:(t + 1) * KC], T)
                        last.then_inc(ca["t_ready"], 1)

                    def attend(h):
                        i, b = h // 8, h // H
                        pe.wait_ge(ca["pt_done"][h % 2], PRIME + it * H + h // 2 + 1)
                        if h % 8 == 0:
                            pe.wait_ge(ca["o_done"][i % 2], PRIME + it * 2 + i // 2)
                        if h % H == 0:
                            pj_out(CA_JOBS[("v", b, 4)])
                            pj_out(CA_JOBS[("v", b, 5)])
                        oc = (h % 8) * DH
                        for t in range(KT):
                            vc = t * INNER + (h % H) * DH
                            last = nc.tensor.matmul(OA[i % 2][0:T, oc:oc + DH], PT[0:KC, h % 2, t * T:(t + 1) * T],
                                                    V[0:KC, b, vc:vc + DH], start=t == 0, stop=t == KT - 1)
                        if h % 8 == 7:
                            last.then_inc(ca["o_ready"], 1)

                    for step in CA_STEPS:
                        for job in step:
                            if job[0] == "v":
                                if job[2] == 0:
                                    pe.wait_ge(ctx_in[job[1]], 16 * (it + 1))
                                values(job[1], job[2])
                            elif job[0] == "k":
                                keys(job[1])
                            elif job[0] == "ln":
                                jn[0] += 2
                                ln_turn(CA_JOBS[job], ca["pj_done"], pb, git0 + PAIRS + pair + 1)
                            elif job[0] == "ot":
                                turn_out(job[1])
                            elif job[0] == "y":
                                project(job[1])
                            elif job[0] == "s":
                                scores(job[1])
                            elif job[0] == "t":
                                turn_probs(job[1])
                            elif job[0] == "pv":
                                attend(job[1])

                with pe.Fori(0, PAIRS) as pair:
                    for i in range(2):
                        pe.wait_ge(ca["pj_done"][i], PRIME + (lay + 1) * (PAIRS * CA_J // 2))
                        pe.wait_ge(w_split[i], PRIME + w0 + 10)
                    it = lay * PAIRS + pair
                    pb = it * (FF_J // 2)

                    def pj(j):
                        pe.wait_ge(ff["pj_done"][j % 2], PRIME + pb + j // 2)
                        return PJ[j % 2]

                    pe.wait_ge(ln_low, git0 + 2 * PAIRS + pair + 1)
                    for q in range(4):
                        o = pj(q)
                        for a in range(2):
                            for k in range(2):
                                w = wcol(k, (2 * q + a) * 128, 128)
                                last = three(o[:, a * T2:(a + 1) * T2], WH[:, w], WL[:, w], hTh[:, k, :], hTl[:, k, :],
                                             k == 0, k == 1)
                        last.then_inc(ff["f_ready"], 1)
                    ln_turn(4, ff["pj_done"], pb, git0 + 2 * PAIRS + pair + 1)
                    for b in range(2):
                        o = pj(6 + b)
                        for f in range(8):
                            if b == 0 and f % 2 == 0:
                                pe.wait_ge(ff["g_split"], it * 4 + f // 2 + 1)
                            w = wcol(3 + 2 * (f // 4), (f % 4) * D, D)
                            tt = slice(b * T, (b + 1) * T)
                            last = three(o[0:T, 0:D], Gh[:, f, tt], Gl[:, f, tt], WH[:, w], WL[:, w], f == 0, f == 7)
                        last.then_inc(ff["y_ready"], 1)

            for i in range(2):
                pe.wait_ge(ff["pj_done"][i], PRIME + L * (PAIRS * FF_J // 2))
            nblk = L * PER_LAYER + len(L1_BLOCKS)
            pe.wait_ge(w_split[0], PRIME + (nblk + 1) // 2)
            pe.wait_ge(w_split[1], PRIME + nblk // 2)
            with pe.Fori(0, PAIRS) as pair:
                pb = pair * (L1_J // 2)

                def pj(j):
                    pe.wait_ge(l1["pj_done"][j % 2], PRIME + pb + j // 2)
                    return PJ[j % 2]

                def pj_out(j):
                    pe.wait_ge(l1["pj_done"][j % 2], PRIME + pb + j // 2 + 1)

                pe.wait_ge(l1["xs_done"], pair + 1)
                o = pj(0)
                for b in range(2):
                    for k in range(2):
                        last = turn(o[:, k * T2 + b * T:k * T2 + (b + 1) * T], xs[:, b, k * 128:(k + 1) * 128], T)
                last.then_inc(l1["x_ready"], 1)
                for b in range(2):
                    pe.wait_ge(ctx_in[b], 16 * (L * PAIRS + pair + 1))
                    for m in range(2):
                        o = pj(1 + 4 * b + m)
                        w, wl = wcol(7, m * 128, 128), wcol(0, m * 128, 128)
                        three(o[:, 0:SP], WH[:, w], WL[:, w], CT[:, b, 0, :], CT[:, b, 1, :], True, False)
                        nc.tensor.matmul(o[:, 0:SP], WH[:, wl], CT[:, b, 2, :], start=False, stop=False)
                        nc.tensor.matmul(o[:, 0:SP], WL[:, wl], CT[:, b, 2, :], start=False, stop=True) \
                            .then_inc(l1["tok_ready"], 1)
                    for n, ts in enumerate(((0, 1), (2,))):
                        o = pj(3 + 4 * b + n)
                        for c, t in enumerate(ts):
                            tt = slice(t * KC, (t + 1) * KC)
                            oc = o[0:KC, c * D:(c + 1) * D]
                            w, wl = wcol(7, 0, D), wcol(0, 0, D)
                            three(oc, CT[:, b, 0, tt], CT[:, b, 1, tt], WH[:, w], WL[:, w], True, False)
                            nc.tensor.matmul(oc, CT[:, b, 2, tt], WH[:, wl], start=False, stop=False)
                            last = nc.tensor.matmul(oc, CT[:, b, 2, tt], WL[:, wl], start=False, stop=True)
                        last.then_inc(l1["tok_ready"], 1)
                    pj_out(0)
                    pj_out(1 + 4 * b)
                    pj_out(2 + 4 * b)
                    for k in range(2):
                        last = nc.tensor.matmul(SC[b][0:T, 0:SP], xT[:, k, b * T:(b + 1) * T], tokT[:, k, :],
                                                start=k == 0, stop=k == 1)
                    last.then_inc(l1["s_ready"], 1)
                    pe.wait_ge(l1["exp_done"], pair * 2 + b + 1)
                    pe.wait_ge(l1["pt_done"][b], PRIME + pair)
                    for t in range(KT):
                        last = turn(TR[b][0:KC, t * T:(t + 1) * T], P[:, b, t * KC:(t + 1) * KC], T)
                    last.then_inc(l1["t_ready"], 1)
                    pj_out(3 + 4 * b)
                    pj_out(4 + 4 * b)
                    pe.wait_ge(l1["pt_done"][b], PRIME + pair + 1)
                    for t in range(KT):
                        last = nc.tensor.matmul(OA[b][0:T, 0:D], PT[0:KC, b, t * T:(t + 1) * T], tok[:, t, :],
                                                start=t == 0, stop=t == KT - 1)
                    last.then_inc(l1["o_ready"], 1)
                for b in range(2):
                    o = pj(9 + b)
                    pe.wait_ge(l1["norm"], pair * 2 + b + 1)
                    for k in range(2):
                        last = turn(o[:, k * T:(k + 1) * T], xn[:, b, k * 128:(k + 1) * 128], T)
                    last.then_inc(l1["in_ready"], 1)
                pe.wait_ge(ln_low, L * (PHASES * PAIRS) + pair + 1)
                pe.wait_ge(l1["in_low"], pair + 1)

                def gate(j, blk, kh, kl):
                    o = pj(j)
                    srcs = [(kh, kl, 0), (kh, kl, 1), (inTh, inTl, 0), (inTh, inTl, 1)]
                    for m in range(2):
                        for n, (h, l, k) in enumerate(srcs):
                            w = wcol(blk, n * D + m * 128, 128)
                            last = three(o[:, m * T2:(m + 1) * T2], WH[:, w], WL[:, w], h[:, k, :], l[:, k, :],
                                         n == 0, n == 3)
                    last.then_inc(l1["g_ready"], 1)

                gate(11, 4, hTh, hTl)
                gate(12, 2, hTh, hTl)
                pe.wait_ge(l1["rp_split"], pair + 1)
                gate(13, 6, rph, rpl)
                pe.wait_ge(l1["ns_done"], pair + 1)
                for b in range(2):
                    o = pj(14 + b)
                    for k in range(2):
                        last = turn(o[0:T, k * 128:(k + 1) * 128], nsT[:, k, b * T:(b + 1) * T], 128)
                    last.then_inc(l1["out_ready"], 1)
                ln_turn(16, l1["pj_done"], pb, L * (PHASES * PAIRS) + pair + 1)

        @block.scalar
        def _(act):
            def copy(o, i):
                return nc.scalar.activation(o, i, ACT.Copy)

            def affine_done(pj_done, base, j):
                for n in (j, j + 1):
                    act.wait_ge(pj_done[n % 2], PRIME + base + n // 2 + 1)

            act.wait_ge(consts_set, 9)
            with act.Fori(0, PAIRS) as i:
                for b in range(2):
                    act.wait_ge(ctx_turned, PRIME + 2 * i + b + 1)
                    act.wait_ge(ctx_stored[b], PRIME + 16 * i)
                    copy(CT[:, b, 0, 0:S], SC[b][:, 0:S])
                    copy(CT[0:CL, b, 2, 0:S], TR[b][0:CL, 0:S]).then_inc(ctx_high, 1)
            act.wait_ge(first_affine, 2)
            copy(hTh[:, :, :], hTf[:, :, :]).then_inc(ln_high, 1)

            with act.Fori(0, L) as lay:
                with act.Fori(0, PAIRS) as pair:
                    it = lay * PAIRS + pair
                    pb = it * (SA_J // 2)
                    for hp in range(HP):
                        act.wait_ge(sa["qk_ready"], it * 8 + hp + 1)
                        o = PJ[hp % 2]
                        copy(qT[:, hp, :], o[:, 0:T2])
                        copy(kz[0:64, hp, 0, :], o[0:64, T2:2 * T2])
                        copy(kz[64:128, hp, 1, :], o[64:128, T2:2 * T2]).then_inc(sa["pj_done"][hp % 2], 1)

                    def out_high(i, j):
                        act.wait_ge(sa["ot_ready"], it * 4 + i + 1)
                        copy(OTh[:, 4 * (i % 2):4 * (i % 2) + 4, :].rearrange("p c t -> p (c t)"), PJ[j % 2][:, 0:4 * T]) \
                            .then_inc(sa["ot_high"], 1)

                    for s in range(12):
                        if s < 8:
                            act.wait_ge(sa["nb_ready"], it * 8 + s + 1)
                            for c in range(4):
                                h = 4 * (s % 4) + c
                                last = nc.scalar.activation(P[:, s % 2, c * T:(c + 1) * T], SC[s % 2][0:T, c * T:(c + 1) * T],
                                                            ACT.Exp, bias=nb[:, s % 2, c:c + 1], scale=SCALE,
                                                            accum_out=rs[:, s // 4, h:h + 1])
                            last.then_inc(sa["exp_done"], 1)
                        if s == 4:
                            affine_done(sa["pj_done"], pb, 12)
                            copy(hTh[:, :, :], hTf[:, :, :]).then_inc(ln_high, 1)
                        if s == 5:
                            out_high(0, 14)
                        if s == 7:
                            out_high(1, 15)
                        if s == 9:
                            out_high(2, 17)
                        if s == 11:
                            out_high(3, 18)

                with act.Fori(0, PAIRS) as pair:
                    it = lay * PAIRS + pair
                    for q in range(4):
                        act.wait_ge(ca["q_ready"], PRIME + it * 4 + q + 1)
                        copy(qT[:, 2 * q:2 * q + 2, :].rearrange("p a t -> p (a t)"), PJ[q % 2][:, 0:2 * T2]) \
                            .then_inc(ca["pj_done"][q % 2], 1)
                    for step in CA_STEPS:
                        for job in step:
                            if job[0] == "k":
                                hp = job[1]
                                b = hp // HP
                                act.wait_ge(ca["k_ready"][b], PRIME + it * HP + hp % HP + 1)
                                copy(Kh[:, hp % 2, :], PJ[CA_JOBS[job] % 2][:, 0:SP]).then_inc(ca["k_high"], 1)
                            elif job[0] == "ln":
                                affine_done(ca["pj_done"], it * (CA_J // 2), CA_JOBS[job])
                                copy(hTh[:, :, :], hTf[:, :, :]).then_inc(ln_high, 1)
                            elif job[0] == "ot":
                                i = job[1]
                                act.wait_ge(ca["ot_ready"], it * 4 + i + 1)
                                copy(OTh[:, 4 * (i % 2):4 * (i % 2) + 4, :].rearrange("p c t -> p (c t)"),
                                     PJ[CA_JOBS[job] % 2][:, 0:4 * T]).then_inc(ca["ot_high"], 1)
                            elif job[0] == "s":
                                h = job[1]
                                act.wait_ge(ca["nb_ready"], it * (2 * H) + h + 1)
                                nc.scalar.activation(P[:, h % 2, 0:S], SC[h % 2][0:T, 0:S], ACT.Exp,
                                                     bias=nb[:, h % 2, 0:1], scale=SCALE,
                                                     accum_out=rs[:, h // H, h % H:h % H + 1]).then_inc(ca["exp_done"], 1)
                            elif job[0] == "t":
                                h = job[1]
                                act.wait_ge(ca["t_ready"], it * (2 * H) + h + 1)
                                copy(PT[0:KC, h % 2, 0:KT * T], TR[h % 2][0:KC, 0:KT * T]).then_inc(ca["pt_done"][h % 2], 1)

                with act.Fori(0, PAIRS) as pair:
                    it = lay * PAIRS + pair
                    for q in range(4):
                        act.wait_ge(ff["f_ready"], PRIME + it * 4 + q + 1)
                        for a in range(2):
                            f = 2 * q + a
                            last = nc.scalar.activation(Gf[:, f, :], PJ[q % 2][:, a * T2:(a + 1) * T2], ACT.Gelu,
                                                        bias=pcol[:, ds(FF_V + lay * 8 + f, 1)])
                        last.then_inc(ff["pj_done"][q % 2], 1)
                    affine_done(ff["pj_done"], it * (FF_J // 2), 4)
                    copy(hTh[:, :, :], hTf[:, :, :]).then_inc(ln_high, 1)

            with act.Fori(0, PAIRS) as pair:
                pb = pair * (L1_J // 2)
                act.wait_ge(ff["dve_step"], L * PAIRS * FF_STEPS)
                copy(xs[:, :, :], X[:, ds(2 * pair, 2), :]).then_inc(l1["xs_done"], 1)
                act.wait_ge(l1["x_ready"], pair + 1)
                copy(xT[:, :, :].rearrange("p k t -> p (k t)"), PJ[0][:, 0:2 * T2]).then_inc(l1["pj_done"][0], 1)
                for b in range(2):
                    act.wait_ge(l1["nb_ready"], pair * 2 + b + 1)
                    nc.scalar.activation(P[:, b, 0:S], SC[b][0:T, 0:S], ACT.Exp, bias=nb[:, b, 0:1], scale=SCALE_OUT,
                                         accum_out=rs[:, b, 0:1]).then_inc(l1["exp_done"], 1)
                    act.wait_ge(l1["t_ready"], pair * 2 + b + 1)
                    copy(PT[0:KC, b, 0:KT * T], TR[b][0:KC, 0:KT * T]).then_inc(l1["pt_done"][b], 1)
                affine_done(l1["pj_done"], pb, 9)
                copy(inTh, inT).then_inc(l1["in_high"], 1)
                for n, (dst, j, c0) in enumerate(((rT, 11, 2), (uT, 12, 0))):
                    act.wait_ge(l1["g_ready"], pair * 3 + n + 1)
                    for m in range(2):
                        last = nc.scalar.activation(dst[:, m, :], PJ[j % 2][:, m * T2:(m + 1) * T2], ACT.Tanh,
                                                    bias=hcols[:, c0 + m:c0 + m + 1], scale=0.5)
                    last.then_inc(l1["pj_done"][j % 2], 1)
                act.wait_ge(l1["g_ready"], pair * 3 + 3)
                for m in range(2):
                    last = nc.scalar.activation(cT[:, m, :], PJ[1][:, m * T2:(m + 1) * T2], ACT.Tanh,
                                                bias=cols[:, 10 + m:11 + m])
                last.then_inc(l1["pj_done"][1], 1)
                affine_done(l1["pj_done"], pb, 16)
                copy(hTh[:, :, :], hTf[:, :, :]).then_inc(ln_high, 1)

        @block.vector
        def _(dve):
            def ln_stats(step, nxt, var_value):
                for b in range(2):
                    last = nc.vector.bn_stats(bst[:, b, :], X[:, ds(2 * nxt + b, 1), :].rearrange("p o d -> p (o d)"))
                step(last, before_aggr=True)
                for b in range(2):
                    last = nc.vector.bn_aggr(mv[:, b, :], bst[:, b, :])
                step(last)
                nc.vector.tensor_scalar(vare[:, :], mv[:, :, 1], EPS, None, ALU.add).then_inc(ln_var, 1)
                dve.wait_ge(ln_rstd, var_value)
                for b in range(2):
                    nc.vector.tensor_scalar(xn[:, b, :], X[:, ds(2 * nxt + b, 1), :].rearrange("p o d -> p (o d)"),
                                            mv[:, b, 0:1], rstd[:, b:b + 1], ALU.subtract, ALU.mult).then_inc(ln_xn, 1)

            def ln_affine_to(gcol, j, pj_done, event):
                for b in range(2):
                    bk = (j + b) % 2
                    dve.wait_ge(ln_turned, event * 2 + b + 1)
                    for k in range(2):
                        ins = nc.vector.tensor_scalar(hTf[:, k, b * T:(b + 1) * T], PJ[bk][:, k * T:(k + 1) * T],
                                                      pcol[:, ds(gcol + k, 1)], pcol[:, ds(gcol + LNV + k, 1)],
                                                      ALU.mult, ALU.add)
                    ins.then_inc(pj_done[bk], 1)

            def ln_low_part(event):
                dve.wait_ge(ln_high, event + 1)
                nc.vector.tensor_tensor(hTl[:, :, :], hTf[:, :, :], hTh[:, :, :].bitcast(f32), ALU.subtract) \
                    .then_inc(ln_low, 1)

            def negmax(step, h, src, n, scale):
                step(nc.vector.reduce_max(mx[:, h % 2, 0:n], src, AX.X))
                return nc.vector.tensor_scalar(nb[:, h % 2, 0:n], mx[:, h % 2, 0:n], -scale, None, ALU.mult)

            def normalise(step, i, s, base_step, done):
                step(nc.vector.reciprocal(rinv[:, i % 2, :], rs[:, i // 2, 8 * (i % 2):8 * (i % 2) + 8]))
                nc.vector.tensor_tensor(O[:, i % 2, :].rearrange("p (h d) -> p h d", h=8),
                                        OA[i % 2][0:T, :].rearrange("p (h d) -> p h d", h=8),
                                        rinv[:, i % 2, :].unsqueeze(2).broadcast_to([T, 8, DH]),
                                        ALU.mult).then_inc(done, 1)

            def out_low(i, bk, s, pj_done):
                nc.vector.tensor_tensor(OTl[:, 4 * (i % 2):4 * (i % 2) + 4, :].rearrange("p c t -> p (c t)"),
                                        PJ[bk][:, 0:4 * T],
                                        OTh[:, 4 * (i % 2):4 * (i % 2) + 4, :].rearrange("p c t -> p (c t)").bitcast(f32),
                                        ALU.subtract).then_inc(pj_done[bk], 1)

            def residual(step, bt, bk, slot, pj_done, added):
                xb = X[:, ds(bt, 1), :].rearrange("p o d -> p (o d)")
                nc.vector.tensor_tensor(xb, PJ[bk][0:T, 0:D], xb, ALU.add).then_inc(pj_done[bk], 1)
                dve.wait_ge(pj_done[bk], PRIME + added)
                step(nc.vector.tensor_tensor(xb, xb, OB[:, ds(slot, 1), :].rearrange("p o d -> p (o d)"), ALU.add))

            dve.wait_ge(consts_set, 9)
            with dve.Fori(0, PAIRS) as i:
                for b in range(2):
                    dve.wait_ge(ctx_high, 2 * i + b + 1)
                    nc.vector.tensor_tensor(CT[:, b, 1, 0:S], SC[b][:, 0:S], CT[:, b, 0, 0:S].bitcast(f32), ALU.subtract)
                    nc.vector.tensor_tensor(CT[CL:2 * CL, b, 2, 0:S], TR[b][0:CL, 0:S], CT[0:CL, b, 2, 0:S].bitcast(f32),
                                            ALU.subtract).then_inc(ctx_split[b], 1)
            dve.wait_ge(params_in, 16 * PARAM_DMAS)
            dve.wait_ge(params_turned, 1)
            nc.vector.tensor_copy(pcol[:, :], OA[0][:, 0:128]).then_inc(first_step, 1)
            dve.wait_ge(first_step, 1)
            nc.vector.tensor_scalar(hcols[:, :], cols[:, 6:10], 0.5, None, ALU.mult)
            step = Steps(dve, first_step, 1, 2)
            ln_stats(step, 0, 1)
            step.close()
            ln_affine_to(0, 0, [first_affine, first_affine], 0)
            ln_low_part(0)

            with dve.Fori(0, L) as lay:
                with dve.Fori(0, PAIRS) as pair:
                    it = lay * PAIRS + pair
                    event = lay * (PHASES * PAIRS) + pair + 1
                    nxt = (pair + 1) % PAIRS
                    gcol = 2 * lay + (pair + 1) // PAIRS * (2 * LNV)
                    step = Steps(dve, sa["dve_step"], it * SA_STEPS, SA_STEPS)
                    for n in range(4):
                        j = 8 + n
                        dve.wait_ge(sa["v_ready"], PRIME + it * 4 + n + 1)
                        nc.vector.tensor_copy(V[0:T, n // 2, (n % 2) * 512:(n % 2) * 512 + 512], PJ[j % 2][0:T, :]) \
                            .then_inc(sa["pj_done"][j % 2], 1)
                    for s in range(13):
                        if s < 8:
                            dve.wait_ge(sa["s_ready"], it * 8 + s + 1)
                            negmax(step, s, SC[s % 2][0:T, 0:4 * T].rearrange("p (c t) -> p c t", c=4), 4, SCALE) \
                                .then_inc(sa["nb_ready"], 1)
                        g = s - 2
                        if 0 <= g < 8:
                            dve.wait_ge(sa["t_ready"], it * 8 + g + 1)
                            nc.vector.tensor_copy(PT[0:T, g % 2, :], TR[g % 2][0:T, 0:4 * T]) \
                                .then_inc(sa["pt_done"][g % 2], 1)
                        if s in (4, 6, 8, 10):
                            i = (s - 4) // 2
                            dve.wait_ge(sa["o_ready"], it * 4 + i + 1)
                            normalise(step, i, s, 0, sa["o_done"][i % 2])
                        if s == 2:
                            ln_stats(step, nxt, event + 1)
                        if s == 4:
                            ln_affine_to(gcol, 12, sa["pj_done"], event)
                        if s == 5:
                            ln_low_part(event)
                        for at, i, j in ((5, 0, 14), (7, 1, 15), (9, 2, 17), (11, 3, 18)):
                            if s == at:
                                if i == 2:
                                    dve.wait_ge(sa["y_ready"], PRIME + it * 2 + 1)
                                    residual(step, 2 * pair, 0, lay * PHASES, sa["pj_done"], it * (SA_J // 2) + 16 // 2 + 1)
                                dve.wait_ge(sa["ot_high"], it * 4 + i + 1)
                                out_low(i, j % 2, s, sa["pj_done"])
                        if s == 12:
                            dve.wait_ge(sa["y_ready"], PRIME + it * 2 + 2)
                            residual(step, 2 * pair + 1, 1, lay * PHASES, sa["pj_done"], it * (SA_J // 2) + 19 // 2 + 1)
                    step.close()

                with dve.Fori(0, PAIRS) as pair:
                    it = lay * PAIRS + pair
                    event = lay * (PHASES * PAIRS) + PAIRS + pair + 1
                    nxt = (pair + 1) % PAIRS
                    gcol = 2 * LNV + 2 * lay + (pair + 1) // PAIRS * (2 * LNV)
                    step = Steps(dve, ca["dve_step"], it * CA_STEPS_DVE, CA_STEPS_DVE)
                    for step_jobs in CA_STEPS:
                        for job in step_jobs:
                            bk = CA_JOBS.get(job, 0) % 2
                            if job[0] == "v":
                                b, n = job[1], job[2]
                                dve.wait_ge(ca["v_ready"], PRIME + it * 12 + 6 * b + n + 1)
                                vc = (n // 2) * INNER + (n % 2) * 512
                                nc.vector.tensor_copy(V[0:KC, b, vc:vc + 512], PJ[bk][0:KC, :]).then_inc(ca["pj_done"][bk], 1)
                            elif job[0] == "k":
                                hp = job[1]
                                dve.wait_ge(ca["k_high"], it * (2 * HP) + hp + 1)
                                nc.vector.tensor_tensor(Kl[:, hp % 2, :], PJ[bk][:, 0:SP], Kh[:, hp % 2, :].bitcast(f32),
                                                        ALU.subtract).then_inc(ca["pj_done"][bk], 1)
                            elif job[0] == "s":
                                h = job[1]
                                dve.wait_ge(ca["s_ready"], it * (2 * H) + h + 1)
                                negmax(step, h, SC[h % 2][0:T, 0:S], 1, SCALE).then_inc(ca["nb_ready"], 1)
                            elif job[0] == "stats":
                                ln_stats(step, nxt, event + 1)
                            elif job[0] == "ln":
                                ln_affine_to(gcol, CA_JOBS[job], ca["pj_done"], event)
                                ln_low_part(event)
                            elif job[0] == "pv" and job[1] % 8 == 7:
                                i = job[1] // 8
                                dve.wait_ge(ca["o_ready"], it * 4 + i + 1)
                                normalise(step, i, 0, 0, ca["o_done"][i % 2])
                            elif job[0] == "ot":
                                dve.wait_ge(ca["ot_high"], it * 4 + job[1] + 1)
                                out_low(job[1], bk, 0, ca["pj_done"])
                            elif job[0] == "y":
                                dve.wait_ge(ca["y_ready"], PRIME + it * 2 + job[1] + 1)
                                residual(step, 2 * pair + job[1], bk, lay * PHASES + 1, ca["pj_done"],
                                         it * (CA_J // 2) + CA_JOBS[job] // 2 + 1)
                    step.close()

                with dve.Fori(0, PAIRS) as pair:
                    it = lay * PAIRS + pair
                    event = lay * (PHASES * PAIRS) + 2 * PAIRS + pair + 1
                    nxt = (pair + 1) % PAIRS
                    gcol = 4 * LNV + 2 * lay - (pair + 1) // PAIRS * (4 * LNV - 2)
                    step = Steps(dve, ff["dve_step"], it * FF_STEPS, FF_STEPS)
                    ln_stats(step, nxt, event + 1)
                    for q in range(4):
                        dve.wait_ge(ff["pj_done"][q % 2], PRIME + it * (FF_J // 2) + q // 2 + 1)
                        step(nc.vector.tensor_copy(Gh[:, 2 * q:2 * q + 2, :], Gf[:, 2 * q:2 * q + 2, :]))
                        nc.vector.tensor_tensor(Gl[:, 2 * q:2 * q + 2, :], Gf[:, 2 * q:2 * q + 2, :],
                                                Gh[:, 2 * q:2 * q + 2, :].bitcast(f32), ALU.subtract).then_inc(ff["g_split"], 1)
                    ln_affine_to(gcol, 4, ff["pj_done"], event)
                    ln_low_part(event)
                    for b in range(2):
                        dve.wait_ge(ff["y_ready"], PRIME + it * 2 + b + 1)
                        residual(step, 2 * pair + b, b, lay * PHASES + 2, ff["pj_done"], (it + 1) * (FF_J // 2))
                    step.close()

            with dve.Fori(0, PAIRS) as pair:
                event = L * (PHASES * PAIRS) + pair + 1
                step = Steps(dve, l1["dve_step"], pair * L1_STEPS, L1_STEPS)
                for b in range(2):
                    for m in range(2):
                        j = 1 + 4 * b + m
                        dve.wait_ge(l1["tok_ready"], pair * 8 + 4 * b + m + 1)
                        nc.vector.tensor_scalar(tokT[:, m, :], PJ[j % 2][:, 0:SP], cols[:, 4 + m:5 + m], None, ALU.add) \
                            .then_inc(l1["pj_done"][j % 2], 1)
                    for n, ts in enumerate(((0, 1), (2,))):
                        j = 3 + 4 * b + n
                        dve.wait_ge(l1["tok_ready"], pair * 8 + 4 * b + n + 3)
                        for c, t in enumerate(ts):
                            last = nc.vector.tensor_tensor(tok[:, t, :], PJ[j % 2][0:KC, c * D:(c + 1) * D], BP[:, :], ALU.add)
                        last.then_inc(l1["pj_done"][j % 2], 1)
                    dve.wait_ge(l1["s_ready"], pair * 2 + b + 1)
                    negmax(step, b, SC[b][0:T, 0:S], 1, SCALE_OUT).then_inc(l1["nb_ready"], 1)
                    dve.wait_ge(l1["o_ready"], pair * 2 + b + 1)
                    step(nc.vector.reciprocal(rinv[:, b, 0:1], rs[:, b, 0:1]))
                    step(nc.vector.tensor_scalar(routed[:, b, :], OA[b][0:T, 0:D], rinv[:, b, 0:1], None, ALU.mult))
                    step(nc.vector.bn_stats(bst[:, b, :], routed[:, b, :]), before_aggr=True)
                    step(nc.vector.bn_aggr(mv[:, b, :], bst[:, b, :]))
                nc.vector.tensor_scalar(vare[:, :], mv[:, :, 1], EPS, None, ALU.add).then_inc(l1["var"], 1)
                dve.wait_ge(l1["rstd"], pair * 2 + 1)
                for b in range(2):
                    nc.vector.tensor_scalar(xn[:, b, :], routed[:, b, :], mv[:, b, 0:1], rstd[:, b:b + 1],
                                            ALU.subtract, ALU.mult).then_inc(l1["norm"], 1)
                for b in range(2):
                    dve.wait_ge(l1["in_ready"], pair * 2 + b + 1)
                    for k in range(2):
                        ins = nc.vector.tensor_scalar(inT[:, k, b * T:(b + 1) * T], PJ[(9 + b) % 2][:, k * T:(k + 1) * T],
                                                      cols[:, k:k + 1], cols[:, 2 + k:3 + k], ALU.mult, ALU.add)
                    ins.then_inc(l1["pj_done"][(9 + b) % 2], 1)
                dve.wait_ge(l1["in_high"], pair + 1)
                nc.vector.tensor_tensor(inTl, inT, inTh.bitcast(f32), ALU.subtract).then_inc(l1["in_low"], 1)
                pb = pair * (L1_J // 2)
                dve.wait_ge(l1["pj_done"][1], PRIME + pb + 11 // 2 + 1)
                step(nc.vector.tensor_scalar(rT, rT, 0.5, 0.5, ALU.mult, ALU.add))
                step(nc.vector.tensor_tensor(rp, rT, hTf[:, :, :], ALU.mult))
                step(nc.vector.tensor_copy(rph, rp))
                nc.vector.tensor_tensor(rpl, rp, rph.bitcast(f32), ALU.subtract).then_inc(l1["rp_split"], 1)
                dve.wait_ge(l1["pj_done"][0], PRIME + pb + 12 // 2 + 1)
                step(nc.vector.tensor_scalar(uT, uT, 0.5, 0.5, ALU.mult, ALU.add))
                dve.wait_ge(l1["pj_done"][1], PRIME + pb + 13 // 2 + 1)
                step(nc.vector.tensor_tensor(cT, cT, xT, ALU.subtract))
                step(nc.vector.tensor_tensor(cT, cT, uT, ALU.mult))
                nc.vector.tensor_tensor(nsT, cT, xT, ALU.add).then_inc(l1["ns_done"], 1)
                for b in range(2):
                    dve.wait_ge(l1["out_ready"], pair * 2 + b + 1)
                    nc.vector.tensor_copy(yn[:, b, :], PJ[b][0:T, 0:D]).then_inc(l1["pj_done"][b], 1)
                    dve.wait_ge(l1["pj_done"][b], PRIME + pb + 14 // 2 + 1)
                    step(nc.vector.bn_stats(bst[:, b, :], yn[:, b, :]), before_aggr=True)
                    step(nc.vector.bn_aggr(mv[:, b, :], bst[:, b, :]))
                nc.vector.tensor_scalar(vare[:, :], mv[:, :, 1], EPS, None, ALU.add).then_inc(l1["var"], 1)
                dve.wait_ge(l1["rstd"], pair * 2 + 2)
                for b in range(2):
                    step(nc.vector.tensor_scalar(yn[:, b, :], yn[:, b, :], mv[:, b, 0:1], rstd[:, b:b + 1],
                                                 ALU.subtract, ALU.mult))
                    step(nc.vector.tensor_tensor(yn[:, b, :], yn[:, b, :], GO[:, 0, :], ALU.mult))
                    dve.wait_ge(l1["y_stored"], PRIME + pair * 32)
                    nc.vector.tensor_tensor(y[:, b, :], yn[:, b, :], GO[:, 1, :], ALU.add).then_inc(l1["y_done"], 1)
                ln_stats(step, (pair + 1) % PAIRS, event + 1)
                ln_affine_to(2 * L, 16, l1["pj_done"], event)
                ln_low_part(event)
                step.close()


def _ca_order():
    steps = [[("v", 0, n) for n in range(6)] + [("k", 0)]]
    for s in range(35):
        jobs = []
        if s % 2 == 0 and s // 2 + 1 < 16:
            jobs.append(("k", s // 2 + 1))
        if 0 <= s - 2 < 32:
            jobs.append(("t", s - 2))
        if s < 32:
            jobs.append(("s", s))
        if 0 <= s - 3 < 32:
            jobs.append(("pv", s - 3))
        if 4 <= s < 10:
            jobs.append(("v", 1, s - 4))
        if s == 18:
            jobs.append(("stats",))
        if s == 21:
            jobs.append(("ln",))
        if s in (12, 20, 28):
            jobs.append(("ot", {12: 0, 20: 1, 28: 2}[s]) if s != 28 else ("y", 0))
            if s == 28:
                jobs.append(("ot", 2))
        steps.append(jobs)
    steps.append([("ot", 3)])
    steps.append([("y", 1)])
    return steps


def _ca_jobs(steps):
    at, n = {}, 4
    for jobs in steps:
        for job in jobs:
            if job[0] in ("v", "k", "ot", "y"):
                at[job] = n
                n += 1
            if job[0] == "ln":
                at[job] = n
                n += 2
    assert n == 40, n
    return at


CA_STEPS = _ca_order()
CA_JOBS = _ca_jobs(CA_STEPS)
SA_STEPS, CA_STEPS_DVE, FF_STEPS, L1_STEPS = 16, 40, 8, 26
PARAM_DMAS = 1 + 6 + 2 + 1 + 6 + 3 + 3


def kernel(**inputs):
    import numpy as np
    import concourse.bacc as bacc
    from concourse.bass_utils import run_bass_kernel_spmd

    nc = bacc.Bacc("TRN2", target_bir_lowering=False, num_devices=1)
    arrays, args = {}, []
    for name in INPUTS:
        a = np.ascontiguousarray(inputs[name])
        arrays[name] = a
        args.append(nc.dram_tensor(name, a.shape, mybir.dt.from_np(a.dtype), kind="ExternalInput").ap())
    shape = inputs['x'].shape
    args.append(nc.dram_tensor("out", shape, mybir.dt.float32, kind="ExternalOutput").ap())
    xattn_stack_kernel(nc, *args)
    r = run_bass_kernel_spmd(nc, [arrays], core_ids=[0])
    return r.results[0]["out"]
```

```python
import concourse.bass as bass
from concourse import mybir
from contextlib import ExitStack

INPUTS = ['x', 'ctx_768',
          'L0_xattn_ln1_g', 'L0_xattn_ln1_b', 'L0_xattn_w_qkv', 'L0_xattn_w_sa_o', 'L0_xattn_b_sa_o',
          'L0_xattn_ln2_g', 'L0_xattn_ln2_b', 'L0_xattn_w_q', 'L0_xattn_w_kv', 'L0_xattn_w_ca_o', 'L0_xattn_b_ca_o',
          'L0_xattn_ln3_g', 'L0_xattn_ln3_b', 'L0_xattn_w_ff1', 'L0_xattn_b_ff1', 'L0_xattn_w_ff2', 'L0_xattn_b_ff2',
          'L1_xattn_W_proj', 'L1_xattn_b_proj', 'L1_xattn_g_state', 'L1_xattn_beta_state',
          'L1_xattn_g_input', 'L1_xattn_beta_input', 'L1_xattn_g_out', 'L1_xattn_beta_out',
          'L1_xattn_W_u', 'L1_xattn_b_u', 'L1_xattn_W_r', 'L1_xattn_b_r', 'L1_xattn_W_n', 'L1_xattn_b_n']


def xattn_stack_kernel(nc, x, ctx_768, ln1_g, ln1_b, w_qkv, w_sa_o, b_sa_o, ln2_g, ln2_b, w_q, w_kv, w_ca_o, b_ca_o,
                       ln3_g, ln3_b, w_ff1, b_ff1, w_ff2, b_ff2, W_proj, b_proj, g_state, beta_state,
                       g_input, beta_input, g_out, beta_out, W_u, b_u, W_r, b_r, W_n, b_n, out):
    f32 = mybir.dt.float32
    f32r = mybir.dt.float32r
    ALU = mybir.AluOpType
    ACT = mybir.ActivationFunctionType
    AX = mybir.AxisListType
    ds = bass.ds

    B, T, D = x.shape
    S, C = ctx_768.shape[1:]
    L = w_qkv.shape[0]
    INNER = w_q.shape[2]
    DH = 64
    H = INNER // DH
    HP = H // 2
    SP = S + S % 2
    KT = 3
    KC = S // KT
    CL = C - 128
    PAIRS = B // 2
    T2 = 2 * T
    BLK = 1024
    SCALE = DH ** -0.5
    SCALE_OUT = float(D) ** -0.5
    EPS = 1e-5
    PHASES = 3

    SA_J, CA_J, FF_J, L1_J = 20, 40, 4, 18

    ctx = ExitStack()
    with ctx:
        def sb(name, shape, dt=f32):
            return ctx.enter_context(nc.sbuf_tensor(name, shape, dt))

        def sem(name):
            return ctx.enter_context(nc.semaphore(name))

        X = sb("X", [T, B, D])
        WH = sb("WH", [128, 8 * BLK], f32r)
        WL = sb("WL", [128, 8 * BLK], f32r)
        stage = sb("stage", [128, 2, BLK])
        zeros = sb("zeros", [128, BLK // 2])
        hTf = sb("hTf", [128, 2, T2])
        hTh = sb("hTh", [128, 2, T2], f32r)
        hTl = sb("hTl", [128, 2, T2], f32r)
        xn = sb("xn", [T, 2, D])
        bst = sb("bst", [T, 2, 6])
        mv = sb("mv", [T, 2, 2])
        vare = sb("vare", [T, 2])
        rstd = sb("rstd", [T, 2])
        mhalf = sb("mhalf", [128, 2])
        qT = sb("qT", [128, HP, T2])
        kz = sb("kz", [128, HP, 2, T2])
        V = sb("V", [128, 2, KT * INNER])
        qzh = sb("qzh", [128, 2, 2, T], f32r)
        qzl = sb("qzl", [128, 2, 2, T], f32r)
        Kh = sb("Kh", [128, 2, SP], f32r)
        Kl = sb("Kl", [128, 2, SP], f32r)
        CT = sb("CT", [128, 2, 3, SP], f32r)
        P = sb("P", [T, 2, 4 * T])
        PT = sb("PT", [128, 2, 4 * T])
        rs = sb("rs", [T, 2, H])
        rinv = sb("rinv", [T, 2, HP])
        mx = sb("mx", [T, 2, 4])
        spare = sb("spare", [T, 1])
        nb = sb("nb", [T, 2, 4])
        O = sb("O", [T, 2, 8 * DH])
        Gh = sb("Gh", [128, 8, T2], f32r)
        Gl = sb("Gl", [128, 8, T2], f32r)
        ident = sb("ident", [128, 128])
        prow = sb("prow", [128, 128])
        pcol = sb("pcol", [128, 128])
        OB = sb("OB", [T, L * PHASES, D])
        hcols = sb("hcols", [128, 4])
        BP = sb("BP", [KC, D])
        GO = sb("GO", [T, 2, D])

        LNV = 2 * L + 2
        FF_V = 6 * LNV
        L1_V = FF_V + 8 * L
        cols = pcol[:, L1_V:L1_V + 12]

        OTh = Gh[:, :, :].rearrange("p f (a t) -> p (f a) t", a=2)
        OTl = Gl[:, :, :].rearrange("p f (a t) -> p (f a) t", a=2)
        Gf = V[:, 0, 0:8 * T2].rearrange("p (f t) -> p f t", f=8)
        craw = V[0:KC, :, 0:KT * C].rearrange("p b (t c) -> p b t c", t=KT)
        tokT = kz[:, 0:4, :, :].rearrange("p a b c -> p (a b c)")[:, 0:2 * SP].rearrange("p (m s) -> p m s", m=2)
        tok = V[0:KC, 0, 0:KT * D].rearrange("p (t d) -> p t d", t=KT)
        xT = qT[:, 0:2, :]
        uT = qT[:, 2:4, :]
        rT = qT[:, 4:6, :]
        cT = qT[:, 6:8, :]
        inT = kz[:, 4:5, :, :].rearrange("p a m t -> p (a m) t")
        nsT = kz[:, 5:6, :, :].rearrange("p a m t -> p (a m) t")
        rp = kz[:, 6:7, :, :].rearrange("p a m t -> p (a m) t")
        inTh, inTl = Gh[:, 0:2, :], Gl[:, 0:2, :]
        rph, rpl = Gh[:, 2:4, :], Gl[:, 2:4, :]
        xs = V[0:T, 0, 1024:1024 + 2 * D].rearrange("p (b d) -> p b d", b=2)
        routed = V[0:T, 0, 2048:2048 + 2 * D].rearrange("p (b d) -> p b d", b=2)
        y = V[0:T, 1, 0:2 * D].rearrange("p (b d) -> p b d", b=2)
        yn = V[0:T, 1, 1024:1024 + 2 * D].rearrange("p (b d) -> p b d", b=2)

        def bank(name):
            return ctx.enter_context(nc.psum_tensor(name, [128, 512], f32))

        PJ = [bank(f"proj{i}") for i in range(2)]
        SC = [bank(f"scores{i}") for i in range(2)]
        TR = [bank(f"probsT{i}") for i in range(2)]
        OA = [bank(f"attn{i}") for i in range(2)]

        ctxT = nc.dram_tensor("ctxT_scratch", (B, 128, 3 * SP), f32).ap()

        consts_set = sem("consts_set")
        params_in = sem("params_in")
        params_turned = sem("params_turned")
        stage_in = [sem(f"stage_in{i}") for i in range(2)]
        w_split = [sem(f"w_split{i}") for i in range(2)]
        w_high = sem("w_high")
        ctx_raw_in = [sem(f"ctx_raw_in{i}") for i in range(2)]
        ctx_turned = sem("ctx_turned")
        ctx_high = sem("ctx_high")
        ctx_split = [sem(f"ctx_split{i}") for i in range(2)]
        ctx_stored = [sem(f"ctx_stored{i}") for i in range(2)]
        ctx_in = [sem(f"ctx_in{i}") for i in range(2)]
        ln_var = sem("ln_var")
        ln_rstd = sem("ln_rstd")
        ln_xn = sem("ln_xn")
        ln_turned = sem("ln_turned")
        first_affine = sem("first_affine")
        ln_high = sem("ln_high")
        ln_low = sem("ln_low")

        def group(prefix, names, pairs=()):
            return {**{n: sem(f"{prefix}_{n}") for n in names},
                    **{n: [sem(f"{prefix}_{n}{i}") for i in range(2)] for n in pairs}}

        sa = group("sa", ["qk_ready", "v_ready", "s_ready", "nb_ready", "exp_done", "t_ready", "o_ready",
                          "ot_ready", "ot_high", "y_ready", "dve_step"], ["pj_done", "pt_done", "o_done"])
        ca = group("ca", ["q_ready", "v_ready", "k_high", "s_ready", "nb_ready", "exp_done", "t_ready", "o_ready",
                          "ot_ready", "ot_high", "y_ready", "dve_step", "qz_done"],
                   ["pj_done", "pt_done", "o_done", "k_ready"])
        ff = group("ff", ["f_ready", "g_split", "y_ready", "ln_done", "dve_step"], ["pj_done", "y_done"])
        l1 = group("l1", ["xs_done", "x_ready", "tok_ready", "s_ready", "nb_ready", "exp_done", "t_ready", "o_ready",
                          "norm", "var", "rstd", "in_ready", "in_high", "in_low", "g_ready", 
                          "rp_split", "ns_done", "out_ready", "y_done", "y_stored", "dve_step"],
                   ["pj_done", "pt_done"])
        first_step = sem("first_step")

        PRIME = 1
        primed = [*w_split, ctx_turned, *ctx_split, *ctx_stored, *ca["k_ready"], ca["y_ready"], ff["y_ready"], ff["f_ready"],
                  sa["y_ready"], sa["v_ready"], ca["q_ready"], ca["v_ready"], ca["qz_done"], *sa["pj_done"], *sa["pt_done"], *sa["o_done"],
                  sa["exp_done"], *ca["pj_done"], *ca["pt_done"], *ca["o_done"], ca["exp_done"], *ff["pj_done"], *ff["y_done"], *l1["pj_done"],
                  *l1["pt_done"], l1["y_stored"]]

        class Steps:

            def __init__(self, eng, s, base, per):
                self.eng, self.s, self.base, self.per, self.n = eng, s, base, per, 0

            def __call__(self, ins, before_aggr=False):
                self.n += 1
                ins.then_inc(self.s, 1)
                self.eng.wait_ge(self.s, self.base + self.n)
                if before_aggr:
                    nc.vector.tensor_copy(spare[:, :], mhalf[0:T, 0:1])

            def close(self):
                assert self.n == self.per, (self.n, self.per)

        def rows_of(w, k, c0, n):
            return lambda lay, h: w[ds(lay, 1), k * 128 + 64 * h:k * 128 + 64 * h + 64, c0:c0 + n].rearrange(
                "l p n -> (l p) n")

        def tiles_of(w, k0, n=4):
            return lambda lay, h: w[ds(lay, 1), k0 * 128:(k0 + n) * 128, :].rearrange(
                "l (k p) n -> p (l k) n", p=128)[64 * h:64 * h + 64]

        def last_rows_of(w, c0, n):
            return lambda lay, h: w[ds(lay, 1), 128:128 + CL, c0:c0 + n].rearrange("l p n -> (l p) n")

        SA_BLOCKS = [(2, rows_of(w_qkv, 0, INNER, BLK)), (4, rows_of(w_qkv, 0, 2 * INNER, BLK)),
                     (0, rows_of(w_qkv, 0, 0, BLK)), (1, rows_of(w_qkv, 1, 0, BLK)),
                     (3, rows_of(w_qkv, 1, INNER, BLK)), (5, rows_of(w_qkv, 1, 2 * INNER, BLK)),
                     (6, tiles_of(w_sa_o, 0)), (7, tiles_of(w_sa_o, 4))]
        CA_BLOCKS = [(0, rows_of(w_q, 0, 0, BLK)), (1, rows_of(w_q, 1, 0, BLK)),
                     (2, rows_of(w_kv, 0, 0, BLK)), (4, last_rows_of(w_kv, 0, BLK)),
                     (3, rows_of(w_kv, 0, INNER, BLK)), (5, last_rows_of(w_kv, INNER, BLK)),
                     (6, tiles_of(w_ca_o, 0)), (7, tiles_of(w_ca_o, 4))]
        FF_BLOCKS = [(0, rows_of(w_ff1, 0, 0, BLK)), (1, rows_of(w_ff1, 1, 0, BLK)),
                     (3, tiles_of(w_ff2, 0)), (5, tiles_of(w_ff2, 4))]
        flat = lambda w: w.rearrange("(k p) n -> p k n", p=128)
        L1_BLOCKS = [(7, D, lambda h: W_proj[64 * h:64 * h + 64, :]), (0, D, lambda h: W_proj[128:128 + CL, :]),
                     (4, BLK, lambda h: flat(W_r)[64 * h:64 * h + 64]), (2, BLK, lambda h: flat(W_u)[64 * h:64 * h + 64]),
                     (6, BLK, lambda h: flat(W_n)[64 * h:64 * h + 64])]
        PER_LAYER = len(SA_BLOCKS) + len(CA_BLOCKS) + len(FF_BLOCKS)

        SHARED = {"sa": (2, 3, 4, 5), "ca": (14, 15), "ff": (16, 17, 18, 19)}
        LAYER_BLOCKS = SA_BLOCKS + CA_BLOCKS + FF_BLOCKS

        def last_use(n, lay):
            blk = LAYER_BLOCKS[n][0]
            if n < 8:
                if blk in (2, 4):
                    return [(ca["k_ready"][1], lay * (PAIRS * HP))]
                if blk in (6, 7):
                    return [(ca["y_ready"], lay * (PAIRS * 2))]
                if blk in (0, 1):
                    return [(ff["f_ready"], lay * (PAIRS * 4))]
                return [(ff["y_ready"], lay * (PAIRS * 2))]
            if n < 16:
                return [(sa["y_ready"], (lay + 1) * (PAIRS * 2)) if blk in (6, 7) else
                        (sa["v_ready"], (lay + 1) * (PAIRS * 4))]
            return [(ca["q_ready"], (lay + 1) * (PAIRS * 4)) if blk in (0, 1) else
                    (ca["v_ready"], (lay + 1) * (PAIRS * 12))]

        def loads(n, lay):
            return 32 * (lay * (PER_LAYER // 2) + n // 2 + 1)

        def highs(n, lay):
            return 2 * (lay * PER_LAYER + n + 1)

        def wcol(blk, off, n):
            return slice(blk * BLK + off, blk * BLK + off + n)

        block = ctx.enter_context(nc.Block())

        @block.sync
        def _(sp):
            def load_block(n, cols_n, src, done_before):
                sp.wait_ge(w_split[n % 2], PRIME + done_before)
                for h in (1, 0):
                    dst = stage[64 * h:64 * h + 64, n % 2, 0:cols_n]
                    a = src(h)
                    if len(a.shape) == 3:
                        dst = dst.rearrange("p (k n) -> p k n", k=a.shape[1])
                    sp.dma_start(dst, a).then_inc(stage_in[n % 2], 16)

            sp.wait_ge(consts_set, 9)
            sp.dma_start(X[:, :, :], x.rearrange("b t d -> t b d")).then_inc(params_in, 16)
            for n, v in enumerate((ln1_g, ln1_b, ln2_g, ln2_b, ln3_g, ln3_b)):
                sp.dma_start(prow[n * LNV:n * LNV + 2 * L, :], v.rearrange("l (k p) -> (l k) p", p=128)) \
                    .then_inc(params_in, 16)
            for n, v in enumerate((g_state, beta_state)):
                sp.dma_start(prow[n * LNV + 2 * L:n * LNV + 2 * L + 2, :], v.rearrange("(k p) -> k p", p=128)) \
                    .then_inc(params_in, 16)
            sp.dma_start(prow[FF_V:FF_V + L * 8, :], b_ff1.rearrange("l (f p) -> (l f) p", p=128)) \
                .then_inc(params_in, 16)
            for n, v in enumerate((g_input, beta_input, b_proj, b_u, b_r, b_n)):
                sp.dma_start(prow[L1_V + 2 * n:L1_V + 2 * n + 2, :], v.rearrange("(k p) -> k p", p=128)) \
                    .then_inc(params_in, 16)
            for ph, b in enumerate((b_sa_o, b_ca_o, b_ff2)):
                sp.dma_start(OB[:, ph:(L - 1) * PHASES + ph + 1:PHASES, :], b.partition_broadcast(T)) \
                    .then_inc(params_in, 16)
            sp.dma_start(BP[:, :], b_proj.partition_broadcast(KC)).then_inc(params_in, 16)
            sp.dma_start(GO[:, 0, :], g_out.partition_broadcast(T)).then_inc(params_in, 16)
            sp.dma_start(GO[:, 1, :], beta_out.partition_broadcast(T)).then_inc(params_in, 16)

            for s in primed:
                sp.sem_inc(s, PRIME)

            with sp.Fori(0, PAIRS) as i:
                for b in range(2):
                    sp.wait_ge(ctx_turned, PRIME + 2 * i + b)
                    sp.dma_start(craw[:, b, :, :], ctx_768[ds(2 * i + b, 1), :, :].rearrange(
                        "o (t p) c -> p (o t) c", p=KC)).then_inc(ctx_raw_in[b], 16)
                for b in range(2):
                    sp.wait_ge(ctx_split[b], PRIME + i + 1)
                    sp.dma_start(ctxT[ds(2 * i + b, 1), :, :].rearrange("o p n -> p (o n)"),
                                 CT[:, b, :, :].rearrange("p a s -> p (a s)").bitcast(f32)).then_inc(ctx_stored[b], 16)

            def load_ctx(pair, b):
                sp.dma_start(CT[:, b, :, :].rearrange("p a s -> p (a s)").bitcast(f32),
                             ctxT[ds(2 * pair + b, 1), :, :].rearrange("o p n -> p (o n)")).then_inc(ctx_in[b], 16)

            for b in range(2):
                sp.wait_ge(ctx_stored[0], PRIME + 16 * PAIRS)
                sp.wait_ge(ctx_stored[1], PRIME + 16 * PAIRS)
                load_ctx(0, b)

            with sp.Fori(0, L) as lay:
                for n in range(18):
                    load_block(n, BLK, lambda h: LAYER_BLOCKS[n][1](lay, h), lay * (PER_LAYER // 2) + n // 2)
                with sp.Fori(0, PAIRS) as pair:
                    it = lay * PAIRS + pair
                    for b in range(2):
                        sp.wait_ge(ca["k_ready"][b], PRIME + (it + 1) * HP)
                        load_ctx((pair + 1) % PAIRS, b)
                for n in (18, 19):
                    load_block(n, BLK, lambda h: LAYER_BLOCKS[n][1](lay, h), lay * (PER_LAYER // 2) + n // 2)
            for m, (blk, cn, src) in enumerate(L1_BLOCKS):
                load_block(m, cn, src, L * PER_LAYER // 2 + m // 2)
            with sp.Fori(0, PAIRS) as pair:
                for b in range(2):
                    sp.wait_ge(l1["tok_ready"], pair * 8 + 4 * b + 4)
                    load_ctx((pair + 1) % PAIRS, b)
                for b in range(2):
                    sp.wait_ge(l1["y_done"], pair * 2 + b + 1)
                    sp.dma_start(out[ds(2 * pair + b, 1), :, :].rearrange("o t d -> t (o d)"), y[:, b, :]) \
                        .then_inc(l1["y_stored"], 16)
            sp.wait_ge(l1["y_stored"], PRIME + 16 * B)
            for b in range(2):
                sp.wait_ge(ctx_in[b], 16 * (1 + (L + 1) * PAIRS))

        @block.gpsimd
        def _(pool):
            nc.gpsimd.memset(zeros[:, :], 0.0).then_inc(consts_set, 1)
            nc.gpsimd.memset(mhalf[:, :], -0.5).then_inc(consts_set, 1)
            nc.gpsimd.memset(prow[:, :], 0.0).then_inc(consts_set, 1)
            nc.gpsimd.memset(kz[:, :, :, :], 0.0).then_inc(consts_set, 1)
            nc.gpsimd.memset(qzh[:, :, :, :].bitcast(f32), 0.0).then_inc(consts_set, 1)
            nc.gpsimd.memset(qzl[:, :, :, :].bitcast(f32), 0.0).then_inc(consts_set, 1)
            nc.gpsimd.memset(CT[:, :, :, S:SP].bitcast(f32), 0.0).then_inc(consts_set, 1)
            nc.gpsimd.memset(ident[:, :], 0.0).then_inc(consts_set, 1)
            pool.wait_ge(consts_set, 8)
            nc.gpsimd.affine_select(out=ident[:, :], in_=ident[:, :], compare_op=ALU.not_equal, fill=1.0,
                                    base=0, pattern=[[-1, 128]], channel_multiplier=1).then_inc(consts_set, 1)
            pool.wait_ge(consts_set, 9)

            def split_block(n, blk, cols_n, loaded, high, before):
                pool.wait_ge(stage_in[n % 2], loaded)
                pool.wait_ge(w_split[(n + 1) % 2], PRIME + before)
                half = min(cols_n, BLK // 2)
                for c in range(0, cols_n, half):
                    nc.gpsimd.tensor_tensor(WH[:, wcol(blk, c, half)], stage[:, n % 2, c:c + half],
                                            zeros[:, 0:half], ALU.add).then_inc(w_high, 1)
                pool.wait_ge(w_high, high)
                nc.gpsimd.tensor_tensor(WL[:, wcol(blk, 0, cols_n)], stage[:, n % 2, 0:cols_n],
                                        WH[:, wcol(blk, 0, cols_n)].bitcast(f32), ALU.subtract) \
                    .then_inc(w_split[n % 2], 1)

            def layer_blocks(blocks, lay, powers):
                pool.wait_ge(ln_rstd, powers)
                for n in blocks:
                    for s, v in last_use(n, lay):
                        pool.wait_ge(s, PRIME + v)
                    split_block(n, LAYER_BLOCKS[n][0], BLK, loads(n, lay), highs(n, lay),
                                lay * (PER_LAYER // 2) + (n + 1) // 2)

            def power(event, src, dst, ready, done, per=1):
                pool.wait_ge(ready, event)
                nc.gpsimd.tensor_tensor(dst, src, mhalf[0:T, 0:2], ALU.pow).then_inc(done, 1)

            power(1, vare[:, :], rstd[:, :], ln_var, ln_rstd)
            with pool.Fori(0, L) as lay:
                layer_blocks((0, 1, 6, 7), lay, lay * (PHASES * PAIRS) + 1)
                with pool.Fori(0, PAIRS) as pair:
                    pool.wait_ge(w_split[1], PRIME + lay * (PER_LAYER // 2) + 4)
                    pool.wait_ge(ln_rstd, lay * (PHASES * PAIRS) + pair + 1)
                    power(lay * (PHASES * PAIRS) + pair + 2, vare[:, :], rstd[:, :], ln_var, ln_rstd)
                layer_blocks(range(8, 14), lay, lay * (PHASES * PAIRS) + PAIRS + 1)
                with pool.Fori(0, PAIRS) as pair:
                    pool.wait_ge(w_split[1], PRIME + lay * (PER_LAYER // 2) + 7)
                    it = lay * PAIRS + pair
                    pool.wait_ge(ca["qz_done"], PRIME + it * (8 * HP))
                    pool.wait_ge(ln_rstd, lay * (PHASES * PAIRS) + PAIRS + pair + 1)
                    power(lay * (PHASES * PAIRS) + PAIRS + pair + 2, vare[:, :], rstd[:, :], ln_var, ln_rstd)
                    pool.wait_ge(ln_rstd, lay * (PHASES * PAIRS) + PAIRS + pair + 2)
                    for hp in range(2 * HP):
                        b, h2 = hp // HP, hp % HP
                        if hp == 0:
                            for i in range(2):
                                pool.wait_ge(ca["pj_done"][i], PRIME + it * (CA_J // 2) + 2)
                        if hp >= 2:
                            pool.wait_ge(ca["s_ready"], it * (2 * H) + 2 * hp - 2)
                        pool.wait_ge(ca["qz_done"], PRIME + it * (8 * HP) + 4 * hp)
                        for a in range(2):
                            src = qT[64 * a:64 * a + 64, h2, b * T:(b + 1) * T]
                            nc.gpsimd.tensor_tensor(qzh[64 * a:64 * a + 64, hp % 2, a, :], src,
                                                    zeros[64 * a:64 * a + 64, 0:T], ALU.add).then_inc(ca["qz_done"], 1)
                        pool.wait_ge(ca["qz_done"], PRIME + it * (8 * HP) + 4 * hp + 2)
                        for a in range(2):
                            src = qT[64 * a:64 * a + 64, h2, b * T:(b + 1) * T]
                            nc.gpsimd.tensor_tensor(qzl[64 * a:64 * a + 64, hp % 2, a, :], src,
                                                    qzh[64 * a:64 * a + 64, hp % 2, a, :].bitcast(f32),
                                                    ALU.subtract).then_inc(ca["qz_done"], 1)
                with pool.Fori(0, PAIRS) as pair:
                    pool.wait_ge(ca["qz_done"], PRIME + (lay + 1) * (PAIRS * 8 * HP))
                    pool.wait_ge(ln_rstd, lay * (PHASES * PAIRS) + 2 * PAIRS + pair + 1)
                    power(lay * (PHASES * PAIRS) + 2 * PAIRS + pair + 2, vare[:, :], rstd[:, :], ln_var, ln_rstd)
            high = L * PER_LAYER * 2
            for m, (blk, cn, src) in enumerate(L1_BLOCKS):
                if m == 0:
                    pool.wait_ge(ln_rstd, L * (PHASES * PAIRS) + 1)
                    pool.wait_ge(ca["y_ready"], PRIME + L * PAIRS * 2)
                if m == 1:
                    pool.wait_ge(ff["f_ready"], PRIME + L * PAIRS * 4)
                high += max(1, cn // (BLK // 2))
                split_block(m, blk, cn, loads(m, L), high, L * (PER_LAYER // 2) + (m + 1) // 2)
            with pool.Fori(0, PAIRS) as pair:
                pool.wait_ge(w_split[0], PRIME + (L * PER_LAYER + len(L1_BLOCKS) + 1) // 2)
                pool.wait_ge(ln_rstd, L * (PHASES * PAIRS) + pair + 1)
                power(pair * 2 + 1, vare[:, :], rstd[:, :], l1["var"], l1["rstd"])
                pool.wait_ge(l1["rstd"], pair * 2 + 1)
                power(pair * 2 + 2, vare[:, :], rstd[:, :], l1["var"], l1["rstd"])
                pool.wait_ge(l1["rstd"], pair * 2 + 2)
                power(L * (PHASES * PAIRS) + pair + 2, vare[:, :], rstd[:, :], ln_var, ln_rstd)

        @block.tensor
        def _(pe):
            def three(o, sh, sl, mh, ml, start, stop):
                nc.tensor.matmul(o, sh, mh, start=start, stop=False)
                nc.tensor.matmul(o, sh, ml, start=False, stop=False)
                return nc.tensor.matmul(o, sl, mh, start=False, stop=stop)

            def turn(o, src, n):
                return nc.tensor.transpose(o, src, ident[0:n, 0:n])

            def ln_turn(banks, event, pj=None, j=0):
                for b in range(2):
                    if pj:
                        pj(j + b)
                    pe.wait_ge(ln_xn, event * 2 + b + 1)
                    turn(banks[b][:, 0:T], xn[:, b, 0:128], T)
                    turn(banks[b][:, T:T2], xn[:, b, 128:256], T).then_inc(ln_turned, 1)

            pe.wait_ge(consts_set, 9)
            with pe.Fori(0, PAIRS) as i:
                for b in range(2):
                    pe.wait_ge(ctx_raw_in[b], 16 * (i + 1))
                    pe.wait_ge(ctx_split[b], PRIME + i)
                    for t in range(KT):
                        turn(SC[b][:, t * KC:(t + 1) * KC], craw[:, b, t, 0:128], KC)
                    for t in range(KT):
                        last = turn(TR[b][0:CL, t * KC:(t + 1) * KC], craw[:, b, t, 128:C], KC)
                    last.then_inc(ctx_turned, 1)
            for b in range(2):
                pe.wait_ge(ctx_split[b], PRIME + PAIRS)
            pe.wait_ge(params_in, 16 * PARAM_DMAS)
            turn(OA[0][:, 0:128], prow[:, :], 128).then_inc(params_turned, 1)
            for b in range(2):
                pe.wait_ge(ln_xn, b + 1)
                turn(PJ[b][:, 0:T], xn[:, b, 0:128], T)
                turn(PJ[b][:, T:T2], xn[:, b, 128:256], T).then_inc(ln_turned, 1)

            with pe.Fori(0, L) as lay:
                w0 = lay * (PER_LAYER // 2)
                git0 = lay * (PHASES * PAIRS)
                with pe.Fori(0, PAIRS) as pair:
                    pe.wait_ge(w_split[0], PRIME + w0 + 3)
                    pe.wait_ge(w_split[1], PRIME + w0 + 2)
                    for i in range(2):
                        pe.wait_ge(ff["pj_done"][i], PRIME + lay * (PAIRS * FF_J // 2))
                        pe.wait_ge(ff["y_done"][i], PRIME + lay * PAIRS)
                        pe.wait_ge(ca["exp_done"], PRIME + lay * (PAIRS * 2 * H))
                        pe.wait_ge(ca["pt_done"][i], PRIME + lay * (PAIRS * H))
                        pe.wait_ge(ca["o_done"][i], PRIME + lay * (PAIRS * 2))
                    it = lay * PAIRS + pair
                    pb = it * (SA_J // 2)

                    def pj(j):
                        pe.wait_ge(sa["pj_done"][j % 2], PRIME + pb + j // 2)
                        return PJ[j % 2]

                    def pj_out(j):
                        pe.wait_ge(sa["pj_done"][j % 2], PRIME + pb + j // 2 + 1)

                    pe.wait_ge(ln_low, git0 + pair + 1)
                    for hp in range(HP):
                        o = pj(hp)
                        for a in range(2):
                            for k in range(2):
                                w = wcol(2 * a + k, hp * 128, 128)
                                last = three(o[:, a * T2:(a + 1) * T2], WH[:, w], WL[:, w], hTh[:, k, :], hTl[:, k, :],
                                             k == 0, k == 1)
                        last.then_inc(sa["qk_ready"], 1)

                    def scores(s):
                        b = s // 4
                        for c in range(2):
                            hp = 2 * (s % 4) + c
                            last = nc.tensor.matmul(SC[s % 2][0:T, c * T2:(c + 1) * T2], qT[:, hp, b * T:(b + 1) * T],
                                                    kz[:, hp, :, b * T:(b + 1) * T], start=True, stop=True)
                        last.then_inc(sa["s_ready"], 1)

                    pe.wait_ge(sa["exp_done"], PRIME + it * 8)
                    scores(0)
                    scores(1)
                    pe.wait_ge(w_split[1], PRIME + w0 + 3)
                    for b in range(2):
                        for n in range(2):
                            o = pj(8 + 2 * b + n)
                            for k in range(2):
                                w = wcol(4 + k, n * 512, 512)
                                tt = slice(b * T, (b + 1) * T)
                                last = three(o[0:T, :], hTh[:, k, tt], hTl[:, k, tt], WH[:, w], WL[:, w], k == 0, k == 1)
                            last.then_inc(sa["v_ready"], 1)
                    ln_turn([PJ[0], PJ[1]], git0 + pair + 1, pj, 12)

                    def turn_out(i, j):
                        o = pj(j)
                        pe.wait_ge(sa["o_done"][i % 2], PRIME + it * 2 + i // 2 + 1)
                        for c in range(4):
                            last = turn(o[:, c * T:(c + 1) * T], O[:, i % 2, c * 128:(c + 1) * 128], T)
                        last.then_inc(sa["ot_ready"], 1)

                    def project(o, b, cs):
                        for c in cs:
                            w = wcol(6, c * D, D)
                            last = three(o[0:T, 0:D], OTh[:, 8 * b + c, :], OTl[:, 8 * b + c, :], WH[:, w], WL[:, w],
                                         c == 0, c == HP - 1)
                        return last

                    for s in range(2, 11):
                        g = s - 2
                        if 0 <= g < 8:
                            pe.wait_ge(sa["exp_done"], PRIME + it * 8 + g + 1)
                            pe.wait_ge(sa["pt_done"][g % 2], PRIME + it * 4 + g // 2)
                            for c in range(4):
                                last = turn(TR[g % 2][0:T, c * T:(c + 1) * T], P[:, g % 2, c * T:(c + 1) * T], T)
                            last.then_inc(sa["t_ready"], 1)
                        if 2 <= s < 8:
                            scores(s)
                        g = s - 3
                        if 0 <= g < 8:
                            i = g // 2
                            pe.wait_ge(sa["pt_done"][g % 2], PRIME + it * 4 + g // 2 + 1)
                            if g % 2 == 0:
                                pe.wait_ge(sa["o_done"][i % 2], PRIME + it * 2 + i // 2)
                            if g % 4 == 0:
                                pj_out(8 + 2 * (g // 4))
                                pj_out(9 + 2 * (g // 4))
                            for c in range(4):
                                h = 4 * (g % 4) + c
                                oc = (4 * (g % 2) + c) * DH
                                last = nc.tensor.matmul(OA[i % 2][0:T, oc:oc + DH], PT[0:T, g % 2, c * T:(c + 1) * T],
                                                        V[0:T, g // 4, h * DH:(h + 1) * DH], start=True, stop=True)
                            if g % 2 == 1:
                                last.then_inc(sa["o_ready"], 1)
                        if s == 5:
                            turn_out(0, 14)
                        if s == 7:
                            turn_out(1, 16)
                        if s == 9:
                            turn_out(2, 15)
                    for k in range(2):
                        pe.wait_ge(w_split[k], PRIME + w0 + 4)
                    pj_out(16)
                    y0 = pj(18)
                    project(y0, 0, range(0, 5))
                    turn_out(3, 17)
                    project(y0, 0, range(5, HP)).then_inc(sa["y_ready"], 1)
                    pj_out(15)
                    project(pj(19), 1, range(HP)).then_inc(sa["y_ready"], 1)

                with pe.Fori(0, PAIRS) as pair:
                    for i in range(2):
                        pe.wait_ge(sa["pj_done"][i], PRIME + (lay + 1) * (PAIRS * SA_J // 2))
                        pe.wait_ge(sa["pt_done"][i], PRIME + (lay + 1) * (PAIRS * 4))
                        pe.wait_ge(sa["o_done"][i], PRIME + (lay + 1) * (PAIRS * 2))
                        pe.wait_ge(w_split[i], PRIME + w0 + 5)
                    pe.wait_ge(sa["exp_done"], PRIME + (lay + 1) * (PAIRS * 8))
                    it = lay * PAIRS + pair
                    pb = it * (CA_J // 2)

                    def pj(j):
                        pe.wait_ge(ca["pj_done"][j % 2], PRIME + pb + j // 2)
                        return PJ[j % 2]

                    def pj_out(j):
                        pe.wait_ge(ca["pj_done"][j % 2], PRIME + pb + j // 2 + 1)

                    pe.wait_ge(ln_low, git0 + PAIRS + pair + 1)
                    for q in range(4):
                        o = pj(q)
                        for a in range(2):
                            for k in range(2):
                                w = wcol(k, (2 * q + a) * 128, 128)
                                last = three(o[:, a * T2:(a + 1) * T2], WH[:, w], WL[:, w], hTh[:, k, :], hTl[:, k, :],
                                             k == 0, k == 1)
                        last.then_inc(ca["q_ready"], 1)

                    def values(b, n):
                        t, c = n // 2, n % 2
                        tt = slice(t * KC, (t + 1) * KC)
                        o = pj(CA_JOBS[("v", b, n)])
                        w, wl = wcol(3, c * 512, 512), wcol(5, c * 512, 512)
                        three(o[0:KC, :], CT[:, b, 0, tt], CT[:, b, 1, tt], WH[:, w], WL[:, w], True, False)
                        nc.tensor.matmul(o[0:KC, :], CT[:, b, 2, tt], WH[:, wl], start=False, stop=False)
                        nc.tensor.matmul(o[0:KC, :], CT[:, b, 2, tt], WL[:, wl], start=False, stop=True) \
                            .then_inc(ca["v_ready"], 1)

                    def keys(hp):
                        b, h2 = hp // HP, hp % HP
                        o = pj(CA_JOBS[("k", hp)])
                        w, wl = wcol(2, h2 * 128, 128), wcol(4, h2 * 128, 128)
                        three(o[:, 0:SP], WH[:, w], WL[:, w], CT[:, b, 0, :], CT[:, b, 1, :], True, False)
                        nc.tensor.matmul(o[:, 0:SP], WH[:, wl], CT[:, b, 2, :], start=False, stop=False)
                        nc.tensor.matmul(o[:, 0:SP], WL[:, wl], CT[:, b, 2, :], start=False, stop=True) \
                            .then_inc(ca["k_ready"][b], 1)

                    def turn_out(i):
                        o = pj(CA_JOBS[("ot", i)])
                        pe.wait_ge(ca["o_done"][i % 2], PRIME + it * 2 + i // 2 + 1)
                        for c in range(4):
                            last = turn(o[:, c * T:(c + 1) * T], O[:, i % 2, c * 128:(c + 1) * 128], T)
                        last.then_inc(ca["ot_ready"], 1)

                    def project(b, cs):
                        j = CA_JOBS[("y", b)]
                        o = pj(j) if cs[0] == 0 else PJ[j % 2]
                        if cs[0] == 0:
                            pj_out(CA_JOBS[("ot", 2 * b + 1)])
                        for c in cs:
                            w = wcol(6, c * D, D)
                            last = three(o[0:T, 0:D], OTh[:, 8 * b + c, :], OTl[:, 8 * b + c, :], WH[:, w], WL[:, w],
                                         c == 0, c == HP - 1)
                        if cs[-1] == HP - 1:
                            last.then_inc(ca["y_ready"], 1)

                    def scores(h):
                        hp, a = h // 2, h % 2
                        if h < 2:
                            pe.wait_ge(ca["exp_done"], PRIME + it * (2 * H))
                        if a == 0:
                            pe.wait_ge(ca["qz_done"], PRIME + it * (8 * HP) + 4 * hp + 4)
                            pj_out(CA_JOBS[("k", hp)])
                        three(SC[h % 2][0:T, 0:SP], qzh[:, hp % 2, a, :], qzl[:, hp % 2, a, :], Kh[:, hp % 2, :],
                              Kl[:, hp % 2, :], True, True).then_inc(ca["s_ready"], 1)

                    def turn_probs(h):
                        pe.wait_ge(ca["exp_done"], PRIME + it * (2 * H) + h + 1)
                        pe.wait_ge(ca["pt_done"][h % 2], PRIME + it * H + h // 2)
                        for t in range(KT):
                            last = turn(TR[h % 2][0:KC, t * T:(t + 1) * T], P[:, h % 2, t * KC:(t + 1) * KC], T)
                        last.then_inc(ca["t_ready"], 1)

                    def attend(h):
                        i, b = h // 8, h // H
                        pe.wait_ge(ca["pt_done"][h % 2], PRIME + it * H + h // 2 + 1)
                        if h % 8 == 0:
                            pe.wait_ge(ca["o_done"][i % 2], PRIME + it * 2 + i // 2)
                        if h % H == 0:
                            pj_out(CA_JOBS[("v", b, 4)])
                            pj_out(CA_JOBS[("v", b, 5)])
                        oc = (h % 8) * DH
                        for t in range(KT):
                            vc = t * INNER + (h % H) * DH
                            last = nc.tensor.matmul(OA[i % 2][0:T, oc:oc + DH], PT[0:KC, h % 2, t * T:(t + 1) * T],
                                                    V[0:KC, b, vc:vc + DH], start=t == 0, stop=t == KT - 1)
                        if h % 8 == 7:
                            last.then_inc(ca["o_ready"], 1)

                    for job in CA_ORDER:
                        if job[0] == "v":
                            if job[2] == 0:
                                pe.wait_ge(ctx_in[job[1]], 16 * (it + 1))
                                for i in range(2):
                                    pe.wait_ge(w_split[i], PRIME + w0 + 7)
                            values(job[1], job[2])
                        elif job[0] == "k":
                            if job[1] == 0:
                                pe.wait_ge(ctx_in[0], 16 * (it + 1))
                                for i in range(2):
                                    pe.wait_ge(w_split[i], PRIME + w0 + 6)
                            keys(job[1])
                        elif job[0] == "ln":
                            ln_turn([PJ[CA_JOBS[job] % 2], PJ[(CA_JOBS[job] + 1) % 2]], git0 + PAIRS + pair + 1,
                                    pj, CA_JOBS[job])
                        elif job[0] == "ot":
                            turn_out(job[1])
                        elif job[0] == "y":
                            if job[1] == 0:
                                for i in range(2):
                                    pe.wait_ge(w_split[i], PRIME + w0 + 8)
                            project(job[1], job[2])
                        elif job[0] == "s":
                            scores(job[1])
                        elif job[0] == "t":
                            turn_probs(job[1])
                        elif job[0] == "pv":
                            attend(job[1])

                with pe.Fori(0, PAIRS) as pair:
                    for i in range(2):
                        pe.wait_ge(ca["pj_done"][i], PRIME + (lay + 1) * (PAIRS * CA_J // 2))
                        pe.wait_ge(w_split[i], PRIME + w0 + 9)
                    it = lay * PAIRS + pair
                    pb = it * (FF_J // 2)

                    def pj(j):
                        pe.wait_ge(ff["pj_done"][j % 2], PRIME + pb + j // 2)
                        return PJ[j % 2]

                    pe.wait_ge(ln_low, git0 + 2 * PAIRS + pair + 1)
                    for q in range(4):
                        o = pj(q)
                        for a in range(2):
                            for k in range(2):
                                w = wcol(k, (2 * q + a) * 128, 128)
                                last = three(o[:, a * T2:(a + 1) * T2], WH[:, w], WL[:, w], hTh[:, k, :], hTl[:, k, :],
                                             k == 0, k == 1)
                        last.then_inc(ff["f_ready"], 1)
                    ln_turn([SC[0], SC[1]], git0 + 2 * PAIRS + pair + 1)
                    for i in range(2):
                        pe.wait_ge(w_split[i], PRIME + w0 + 10)
                        pe.wait_ge(ff["y_done"][i], PRIME + it)
                    for f0, f1 in ((0, 6), (6, 8)):
                        for b in range(2):
                            for f in range(f0, f1):
                                if b == 0 and f % 2 == 0:
                                    pe.wait_ge(ff["g_split"], it * 4 + f // 2 + 1)
                                w = wcol(3 + 2 * (f // 4), (f % 4) * D, D)
                                tt = slice(b * T, (b + 1) * T)
                                last = three(OA[b][0:T, 0:D], Gh[:, f, tt], Gl[:, f, tt], WH[:, w], WL[:, w],
                                             f == 0, f == 7)
                            if f1 == 8:
                                last.then_inc(ff["y_ready"], 1)

            for i in range(2):
                pe.wait_ge(ff["pj_done"][i], PRIME + L * (PAIRS * FF_J // 2))
                pe.wait_ge(ff["y_done"][i], PRIME + L * PAIRS)
                pe.wait_ge(w_split[i], PRIME + L * (PER_LAYER // 2) + 1)
            with pe.Fori(0, PAIRS) as pair:
                pb = pair * (L1_J // 2)

                def pj(j):
                    pe.wait_ge(l1["pj_done"][j % 2], PRIME + pb + j // 2)
                    return PJ[j % 2]

                def pj_out(j):
                    pe.wait_ge(l1["pj_done"][j % 2], PRIME + pb + j // 2 + 1)

                pe.wait_ge(l1["xs_done"], pair + 1)
                o = pj(0)
                for b in range(2):
                    for k in range(2):
                        last = turn(o[:, k * T2 + b * T:k * T2 + (b + 1) * T], xs[:, b, k * 128:(k + 1) * 128], T)
                last.then_inc(l1["x_ready"], 1)
                for b in range(2):
                    pe.wait_ge(ctx_in[b], 16 * (L * PAIRS + pair + 1))
                    for m in range(2):
                        o = pj(1 + 4 * b + m)
                        w, wl = wcol(7, m * 128, 128), wcol(0, m * 128, 128)
                        three(o[:, 0:SP], WH[:, w], WL[:, w], CT[:, b, 0, :], CT[:, b, 1, :], True, False)
                        nc.tensor.matmul(o[:, 0:SP], WH[:, wl], CT[:, b, 2, :], start=False, stop=False)
                        nc.tensor.matmul(o[:, 0:SP], WL[:, wl], CT[:, b, 2, :], start=False, stop=True) \
                            .then_inc(l1["tok_ready"], 1)
                    for n, ts in enumerate(((0, 1), (2,))):
                        o = pj(3 + 4 * b + n)
                        for c, t in enumerate(ts):
                            tt = slice(t * KC, (t + 1) * KC)
                            oc = o[0:KC, c * D:(c + 1) * D]
                            w, wl = wcol(7, 0, D), wcol(0, 0, D)
                            three(oc, CT[:, b, 0, tt], CT[:, b, 1, tt], WH[:, w], WL[:, w], True, False)
                            nc.tensor.matmul(oc, CT[:, b, 2, tt], WH[:, wl], start=False, stop=False)
                            last = nc.tensor.matmul(oc, CT[:, b, 2, tt], WL[:, wl], start=False, stop=True)
                        last.then_inc(l1["tok_ready"], 1)
                    pj_out(0)
                    pj_out(1 + 4 * b)
                    pj_out(2 + 4 * b)
                    for k in range(2):
                        last = nc.tensor.matmul(SC[b][0:T, 0:SP], xT[:, k, b * T:(b + 1) * T], tokT[:, k, :],
                                                start=k == 0, stop=k == 1)
                    last.then_inc(l1["s_ready"], 1)
                    pe.wait_ge(l1["exp_done"], pair * 2 + b + 1)
                    pe.wait_ge(l1["pt_done"][b], PRIME + pair)
                    for t in range(KT):
                        last = turn(TR[b][0:KC, t * T:(t + 1) * T], P[:, b, t * KC:(t + 1) * KC], T)
                    last.then_inc(l1["t_ready"], 1)
                    pj_out(3 + 4 * b)
                    pj_out(4 + 4 * b)
                    pe.wait_ge(l1["pt_done"][b], PRIME + pair + 1)
                    for t in range(KT):
                        last = nc.tensor.matmul(OA[b][0:T, 0:D], PT[0:KC, b, t * T:(t + 1) * T], tok[:, t, :],
                                                start=t == 0, stop=t == KT - 1)
                    last.then_inc(l1["o_ready"], 1)
                for b in range(2):
                    o = pj(9 + b)
                    pe.wait_ge(l1["norm"], pair * 2 + b + 1)
                    for k in range(2):
                        last = turn(o[:, k * T:(k + 1) * T], xn[:, b, k * 128:(k + 1) * 128], T)
                    last.then_inc(l1["in_ready"], 1)
                pe.wait_ge(ln_low, L * (PHASES * PAIRS) + pair + 1)
                pe.wait_ge(l1["in_low"], pair + 1)

                def gate(j, blk, kh, kl):
                    o = pj(j)
                    srcs = [(kh, kl, 0), (kh, kl, 1), (inTh, inTl, 0), (inTh, inTl, 1)]
                    for m in range(2):
                        for n, (h, l, k) in enumerate(srcs):
                            w = wcol(blk, n * D + m * 128, 128)
                            last = three(o[:, m * T2:(m + 1) * T2], WH[:, w], WL[:, w], h[:, k, :], l[:, k, :],
                                         n == 0, n == 3)
                    last.then_inc(l1["g_ready"], 1)

                pe.wait_ge(w_split[0], PRIME + L * (PER_LAYER // 2) + 3)
                pe.wait_ge(w_split[1], PRIME + L * (PER_LAYER // 2) + 2)
                gate(11, 4, hTh, hTl)
                gate(12, 2, hTh, hTl)
                pe.wait_ge(l1["rp_split"], pair + 1)
                gate(13, 6, rph, rpl)
                pe.wait_ge(l1["ns_done"], pair + 1)
                for b in range(2):
                    o = pj(14 + b)
                    for k in range(2):
                        last = turn(o[0:T, k * 128:(k + 1) * 128], nsT[:, k, b * T:(b + 1) * T], 128)
                    last.then_inc(l1["out_ready"], 1)
                ln_turn([PJ[0], PJ[1]], L * (PHASES * PAIRS) + pair + 1, pj, 16)

        @block.scalar
        def _(act):
            def copy(o, i):
                return nc.scalar.activation(o, i, ACT.Copy)

            def affine_done(pj_done, base, j):
                for n in (j, j + 1):
                    act.wait_ge(pj_done[n % 2], PRIME + base + n // 2 + 1)

            act.wait_ge(consts_set, 9)
            with act.Fori(0, PAIRS) as i:
                for b in range(2):
                    act.wait_ge(ctx_turned, PRIME + 2 * i + b + 1)
                    act.wait_ge(ctx_stored[b], PRIME + 16 * i)
                    copy(CT[:, b, 0, 0:S], SC[b][:, 0:S])
                    copy(CT[0:CL, b, 2, 0:S], TR[b][0:CL, 0:S]).then_inc(ctx_high, 1)
            def split_high(blocks, lay):
                for n in blocks:
                    for s, v in last_use(n, lay):
                        act.wait_ge(s, PRIME + v)
                    act.wait_ge(stage_in[n % 2], loads(n, lay))
                    act.wait_ge(w_high, highs(n - 1, lay))
                    copy(WH[:, wcol(LAYER_BLOCKS[n][0], 0, BLK)], stage[:, n % 2, :]).then_inc(w_high, 2)

            act.wait_ge(first_affine, 2)
            copy(hTh[:, :, :], hTf[:, :, :]).then_inc(ln_high, 1)

            with act.Fori(0, L) as lay:
                split_high(SHARED["sa"], lay)
                with act.Fori(0, PAIRS) as pair:
                    it = lay * PAIRS + pair
                    pb = it * (SA_J // 2)
                    for hp in range(HP):
                        act.wait_ge(sa["qk_ready"], it * 8 + hp + 1)
                        o = PJ[hp % 2]
                        copy(qT[:, hp, :], o[:, 0:T2])
                        copy(kz[0:64, hp, 0, :], o[0:64, T2:2 * T2])
                        copy(kz[64:128, hp, 1, :], o[64:128, T2:2 * T2]).then_inc(sa["pj_done"][hp % 2], 1)

                    def out_high(i, j):
                        act.wait_ge(sa["ot_ready"], it * 4 + i + 1)
                        copy(OTh[:, 4 * i:4 * i + 4, :].rearrange("p c t -> p (c t)"), PJ[j % 2][:, 0:4 * T]) \
                            .then_inc(sa["ot_high"], 1)

                    for s in range(11):
                        if s < 8:
                            act.wait_ge(sa["nb_ready"], it * 8 + s + 1)
                            for c in range(4):
                                h = 4 * (s % 4) + c
                                last = nc.scalar.activation(P[:, s % 2, c * T:(c + 1) * T], SC[s % 2][0:T, c * T:(c + 1) * T],
                                                            ACT.Exp, bias=nb[:, s % 2, c:c + 1], scale=SCALE,
                                                            accum_out=rs[:, s // 4, h:h + 1])
                            last.then_inc(sa["exp_done"], 1)
                        if s == 2:
                            affine_done(sa["pj_done"], pb, 12)
                            copy(hTh[:, :, :], hTf[:, :, :]).then_inc(ln_high, 1)
                        if s == 5:
                            out_high(0, 14)
                        if s == 7:
                            out_high(1, 16)
                        if s == 9:
                            out_high(2, 15)
                        if s == 10:
                            out_high(3, 17)

                split_high(SHARED["ca"], lay)
                with act.Fori(0, PAIRS) as pair:
                    it = lay * PAIRS + pair
                    for q in range(4):
                        act.wait_ge(ca["q_ready"], PRIME + it * 4 + q + 1)
                        copy(qT[:, 2 * q:2 * q + 2, :].rearrange("p a t -> p (a t)"), PJ[q % 2][:, 0:2 * T2]) \
                            .then_inc(ca["pj_done"][q % 2], 1)
                    for job in CA_ORDER:
                        if job[0] == "k":
                            hp = job[1]
                            b = hp // HP
                            act.wait_ge(ca["k_ready"][b], PRIME + it * HP + hp % HP + 1)
                            copy(Kh[:, hp % 2, :], PJ[CA_JOBS[job] % 2][:, 0:SP]).then_inc(ca["k_high"], 1)
                        elif job[0] == "ln":
                            affine_done(ca["pj_done"], it * (CA_J // 2), CA_JOBS[job])
                            copy(hTh[:, :, :], hTf[:, :, :]).then_inc(ln_high, 1)
                        elif job[0] == "ot":
                            i = job[1]
                            act.wait_ge(ca["ot_ready"], it * 4 + i + 1)
                            copy(OTh[:, 4 * i:4 * i + 4, :].rearrange("p c t -> p (c t)"),
                                 PJ[CA_JOBS[job] % 2][:, 0:4 * T]).then_inc(ca["ot_high"], 1)
                        elif job[0] == "s":
                            h = job[1]
                            act.wait_ge(ca["nb_ready"], it * (2 * H) + h + 1)
                            nc.scalar.activation(P[:, h % 2, 0:S], SC[h % 2][0:T, 0:S], ACT.Exp,
                                                 bias=nb[:, h % 2, 0:1], scale=SCALE,
                                                 accum_out=rs[:, h // H, h % H:h % H + 1]).then_inc(ca["exp_done"], 1)
                        elif job[0] == "t":
                            h = job[1]
                            act.wait_ge(ca["t_ready"], it * (2 * H) + h + 1)
                            copy(PT[0:KC, h % 2, 0:KT * T], TR[h % 2][0:KC, 0:KT * T]).then_inc(ca["pt_done"][h % 2], 1)

                split_high(SHARED["ff"], lay)
                with act.Fori(0, PAIRS) as pair:
                    it = lay * PAIRS + pair
                    for q in range(4):
                        act.wait_ge(ff["f_ready"], PRIME + it * 4 + q + 1)
                        for a in range(2):
                            f = 2 * q + a
                            last = nc.scalar.activation(Gf[:, f, :], PJ[q % 2][:, a * T2:(a + 1) * T2], ACT.Gelu,
                                                        bias=pcol[:, ds(FF_V + lay * 8 + f, 1)])
                        last.then_inc(ff["pj_done"][q % 2], 1)
                    act.wait_ge(ff["ln_done"], 2 * (it + 1))
                    copy(hTh[:, :, :], hTf[:, :, :]).then_inc(ln_high, 1)

            with act.Fori(0, PAIRS) as pair:
                pb = pair * (L1_J // 2)
                act.wait_ge(ff["dve_step"], L * PAIRS * FF_STEPS)
                copy(xs[:, :, :], X[:, ds(2 * pair, 2), :]).then_inc(l1["xs_done"], 1)
                act.wait_ge(l1["x_ready"], pair + 1)
                copy(xT[:, :, :].rearrange("p k t -> p (k t)"), PJ[0][:, 0:2 * T2]).then_inc(l1["pj_done"][0], 1)
                for b in range(2):
                    act.wait_ge(l1["nb_ready"], pair * 2 + b + 1)
                    nc.scalar.activation(P[:, b, 0:S], SC[b][0:T, 0:S], ACT.Exp, bias=nb[:, b, 0:1], scale=SCALE_OUT,
                                         accum_out=rs[:, b, 0:1]).then_inc(l1["exp_done"], 1)
                    act.wait_ge(l1["t_ready"], pair * 2 + b + 1)
                    copy(PT[0:KC, b, 0:KT * T], TR[b][0:KC, 0:KT * T]).then_inc(l1["pt_done"][b], 1)
                affine_done(l1["pj_done"], pb, 9)
                copy(inTh, inT).then_inc(l1["in_high"], 1)
                for n, (dst, j, c0) in enumerate(((rT, 11, 2), (uT, 12, 0))):
                    act.wait_ge(l1["g_ready"], pair * 3 + n + 1)
                    for m in range(2):
                        last = nc.scalar.activation(dst[:, m, :], PJ[j % 2][:, m * T2:(m + 1) * T2], ACT.Tanh,
                                                    bias=hcols[:, c0 + m:c0 + m + 1], scale=0.5)
                    last.then_inc(l1["pj_done"][j % 2], 1)
                act.wait_ge(l1["g_ready"], pair * 3 + 3)
                for m in range(2):
                    last = nc.scalar.activation(cT[:, m, :], PJ[1][:, m * T2:(m + 1) * T2], ACT.Tanh,
                                                bias=cols[:, 10 + m:11 + m])
                last.then_inc(l1["pj_done"][1], 1)
                affine_done(l1["pj_done"], pb, 16)
                copy(hTh[:, :, :], hTf[:, :, :]).then_inc(ln_high, 1)

        @block.vector
        def _(dve):
            def ln_stats(step, nxt):
                for b in range(2):
                    last = nc.vector.bn_stats(bst[:, b, :], X[:, ds(2 * nxt + b, 1), :].rearrange("p o d -> p (o d)"))
                step(last, before_aggr=True)
                for b in range(2):
                    last = nc.vector.bn_aggr(mv[:, b, :], bst[:, b, :])
                step(last)
                nc.vector.tensor_scalar(vare[:, :], mv[:, :, 1], EPS, None, ALU.add).then_inc(ln_var, 1)

            def ln_norm(nxt, var_value):
                dve.wait_ge(ln_rstd, var_value)
                for b in range(2):
                    nc.vector.tensor_scalar(xn[:, b, :], X[:, ds(2 * nxt + b, 1), :].rearrange("p o d -> p (o d)"),
                                            mv[:, b, 0:1], rstd[:, b:b + 1], ALU.subtract, ALU.mult).then_inc(ln_xn, 1)

            def ln_affine_to(gcol, banks, done, event):
                for b in range(2):
                    dve.wait_ge(ln_turned, event * 2 + b + 1)
                    for k in range(2):
                        ins = nc.vector.tensor_scalar(hTf[:, k, b * T:(b + 1) * T], banks[b][:, k * T:(k + 1) * T],
                                                      pcol[:, ds(gcol + k, 1)], pcol[:, ds(gcol + LNV + k, 1)],
                                                      ALU.mult, ALU.add)
                    ins.then_inc(done[b], 1)

            def split_low(blocks, lay):
                for n in blocks:
                    c = wcol(LAYER_BLOCKS[n][0], 0, BLK)
                    dve.wait_ge(w_high, highs(n, lay))
                    nc.vector.tensor_tensor(WL[:, c], stage[:, n % 2, :], WH[:, c].bitcast(f32), ALU.subtract) \
                        .then_inc(w_split[n % 2], 1)

            def ln_low_part(event):
                dve.wait_ge(ln_high, event + 1)
                nc.vector.tensor_tensor(hTl[:, :, :], hTf[:, :, :], hTh[:, :, :].bitcast(f32), ALU.subtract) \
                    .then_inc(ln_low, 1)

            def negmax(step, h, src, n, scale):
                step(nc.vector.reduce_max(mx[:, h % 2, 0:n], src, AX.X))
                return nc.vector.tensor_scalar(nb[:, h % 2, 0:n], mx[:, h % 2, 0:n], -scale, None, ALU.mult)

            def normalise(step, i, s, base_step, done):
                step(nc.vector.reciprocal(rinv[:, i % 2, :], rs[:, i // 2, 8 * (i % 2):8 * (i % 2) + 8]))
                nc.vector.tensor_tensor(O[:, i % 2, :].rearrange("p (h d) -> p h d", h=8),
                                        OA[i % 2][0:T, :].rearrange("p (h d) -> p h d", h=8),
                                        rinv[:, i % 2, :].unsqueeze(2).broadcast_to([T, 8, DH]),
                                        ALU.mult).then_inc(done, 1)

            def out_low(i, bk, s, pj_done):
                nc.vector.tensor_tensor(OTl[:, 4 * i:4 * i + 4, :].rearrange("p c t -> p (c t)"),
                                        PJ[bk][:, 0:4 * T],
                                        OTh[:, 4 * i:4 * i + 4, :].rearrange("p c t -> p (c t)").bitcast(f32),
                                        ALU.subtract).then_inc(pj_done[bk], 1)

            def residual(step, bt, y, slot, read, added):
                xb = X[:, ds(bt, 1), :].rearrange("p o d -> p (o d)")
                nc.vector.tensor_tensor(xb, y[0:T, 0:D], xb, ALU.add).then_inc(read, 1)
                dve.wait_ge(read, PRIME + added)
                step(nc.vector.tensor_tensor(xb, xb, OB[:, ds(slot, 1), :].rearrange("p o d -> p (o d)"), ALU.add))

            dve.wait_ge(consts_set, 9)
            with dve.Fori(0, PAIRS) as i:
                for b in range(2):
                    dve.wait_ge(ctx_high, 2 * i + b + 1)
                    nc.vector.tensor_tensor(CT[:, b, 1, 0:S], SC[b][:, 0:S], CT[:, b, 0, 0:S].bitcast(f32), ALU.subtract)
                    nc.vector.tensor_tensor(CT[CL:2 * CL, b, 2, 0:S], TR[b][0:CL, 0:S], CT[0:CL, b, 2, 0:S].bitcast(f32),
                                            ALU.subtract).then_inc(ctx_split[b], 1)
            dve.wait_ge(params_in, 16 * PARAM_DMAS)
            dve.wait_ge(params_turned, 1)
            nc.vector.tensor_copy(pcol[:, :], OA[0][:, 0:128]).then_inc(first_step, 1)
            dve.wait_ge(first_step, 1)
            nc.vector.tensor_scalar(hcols[:, :], cols[:, 6:10], 0.5, None, ALU.mult)
            step = Steps(dve, first_step, 1, 2)
            ln_stats(step, 0)
            step.close()
            ln_norm(0, 1)
            ln_affine_to(0, PJ, [first_affine, first_affine], 0)
            ln_low_part(0)

            with dve.Fori(0, L) as lay:
                split_low(SHARED["sa"], lay)
                with dve.Fori(0, PAIRS) as pair:
                    it = lay * PAIRS + pair
                    event = lay * (PHASES * PAIRS) + pair + 1
                    nxt = (pair + 1) % PAIRS
                    gcol = 2 * lay + (pair + 1) // PAIRS * (2 * LNV)
                    step = Steps(dve, sa["dve_step"], it * SA_STEPS, SA_STEPS)

                    def sa_negmax(s):
                        dve.wait_ge(sa["s_ready"], it * 8 + s + 1)
                        negmax(step, s, SC[s % 2][0:T, 0:4 * T].rearrange("p (c t) -> p c t", c=4), 4, SCALE) \
                            .then_inc(sa["nb_ready"], 1)

                    ln_stats(step, nxt)
                    ln_norm(nxt, event + 1)
                    for s in range(2):
                        sa_negmax(s)
                    for n in range(4):
                        j = 8 + n
                        dve.wait_ge(sa["v_ready"], PRIME + it * 4 + n + 1)
                        nc.vector.tensor_copy(V[0:T, n // 2, (n % 2) * 512:(n % 2) * 512 + 512], PJ[j % 2][0:T, :]) \
                            .then_inc(sa["pj_done"][j % 2], 1)
                    ln_affine_to(gcol, PJ, sa["pj_done"], event)
                    for s in range(2, 11):
                        if s < 8:
                            sa_negmax(s)
                        g = s - 2
                        if 0 <= g < 8:
                            dve.wait_ge(sa["t_ready"], it * 8 + g + 1)
                            nc.vector.tensor_copy(PT[0:T, g % 2, :], TR[g % 2][0:T, 0:4 * T]) \
                                .then_inc(sa["pt_done"][g % 2], 1)
                        if s == 3:
                            ln_low_part(event)
                        if s in (4, 6, 8, 10):
                            i = (s - 4) // 2
                            dve.wait_ge(sa["o_ready"], it * 4 + i + 1)
                            normalise(step, i, s, 0, sa["o_done"][i % 2])
                        for at, i, j in ((5, 0, 14), (7, 1, 16), (9, 2, 15), (10, 3, 17)):
                            if s == at:
                                dve.wait_ge(sa["ot_high"], it * 4 + i + 1)
                                out_low(i, j % 2, s, sa["pj_done"])
                    for b in range(2):
                        dve.wait_ge(sa["y_ready"], PRIME + it * 2 + b + 1)
                        residual(step, 2 * pair + b, PJ[b], lay * PHASES, sa["pj_done"][b], (it + 1) * (SA_J // 2))
                    step.close()

                split_low(SHARED["ca"], lay)
                with dve.Fori(0, PAIRS) as pair:
                    it = lay * PAIRS + pair
                    event = lay * (PHASES * PAIRS) + PAIRS + pair + 1
                    nxt = (pair + 1) % PAIRS
                    gcol = 2 * LNV + 2 * lay + (pair + 1) // PAIRS * (2 * LNV)
                    step = Steps(dve, ca["dve_step"], it * CA_STEPS_DVE, CA_STEPS_DVE)
                    ln_stats(step, nxt)
                    ln_norm(nxt, event + 1)
                    for job in CA_ORDER:
                        bk = CA_JOBS.get(job[:2] if job[0] == "y" else job, 0) % 2
                        if job[0] == "v":
                            b, n = job[1], job[2]
                            dve.wait_ge(ca["v_ready"], PRIME + it * 12 + 6 * b + n + 1)
                            vc = (n // 2) * INNER + (n % 2) * 512
                            nc.vector.tensor_copy(V[0:KC, b, vc:vc + 512], PJ[bk][0:KC, :]).then_inc(ca["pj_done"][bk], 1)
                        elif job[0] == "k":
                            hp = job[1]
                            dve.wait_ge(ca["k_high"], it * (2 * HP) + hp + 1)
                            nc.vector.tensor_tensor(Kl[:, hp % 2, :], PJ[bk][:, 0:SP], Kh[:, hp % 2, :].bitcast(f32),
                                                    ALU.subtract).then_inc(ca["pj_done"][bk], 1)
                        elif job[0] == "s":
                            h = job[1]
                            dve.wait_ge(ca["s_ready"], it * (2 * H) + h + 1)
                            negmax(step, h, SC[h % 2][0:T, 0:S], 1, SCALE).then_inc(ca["nb_ready"], 1)
                        elif job[0] == "ln":
                            b0 = CA_JOBS[job] % 2
                            ln_affine_to(gcol, (PJ[b0], PJ[1 - b0]), (ca["pj_done"][b0], ca["pj_done"][1 - b0]), event)
                        elif job[0] == "lnlow":
                            ln_low_part(event)
                        elif job[0] == "pv" and job[1] % 8 == 7:
                            i = job[1] // 8
                            dve.wait_ge(ca["o_ready"], it * 4 + i + 1)
                            normalise(step, i, 0, 0, ca["o_done"][i % 2])
                        elif job[0] == "ot":
                            dve.wait_ge(ca["ot_high"], it * 4 + job[1] + 1)
                            out_low(job[1], bk, 0, ca["pj_done"])
                        elif job[0] == "y" and job[2][-1] == HP - 1:
                            dve.wait_ge(ca["y_ready"], PRIME + it * 2 + job[1] + 1)
                            residual(step, 2 * pair + job[1], PJ[bk], lay * PHASES + 1, ca["pj_done"][bk],
                                     it * (CA_J // 2) + CA_JOBS[job[:2]] // 2 + 1)
                    step.close()

                split_low(SHARED["ff"], lay)
                with dve.Fori(0, PAIRS) as pair:
                    it = lay * PAIRS + pair
                    event = lay * (PHASES * PAIRS) + 2 * PAIRS + pair + 1
                    nxt = (pair + 1) % PAIRS
                    gcol = 4 * LNV + 2 * lay - (pair + 1) // PAIRS * (4 * LNV - 2)
                    step = Steps(dve, ff["dve_step"], it * FF_STEPS, FF_STEPS)
                    ln_stats(step, nxt)
                    for q in range(4):
                        dve.wait_ge(ff["pj_done"][q % 2], PRIME + it * (FF_J // 2) + q // 2 + 1)
                        step(nc.vector.tensor_copy(Gh[:, 2 * q:2 * q + 2, :], Gf[:, 2 * q:2 * q + 2, :]))
                        nc.vector.tensor_tensor(Gl[:, 2 * q:2 * q + 2, :], Gf[:, 2 * q:2 * q + 2, :],
                                                Gh[:, 2 * q:2 * q + 2, :].bitcast(f32), ALU.subtract).then_inc(ff["g_split"], 1)
                        if q == 0:
                            ln_norm(nxt, event + 1)
                    ln_affine_to(gcol, SC, (ff["ln_done"], ff["ln_done"]), event)
                    ln_low_part(event)
                    for b in range(2):
                        dve.wait_ge(ff["y_ready"], PRIME + it * 2 + b + 1)
                        residual(step, 2 * pair + b, OA[b], lay * PHASES + 2, ff["y_done"][b], it + 1)
                    step.close()

            with dve.Fori(0, PAIRS) as pair:
                event = L * (PHASES * PAIRS) + pair + 1
                step = Steps(dve, l1["dve_step"], pair * L1_STEPS, L1_STEPS)
                for b in range(2):
                    for m in range(2):
                        j = 1 + 4 * b + m
                        dve.wait_ge(l1["tok_ready"], pair * 8 + 4 * b + m + 1)
                        nc.vector.tensor_scalar(tokT[:, m, :], PJ[j % 2][:, 0:SP], cols[:, 4 + m:5 + m], None, ALU.add) \
                            .then_inc(l1["pj_done"][j % 2], 1)
                    for n, ts in enumerate(((0, 1), (2,))):
                        j = 3 + 4 * b + n
                        dve.wait_ge(l1["tok_ready"], pair * 8 + 4 * b + n + 3)
                        for c, t in enumerate(ts):
                            last = nc.vector.tensor_tensor(tok[:, t, :], PJ[j % 2][0:KC, c * D:(c + 1) * D], BP[:, :], ALU.add)
                        last.then_inc(l1["pj_done"][j % 2], 1)
                    dve.wait_ge(l1["s_ready"], pair * 2 + b + 1)
                    negmax(step, b, SC[b][0:T, 0:S], 1, SCALE_OUT).then_inc(l1["nb_ready"], 1)
                    dve.wait_ge(l1["o_ready"], pair * 2 + b + 1)
                    step(nc.vector.reciprocal(rinv[:, b, 0:1], rs[:, b, 0:1]))
                    step(nc.vector.tensor_scalar(routed[:, b, :], OA[b][0:T, 0:D], rinv[:, b, 0:1], None, ALU.mult))
                    step(nc.vector.bn_stats(bst[:, b, :], routed[:, b, :]), before_aggr=True)
                    step(nc.vector.bn_aggr(mv[:, b, :], bst[:, b, :]))
                nc.vector.tensor_scalar(vare[:, :], mv[:, :, 1], EPS, None, ALU.add).then_inc(l1["var"], 1)
                dve.wait_ge(l1["rstd"], pair * 2 + 1)
                for b in range(2):
                    nc.vector.tensor_scalar(xn[:, b, :], routed[:, b, :], mv[:, b, 0:1], rstd[:, b:b + 1],
                                            ALU.subtract, ALU.mult).then_inc(l1["norm"], 1)
                for b in range(2):
                    dve.wait_ge(l1["in_ready"], pair * 2 + b + 1)
                    for k in range(2):
                        ins = nc.vector.tensor_scalar(inT[:, k, b * T:(b + 1) * T], PJ[(9 + b) % 2][:, k * T:(k + 1) * T],
                                                      cols[:, k:k + 1], cols[:, 2 + k:3 + k], ALU.mult, ALU.add)
                    ins.then_inc(l1["pj_done"][(9 + b) % 2], 1)
                dve.wait_ge(l1["in_high"], pair + 1)
                nc.vector.tensor_tensor(inTl, inT, inTh.bitcast(f32), ALU.subtract).then_inc(l1["in_low"], 1)
                pb = pair * (L1_J // 2)
                dve.wait_ge(l1["pj_done"][1], PRIME + pb + 11 // 2 + 1)
                step(nc.vector.tensor_scalar(rT, rT, 0.5, 0.5, ALU.mult, ALU.add))
                step(nc.vector.tensor_tensor(rp, rT, hTf[:, :, :], ALU.mult))
                step(nc.vector.tensor_copy(rph, rp))
                nc.vector.tensor_tensor(rpl, rp, rph.bitcast(f32), ALU.subtract).then_inc(l1["rp_split"], 1)
                dve.wait_ge(l1["pj_done"][0], PRIME + pb + 12 // 2 + 1)
                step(nc.vector.tensor_scalar(uT, uT, 0.5, 0.5, ALU.mult, ALU.add))
                dve.wait_ge(l1["pj_done"][1], PRIME + pb + 13 // 2 + 1)
                step(nc.vector.tensor_tensor(cT, cT, xT, ALU.subtract))
                step(nc.vector.tensor_tensor(cT, cT, uT, ALU.mult))
                nc.vector.tensor_tensor(nsT, cT, xT, ALU.add).then_inc(l1["ns_done"], 1)
                for b in range(2):
                    dve.wait_ge(l1["out_ready"], pair * 2 + b + 1)
                    nc.vector.tensor_copy(yn[:, b, :], PJ[b][0:T, 0:D]).then_inc(l1["pj_done"][b], 1)
                    dve.wait_ge(l1["pj_done"][b], PRIME + pb + 14 // 2 + 1)
                    step(nc.vector.bn_stats(bst[:, b, :], yn[:, b, :]), before_aggr=True)
                    step(nc.vector.bn_aggr(mv[:, b, :], bst[:, b, :]))
                nc.vector.tensor_scalar(vare[:, :], mv[:, :, 1], EPS, None, ALU.add).then_inc(l1["var"], 1)
                dve.wait_ge(l1["rstd"], pair * 2 + 2)
                for b in range(2):
                    step(nc.vector.tensor_scalar(yn[:, b, :], yn[:, b, :], mv[:, b, 0:1], rstd[:, b:b + 1],
                                                 ALU.subtract, ALU.mult))
                    step(nc.vector.tensor_tensor(yn[:, b, :], yn[:, b, :], GO[:, 0, :], ALU.mult))
                    dve.wait_ge(l1["y_stored"], PRIME + pair * 32)
                    nc.vector.tensor_tensor(y[:, b, :], yn[:, b, :], GO[:, 1, :], ALU.add).then_inc(l1["y_done"], 1)
                ln_stats(step, (pair + 1) % PAIRS)
                ln_norm((pair + 1) % PAIRS, event + 1)
                ln_affine_to(2 * L, PJ, l1["pj_done"], event)
                ln_low_part(event)
                step.close()


def _ca_order():
    order = [("k", 0), ("v", 0, 0), ("v", 0, 1), ("k", 1), ("s", 0), ("s", 1)] + [("v", 0, n) for n in range(2, 6)]
    for s in range(2, 35):
        if s % 2 == 0 and s // 2 + 1 < 16:
            order.append(("k", s // 2 + 1))
        if s - 2 < 32:
            order.append(("t", s - 2))
        if s < 32:
            order.append(("s", s))
        if 0 <= s - 3:
            order.append(("pv", s - 3))
        if 4 <= s < 10:
            order.append(("v", 1, s - 4))
        order += {12: [("ot", 0)], 20: [("ot", 1)], 28: [("ot", 2)], 23: [("ln",)], 25: [("lnlow",)]}.get(s, [])
    return order + [("y", 0, (0, 1, 2, 3, 4)), ("ot", 3), ("y", 0, (5, 6, 7)), ("y", 1, (0, 1, 2, 3, 4, 5, 6, 7))]


def _ca_jobs(order):
    at, n = {}, 4
    for job in order:
        if job[0] in ("v", "k") or job[0] == "ot" and job[1] < 2:
            at[job] = n
            n += 1
        if job[0] == "ln":
            at[job] = n
            n += 2
    assert n == 36, n
    at.update({("ot", 2): 36, ("y", 0): 38, ("ot", 3): 37, ("y", 1): 39})
    return at


CA_ORDER = _ca_order()
CA_JOBS = _ca_jobs(CA_ORDER)
SA_STEPS, CA_STEPS_DVE, FF_STEPS, L1_STEPS = 16, 40, 8, 26
PARAM_DMAS = 1 + 6 + 2 + 1 + 6 + 3 + 3


def kernel(**inputs):
    import numpy as np
    import concourse.bacc as bacc
    from concourse.bass_utils import run_bass_kernel_spmd

    nc = bacc.Bacc("TRN2", target_bir_lowering=False, num_devices=1)
    arrays, args = {}, []
    for name in INPUTS:
        a = np.ascontiguousarray(inputs[name])
        arrays[name] = a
        args.append(nc.dram_tensor(name, a.shape, mybir.dt.from_np(a.dtype), kind="ExternalInput").ap())
    shape = inputs['x'].shape
    args.append(nc.dram_tensor("out", shape, mybir.dt.float32, kind="ExternalOutput").ap())
    xattn_stack_kernel(nc, *args)
    r = run_bass_kernel_spmd(nc, [arrays], core_ids=[0])
    return r.results[0]["out"]
```

```python
import concourse.bass as bass
from concourse import mybir
from contextlib import ExitStack

INPUTS = ['x', 'ctx_768',
          'L0_xattn_ln1_g', 'L0_xattn_ln1_b', 'L0_xattn_w_qkv', 'L0_xattn_w_sa_o', 'L0_xattn_b_sa_o',
          'L0_xattn_ln2_g', 'L0_xattn_ln2_b', 'L0_xattn_w_q', 'L0_xattn_w_kv', 'L0_xattn_w_ca_o', 'L0_xattn_b_ca_o',
          'L0_xattn_ln3_g', 'L0_xattn_ln3_b', 'L0_xattn_w_ff1', 'L0_xattn_b_ff1', 'L0_xattn_w_ff2', 'L0_xattn_b_ff2',
          'L1_xattn_W_proj', 'L1_xattn_b_proj', 'L1_xattn_g_state', 'L1_xattn_beta_state',
          'L1_xattn_g_input', 'L1_xattn_beta_input', 'L1_xattn_g_out', 'L1_xattn_beta_out',
          'L1_xattn_W_u', 'L1_xattn_b_u', 'L1_xattn_W_r', 'L1_xattn_b_r', 'L1_xattn_W_n', 'L1_xattn_b_n']


def xattn_stack_kernel(nc, x, ctx_768, ln1_g, ln1_b, w_qkv, w_sa_o, b_sa_o, ln2_g, ln2_b, w_q, w_kv, w_ca_o, b_ca_o,
                       ln3_g, ln3_b, w_ff1, b_ff1, w_ff2, b_ff2, W_proj, b_proj, g_state, beta_state,
                       g_input, beta_input, g_out, beta_out, W_u, b_u, W_r, b_r, W_n, b_n, out):
    f32 = mybir.dt.float32
    f32r = mybir.dt.float32r
    ALU = mybir.AluOpType
    ACT = mybir.ActivationFunctionType
    AX = mybir.AxisListType
    ds = bass.ds

    B, T, D = x.shape
    S, C = ctx_768.shape[1:]
    L = w_qkv.shape[0]
    INNER = w_q.shape[2]
    DH = 64
    H = INNER // DH
    HP = H // 2
    SP = S + S % 2
    KT = 3
    KC = S // KT
    CL = C - 128
    PAIRS = B // 2
    T2 = 2 * T
    BLK = 1024
    SLOTS = 4
    ROUNDS = B // 4
    SCALE = DH ** -0.5
    SCALE_OUT = float(D) ** -0.5
    EPS = 1e-5
    PHASES = 3

    SA_J, CA_J, FF_J, L1_J = 18, 38, 4, 12

    ctx = ExitStack()
    with ctx:
        def sb(name, shape, dt=f32):
            return ctx.enter_context(nc.sbuf_tensor(name, shape, dt))

        def sem(name):
            return ctx.enter_context(nc.semaphore(name))

        X = sb("X", [T, B, D])
        WH = sb("WH", [128, 8 * BLK], f32r)
        WL = sb("WL", [128, 8 * BLK], f32r)
        stage = sb("stage", [128, SLOTS, BLK])
        zeros = sb("zeros", [128, BLK // 2])
        hTf = sb("hTf", [128, 2, T2])
        hTh = sb("hTh", [128, 2, T2], f32r)
        hTl = sb("hTl", [128, 2, T2], f32r)
        xn = sb("xn", [T, 2, D])
        bst = sb("bst", [T, 2, 6])
        mv = sb("mv", [T, 2, 2])
        vare = sb("vare", [T, 2])
        rstd = sb("rstd", [T, 2])
        mhalf = sb("mhalf", [128, 2])
        qT = sb("qT", [128, HP, T2])
        kz = sb("kz", [128, HP, 2, T2])
        V = sb("V", [128, 2, KT * INNER])
        qzh = sb("qzh", [128, 2, 2, T], f32r)
        qzl = sb("qzl", [128, 2, 2, T], f32r)
        Kh = sb("Kh", [128, 2, SP], f32r)
        Kl = sb("Kl", [128, 2, SP], f32r)
        CT = sb("CT", [128, 2, 3, SP], f32r)
        P = sb("P", [T, 2, 4 * T])
        PT = sb("PT", [128, 2, 4 * T])
        rs = sb("rs", [T, 2, H])
        rinv = sb("rinv", [T, 2, HP])
        mx = sb("mx", [T, 2, 4])
        spare = sb("spare", [T, 1])
        warm = sb("warm", [128, 1])
        nb = sb("nb", [T, 2, 4])
        O = sb("O", [128, 2, 8 * DH])
        Gh = sb("Gh", [128, 8, T2], f32r)
        Gl = sb("Gl", [128, 8, T2], f32r)
        ident = sb("ident", [128, 128])
        prow = sb("prow", [128, 128])
        pcol = sb("pcol", [128, 128])
        OB = sb("OB", [T, L * PHASES, D])
        hcols = sb("hcols", [128, 4])

        LNV = 2 * L + 2
        FF_V = 6 * LNV
        L1_V = FF_V + 8 * L
        cols = pcol[:, L1_V:L1_V + 12]

        OTh = Gh[:, :, :].rearrange("p f (a t) -> p (f a) t", a=2)
        OTl = Gl[:, :, :].rearrange("p f (a t) -> p (f a) t", a=2)
        Gf = V[:, 0, 0:8 * T2].rearrange("p (f t) -> p f t", f=8)
        craw = [V[0:KC, u % 2, (u // 2) * 1024:(u // 2) * 1024 + KT * C].rearrange("p (t c) -> p t c", t=KT)
                for u in range(4)]
        ctx_slots = [CT[:, 0, :, :], CT[:, 1, :, :]] + [
            g.rearrange("p f t -> p (f t)")[:, 0:3 * SP].rearrange("p (a s) -> p a s", a=3) for g in (Gh, Gl)]
        tokT = kz[:, 0:4, :, :].rearrange("p a b c -> p (a b c)")[:, 0:4 * SP].rearrange("p (b m s) -> p b m s", b=2, m=2)
        tok = [V[0:KC, b, c:c + KT * D].rearrange("p (t d) -> p t d", t=KT) for b, c in ((0, 0), (1, 2048))]
        xT = qT[:, 0:2, :]
        uT = qT[:, 2:4, :]
        rT = qT[:, 4:6, :]
        cT = qT[:, 6:8, :]
        inT = kz[:, 4:5, :, :].rearrange("p a m t -> p (a m) t")
        nsT = kz[:, 5:6, :, :].rearrange("p a m t -> p (a m) t")
        rp = kz[:, 6:7, :, :].rearrange("p a m t -> p (a m) t")
        inTh, inTl = Gh[:, 0:2, :], Gl[:, 0:2, :]
        rph, rpl = Gh[:, 2:4, :], Gl[:, 2:4, :]
        GO = O[0:T, 0, :].rearrange("p (v d) -> p v d", v=2)
        BP = O[0:KC, 1, 0:D]
        xs = V[0:T, 0, 1024:1024 + 2 * D].rearrange("p (b d) -> p b d", b=2)
        routed = V[0:T, 0, 2048:2048 + 2 * D].rearrange("p (b d) -> p b d", b=2)
        y = V[0:T, 1, 0:2 * D].rearrange("p (b d) -> p b d", b=2)
        yn = V[0:T, 1, 1024:1024 + 2 * D].rearrange("p (b d) -> p b d", b=2)

        def bank(name):
            return ctx.enter_context(nc.psum_tensor(name, [128, 512], f32))

        PJ = [bank(f"proj{i}") for i in range(2)]
        SC = [bank(f"scores{i}") for i in range(2)]
        TR = [bank(f"probsT{i}") for i in range(2)]
        OA = [bank(f"attn{i}") for i in range(2)]

        ctx_banks = [(SC[0], TR[0]), (SC[1], TR[1]), (OA[0], PJ[0]), (OA[1], PJ[1])]

        ctxT = nc.dram_tensor("ctxT_scratch", (B, 128, 3 * SP), f32).ap()

        consts_set = sem("consts_set")
        params_in = sem("params_in")
        params_turned = sem("params_turned")
        stage_in = [sem(f"stage_in{i}") for i in range(SLOTS)]
        w_split = [sem(f"w_split{i}") for i in range(SLOTS)]
        w_high = sem("w_high")
        ctx_raw_in = [sem(f"ctx_raw_in{i}") for i in range(4)]
        ctx_turned = sem("ctx_turned")
        ctx_high = sem("ctx_high")
        ctx_split = [sem(f"ctx_split{i}") for i in range(4)]
        ctx_stored = [sem(f"ctx_stored{i}") for i in range(4)]
        ctx_in = [sem(f"ctx_in{i}") for i in range(2)]
        ln_var = sem("ln_var")
        ln_rstd = sem("ln_rstd")
        ln_xn = sem("ln_xn")
        ln_turned = sem("ln_turned")
        first_affine = sem("first_affine")
        ln_high = sem("ln_high")
        ln_low = sem("ln_low")

        def group(prefix, names, pairs=()):
            return {**{n: sem(f"{prefix}_{n}") for n in names},
                    **{n: [sem(f"{prefix}_{n}{i}") for i in range(2)] for n in pairs}}

        sa = group("sa", ["qk_ready", "v_ready", "s_ready", "nb_ready", "exp_done", "t_ready", "o_ready",
                          "ot_ready", "ot_high", "y_ready", "dve_step"], ["pj_done", "pt_done", "o_done", "y_done"])
        ca = group("ca", ["q_ready", "v_ready", "k_high", "s_ready", "nb_ready", "exp_done", "t_ready", "o_ready",
                          "ot_ready", "ot_high", "y_ready", "dve_step", "qz_done"],
                   ["pj_done", "pt_done", "o_done", "y_done", "k_ready"])
        ff = group("ff", ["f_ready", "g_split", "y_ready", "ln_done", "dve_step"], ["pj_done", "y_done"])
        l1 = group("l1", ["xs_done", "x_ready", "tok_ready", "s_ready", "nb_ready", "exp_done", "t_ready", "o_ready",
                          "norm", "var", "rstd", "in_ready", "in_high", "in_low", "g_ready", 
                          "rp_split", "ns_done", "out_ready", "y_done", "y_stored", "in_done", "ln_done", "vectors_in", "dve_step"],
                   ["pj_done", "pt_done", "out_read"])
        first_step = sem("first_step")

        PRIME = 1
        primed = [*w_split, *ctx_in, *l1["out_read"], *ctx_split, *ctx_stored, *ca["k_ready"], ca["y_ready"], ff["y_ready"], ff["f_ready"],
                  sa["y_ready"], sa["v_ready"], ca["q_ready"], ca["v_ready"], ca["qz_done"], *sa["pj_done"], *sa["pt_done"], *sa["o_done"],
                  sa["exp_done"], *ca["pj_done"], *ca["pt_done"], *ca["o_done"], ca["exp_done"], *sa["y_done"], *ca["y_done"], *ff["pj_done"], *ff["y_done"], *l1["pj_done"],
                  *l1["pt_done"], l1["y_stored"]]

        class Steps:

            def __init__(self, eng, s, base, per):
                self.eng, self.s, self.base, self.per, self.n = eng, s, base, per, 0

            def __call__(self, ins, before_aggr=False):
                self.n += 1
                ins.then_inc(self.s, 1)
                self.eng.wait_ge(self.s, self.base + self.n)
                if before_aggr:
                    nc.vector.tensor_copy(spare[:, :], mhalf[0:T, 0:1])

            def close(self):
                assert self.n == self.per, (self.n, self.per)

        def rows_of(w, k, c0, n):
            return lambda lay, h: w[ds(lay, 1), k * 128 + 64 * h:k * 128 + 64 * h + 64, c0:c0 + n].rearrange(
                "l p n -> (l p) n")

        def tiles_of(w, k0, n=4):
            return lambda lay, h: w[ds(lay, 1), k0 * 128:(k0 + n) * 128, :].rearrange(
                "l (k p) n -> p (l k) n", p=128)[64 * h:64 * h + 64]

        def last_rows_of(w, c0, n):
            return lambda lay, h: w[ds(lay, 1), 128:128 + CL, c0:c0 + n].rearrange("l p n -> (l p) n")

        SA_BLOCKS = [(2, rows_of(w_qkv, 0, INNER, BLK)), (4, rows_of(w_qkv, 0, 2 * INNER, BLK)),
                     (0, rows_of(w_qkv, 0, 0, BLK)), (1, rows_of(w_qkv, 1, 0, BLK)),
                     (3, rows_of(w_qkv, 1, INNER, BLK)), (5, rows_of(w_qkv, 1, 2 * INNER, BLK)),
                     (6, tiles_of(w_sa_o, 0)), (7, tiles_of(w_sa_o, 4))]
        CA_BLOCKS = [(0, rows_of(w_q, 0, 0, BLK)), (1, rows_of(w_q, 1, 0, BLK)),
                     (2, rows_of(w_kv, 0, 0, BLK)), (4, last_rows_of(w_kv, 0, BLK)),
                     (3, rows_of(w_kv, 0, INNER, BLK)), (5, last_rows_of(w_kv, INNER, BLK)),
                     (6, tiles_of(w_ca_o, 0)), (7, tiles_of(w_ca_o, 4))]
        FF_BLOCKS = [(0, rows_of(w_ff1, 0, 0, BLK)), (1, rows_of(w_ff1, 1, 0, BLK)),
                     (3, tiles_of(w_ff2, 0)), (5, tiles_of(w_ff2, 4))]
        flat = lambda w: w.rearrange("(k p) n -> p k n", p=128)
        L1_BLOCKS = [(7, D, lambda h: W_proj[64 * h:64 * h + 64, :]), (0, D, lambda h: W_proj[128:128 + CL, :]),
                     (4, BLK, lambda h: flat(W_r)[64 * h:64 * h + 64]), (2, BLK, lambda h: flat(W_u)[64 * h:64 * h + 64]),
                     (6, BLK, lambda h: flat(W_n)[64 * h:64 * h + 64])]
        PER_LAYER = len(SA_BLOCKS) + len(CA_BLOCKS) + len(FF_BLOCKS)

        SHARED = {"sa": (2, 3, 4, 5), "ca": (14, 15), "ff": (18, 19)}
        LOW_BY_POOL = (2,)
        LAYER_BLOCKS = SA_BLOCKS + CA_BLOCKS + FF_BLOCKS

        def last_use(n, lay):
            blk = LAYER_BLOCKS[n][0]
            if n < 8:
                if blk in (2, 4):
                    return [(ca["k_ready"][1], lay * (PAIRS * HP))]
                if blk in (6, 7):
                    return [(ca["y_ready"], lay * (PAIRS * 2))]
                if blk in (0, 1):
                    return [(ff["f_ready"], lay * (PAIRS * 4))]
                return [(ff["y_ready"], lay * (PAIRS * 2))]
            if n < 16:
                if blk in (0, 1, 2, 3):
                    return [(sa["qk_ready"], (lay + 1) * (PAIRS * HP) - PRIME)]
                return [(sa["y_ready"], (lay + 1) * (PAIRS * 2)) if blk in (6, 7) else
                        (sa["v_ready"], (lay + 1) * (PAIRS * 4))]
            return [(ca["q_ready"], (lay + 1) * (PAIRS * 4)) if blk in (0, 1) else
                    (ca["v_ready"], (lay + 1) * (PAIRS * 12))]

        def loads(n, lay):
            return 32 * (lay * (PER_LAYER // SLOTS) + n // SLOTS + 1)

        def split_until(n, lay):
            return PRIME + lay * (PER_LAYER // SLOTS) + n // SLOTS + 1

        def highs(n, lay):
            return 2 * (lay * PER_LAYER + n + 1)

        def wcol(blk, off, n):
            return slice(blk * BLK + off, blk * BLK + off + n)

        block = ctx.enter_context(nc.Block())

        @block.sync
        def _(sp):
            def load_block(n, cols_n, src, done_before):
                sp.wait_ge(w_split[n % SLOTS], done_before)
                for h in (1, 0):
                    dst = stage[64 * h:64 * h + 64, n % SLOTS, 0:cols_n]
                    a = src(h)
                    if len(a.shape) == 3:
                        dst = dst.rearrange("p (k n) -> p k n", k=a.shape[1])
                    sp.dma_start(dst, a).then_inc(stage_in[n % SLOTS], 16)

            for s in primed:
                sp.sem_inc(s, PRIME)
            sp.wait_ge(consts_set, 1)
            sp.dma_start(X[:, :, :], x.rearrange("b t d -> t b d")).then_inc(params_in, 16)
            for n, v in enumerate((ln1_g, ln1_b, ln2_g, ln2_b, ln3_g, ln3_b)):
                sp.dma_start(prow[n * LNV:n * LNV + 2 * L, :], v.rearrange("l (k p) -> (l k) p", p=128)) \
                    .then_inc(params_in, 16)
            for n, v in enumerate((g_state, beta_state)):
                sp.dma_start(prow[n * LNV + 2 * L:n * LNV + 2 * L + 2, :], v.rearrange("(k p) -> k p", p=128)) \
                    .then_inc(params_in, 16)
            sp.dma_start(prow[FF_V:FF_V + L * 8, :], b_ff1.rearrange("l (f p) -> (l f) p", p=128)) \
                .then_inc(params_in, 16)
            for n, v in enumerate((g_input, beta_input, b_proj, b_u, b_r, b_n)):
                sp.dma_start(prow[L1_V + 2 * n:L1_V + 2 * n + 2, :], v.rearrange("(k p) -> k p", p=128)) \
                    .then_inc(params_in, 16)
            for ph, b in enumerate((b_sa_o, b_ca_o, b_ff2)):
                sp.dma_start(OB[:, ph:(L - 1) * PHASES + ph + 1:PHASES, :], b.partition_broadcast(T)) \
                    .then_inc(params_in, 16)

            def load_ctx(pair, b):
                sp.dma_start(CT[:, b, :, :].rearrange("p a s -> p (a s)").bitcast(f32),
                             ctxT[ds(2 * pair + b, 1), :, :].rearrange("o p n -> p (o n)")).then_inc(ctx_in[b], 16)

            with sp.Fori(0, L) as lay:
                for n in range(PER_LAYER):
                    load_block(n, BLK, lambda h: LAYER_BLOCKS[n][1](lay, h), split_until(n - SLOTS, lay))
                with sp.Fori(0, PAIRS) as pair:
                    it = lay * PAIRS + pair
                    for b in range(4):
                        sp.wait_ge(ctx_stored[b], PRIME + 16 * ROUNDS)
                    for b in range(2):
                        sp.wait_ge(ca["k_ready"][b], PRIME + (it + 1) * HP)
                        load_ctx((pair + 1) % PAIRS, b)
            sp.wait_ge(ca["ot_ready"], L * PAIRS * 4)
            sp.dma_start(BP, b_proj.partition_broadcast(KC)).then_inc(l1["vectors_in"], 16)
            sp.dma_start(GO[:, 0, :], g_out.partition_broadcast(T)).then_inc(l1["vectors_in"], 16)
            sp.dma_start(GO[:, 1, :], beta_out.partition_broadcast(T)).then_inc(l1["vectors_in"], 16)
            for m, (blk, cn, src) in enumerate(L1_BLOCKS):
                load_block(m, cn, src, split_until(m - SLOTS, L))
            with sp.Fori(0, PAIRS) as pair:
                for b in range(2):
                    sp.wait_ge(l1["tok_ready"], pair * 8 + 6 + 2 * b)
                    load_ctx((pair + 1) % PAIRS, b)
                for b in range(2):
                    sp.wait_ge(l1["y_done"], pair * 2 + b + 1)
                    sp.dma_start(out[ds(2 * pair + b, 1), :, :].rearrange("o t d -> t (o d)"), y[:, b, :]) \
                        .then_inc(l1["y_stored"], 16)
            sp.wait_ge(l1["y_stored"], PRIME + 16 * B)
            for b in range(2):
                sp.wait_ge(ctx_in[b], PRIME + 16 * (L + 1) * PAIRS)

        @block.gpsimd
        def _(pool):
            nc.gpsimd.memset(prow[:, :], 0.0).then_inc(consts_set, 1)
            nc.gpsimd.memset(mhalf[:, :], -0.5).then_inc(consts_set, 1)
            nc.gpsimd.memset(ident[:, :], 0.0).then_inc(consts_set, 1)
            pool.wait_ge(consts_set, 3)
            nc.gpsimd.affine_select(out=ident[:, :], in_=ident[:, :], compare_op=ALU.not_equal, fill=1.0,
                                    base=0, pattern=[[-1, 128]], channel_multiplier=1).then_inc(consts_set, 1)
            for c in ctx_slots:
                nc.gpsimd.memset(c[:, :, S:SP].bitcast(f32), 0.0).then_inc(consts_set, 1)
            nc.gpsimd.memset(zeros[:, :], 0.0).then_inc(consts_set, 1)
            nc.gpsimd.memset(qzh[:, :, :, :].bitcast(f32), 0.0).then_inc(consts_set, 1)
            nc.gpsimd.memset(qzl[:, :, :, :].bitcast(f32), 0.0).then_inc(consts_set, 1)
            nc.gpsimd.memset(kz[:, :, :, :], 0.0).then_inc(consts_set, 1)
            pool.wait_ge(consts_set, 12)

            def split_block(n, blk, cols_n, loaded, high, before):
                pool.wait_ge(stage_in[n % SLOTS], loaded)
                pool.wait_ge(w_split[(n - 1) % SLOTS], before)
                half = min(cols_n, BLK // 2)
                for c in range(0, cols_n, half):
                    nc.gpsimd.tensor_tensor(WH[:, wcol(blk, c, half)], stage[:, n % SLOTS, c:c + half],
                                            zeros[:, 0:half], ALU.add).then_inc(w_high, 1)
                pool.wait_ge(w_high, high)
                nc.gpsimd.tensor_tensor(WL[:, wcol(blk, 0, cols_n)], stage[:, n % SLOTS, 0:cols_n],
                                        WH[:, wcol(blk, 0, cols_n)].bitcast(f32), ALU.subtract) \
                    .then_inc(w_split[n % SLOTS], 1)

            def layer_blocks(blocks, lay, powers):
                pool.wait_ge(ln_rstd, powers)
                for n in blocks:
                    for s, v in last_use(n, lay):
                        pool.wait_ge(s, PRIME + v)
                    split_block(n, LAYER_BLOCKS[n][0], BLK, loads(n, lay), highs(n, lay),
                                split_until(n - 1, lay))

            def power(event, src, dst, ready, done, per=1):
                pool.wait_ge(ready, event)
                nc.gpsimd.tensor_tensor(dst, src, mhalf[0:T, 0:2], ALU.pow).then_inc(done, 1)

            power(1, vare[:, :], rstd[:, :], ln_var, ln_rstd)
            with pool.Fori(0, L) as lay:
                layer_blocks((0, 1), lay, lay * (PHASES * PAIRS) + 1)
                for n in LOW_BY_POOL:
                    c = wcol(LAYER_BLOCKS[n][0], 0, BLK)
                    pool.wait_ge(w_high, highs(n, lay))
                    nc.gpsimd.tensor_tensor(WL[:, c], stage[:, n % SLOTS, :], WH[:, c].bitcast(f32), ALU.subtract) \
                        .then_inc(w_split[n % SLOTS], 1)
                layer_blocks((6, 7), lay, lay * (PHASES * PAIRS) + 1)
                with pool.Fori(0, PAIRS) as pair:
                    pool.wait_ge(w_split[7 % SLOTS], split_until(7, lay))
                    pool.wait_ge(ln_rstd, lay * (PHASES * PAIRS) + pair + 1)
                    power(lay * (PHASES * PAIRS) + pair + 2, vare[:, :], rstd[:, :], ln_var, ln_rstd)
                layer_blocks(range(8, 14), lay, lay * (PHASES * PAIRS) + PAIRS + 1)
                with pool.Fori(0, PAIRS) as pair:
                    pool.wait_ge(w_split[13 % SLOTS], split_until(13, lay))
                    it = lay * PAIRS + pair
                    pool.wait_ge(ca["qz_done"], PRIME + it * (8 * HP))
                    pool.wait_ge(ln_rstd, lay * (PHASES * PAIRS) + PAIRS + pair + 1)
                    power(lay * (PHASES * PAIRS) + PAIRS + pair + 2, vare[:, :], rstd[:, :], ln_var, ln_rstd)
                    pool.wait_ge(ln_rstd, lay * (PHASES * PAIRS) + PAIRS + pair + 2)
                    for hp in range(2 * HP):
                        b, h2 = hp // HP, hp % HP
                        if hp == 0:
                            for i in range(2):
                                pool.wait_ge(ca["pj_done"][i], PRIME + it * (CA_J // 2) + 2)
                        if hp >= 2:
                            pool.wait_ge(ca["s_ready"], it * (2 * H) + 2 * hp - 2)
                        pool.wait_ge(ca["qz_done"], PRIME + it * (8 * HP) + 4 * hp)
                        for a in range(2):
                            src = qT[64 * a:64 * a + 64, h2, b * T:(b + 1) * T]
                            nc.gpsimd.tensor_tensor(qzh[64 * a:64 * a + 64, hp % 2, a, :], src,
                                                    zeros[64 * a:64 * a + 64, 0:T], ALU.add).then_inc(ca["qz_done"], 1)
                        pool.wait_ge(ca["qz_done"], PRIME + it * (8 * HP) + 4 * hp + 2)
                        for a in range(2):
                            src = qT[64 * a:64 * a + 64, h2, b * T:(b + 1) * T]
                            nc.gpsimd.tensor_tensor(qzl[64 * a:64 * a + 64, hp % 2, a, :], src,
                                                    qzh[64 * a:64 * a + 64, hp % 2, a, :].bitcast(f32),
                                                    ALU.subtract).then_inc(ca["qz_done"], 1)
                pool.wait_ge(ca["qz_done"], PRIME + (lay + 1) * (PAIRS * 8 * HP))
                layer_blocks((16, 17), lay, lay * (PHASES * PAIRS) + 2 * PAIRS + 1)
                with pool.Fori(0, PAIRS) as pair:
                    pool.wait_ge(ca["qz_done"], PRIME + (lay + 1) * (PAIRS * 8 * HP))
                    pool.wait_ge(ln_rstd, lay * (PHASES * PAIRS) + 2 * PAIRS + pair + 1)
                    power(lay * (PHASES * PAIRS) + 2 * PAIRS + pair + 2, vare[:, :], rstd[:, :], ln_var, ln_rstd)
            high = L * PER_LAYER * 2
            for m, (blk, cn, src) in enumerate(L1_BLOCKS):
                if m == 0:
                    pool.wait_ge(ln_rstd, L * (PHASES * PAIRS) + 1)
                    pool.wait_ge(ca["y_ready"], PRIME + L * PAIRS * 2)
                if m == 1:
                    pool.wait_ge(ff["f_ready"], PRIME + L * PAIRS * 4)
                high += max(1, cn // (BLK // 2))
                split_block(m, blk, cn, loads(m, L), high, split_until(m - 1, L))
            with pool.Fori(0, PAIRS) as pair:
                pool.wait_ge(w_split[4 % SLOTS], split_until(4, L))
                pool.wait_ge(ln_rstd, L * (PHASES * PAIRS) + pair + 1)
                power(L * (PHASES * PAIRS) + pair + 2, vare[:, :], rstd[:, :], ln_var, ln_rstd)
                pool.wait_ge(ln_rstd, L * (PHASES * PAIRS) + pair + 2)
                power(pair * 2 + 1, vare[:, :], rstd[:, :], l1["var"], l1["rstd"])
                pool.wait_ge(l1["rstd"], pair * 2 + 1)
                power(pair * 2 + 2, vare[:, :], rstd[:, :], l1["var"], l1["rstd"])

        @block.tensor
        def _(pe):
            def three(o, sh, sl, mh, ml, start, stop):
                nc.tensor.matmul(o, sh, mh, start=start, stop=False)
                nc.tensor.matmul(o, sh, ml, start=False, stop=False)
                return nc.tensor.matmul(o, sl, mh, start=False, stop=stop)

            def turn(o, src, n):
                return nc.tensor.transpose(o, src, ident[0:n, 0:n])

            def ln_turn(banks, event, pj=None, j=0):
                for b in range(2):
                    if pj:
                        pj(j + b)
                    pe.wait_ge(ln_xn, event * 2 + b + 1)
                    turn(banks[b][:, 0:T], xn[:, b, 0:128], T)
                    turn(banks[b][:, T:T2], xn[:, b, 128:256], T).then_inc(ln_turned, 1)

            def wait_block(n, lay):
                pe.wait_ge(w_split[n % SLOTS], split_until(n, lay))

            pe.wait_ge(consts_set, 4)
            pe.wait_ge(params_in, 16 * PARAM_DMAS)
            turn(OA[0][:, 0:128], prow[:, :], 128).then_inc(params_turned, 1)
            ln_turn(PJ, 0)
            with pe.Fori(0, ROUNDS) as i:
                for u in range(4):
                    pe.wait_ge(ctx_raw_in[u], 16 * (i + 1))
                    pe.wait_ge(ctx_split[u], PRIME + i)
                    pe.wait_ge(first_affine, 2)
                    for t in range(KT):
                        turn(ctx_banks[u][0][:, t * KC:(t + 1) * KC], craw[u][:, t, 0:128], KC)
                    for t in range(KT):
                        last = turn(ctx_banks[u][1][0:CL, t * KC:(t + 1) * KC], craw[u][:, t, 128:C], KC)
                    last.then_inc(ctx_turned, 1)
            for u in range(4):
                pe.wait_ge(ctx_split[u], PRIME + ROUNDS)
            pe.wait_ge(consts_set, 12)

            with pe.Fori(0, L) as lay:
                git0 = lay * (PHASES * PAIRS)
                with pe.Fori(0, PAIRS) as pair:
                    wait_block(2, lay)
                    wait_block(3, lay)
                    wait_block(4, lay)
                    for i in range(2):
                        pe.wait_ge(ff["pj_done"][i], PRIME + lay * (PAIRS * FF_J // 2))
                        pe.wait_ge(ff["y_done"][i], PRIME + lay * PAIRS)
                        pe.wait_ge(ca["exp_done"], PRIME + lay * (PAIRS * 2 * H))
                        pe.wait_ge(ca["pt_done"][i], PRIME + lay * (PAIRS * H))
                        pe.wait_ge(ca["o_done"][i], PRIME + lay * (PAIRS * 2))
                    it = lay * PAIRS + pair
                    pb = it * (SA_J // 2)

                    def pj(j):
                        pe.wait_ge(sa["pj_done"][j % 2], PRIME + pb + j // 2)
                        return PJ[j % 2]

                    def pj_out(j):
                        pe.wait_ge(sa["pj_done"][j % 2], PRIME + pb + j // 2 + 1)

                    pe.wait_ge(ln_low, git0 + pair + 1)
                    for hp in range(HP):
                        o = pj(hp)
                        for a in range(2):
                            for k in range(2):
                                w = wcol(2 * a + k, hp * 128, 128)
                                last = three(o[:, a * T2:(a + 1) * T2], WH[:, w], WL[:, w], hTh[:, k, :], hTl[:, k, :],
                                             k == 0, k == 1)
                        last.then_inc(sa["qk_ready"], 1)

                    def scores(s):
                        b = s // 4
                        for c in range(2):
                            hp = 2 * (s % 4) + c
                            last = nc.tensor.matmul(SC[s % 2][0:T, c * T2:(c + 1) * T2], qT[:, hp, b * T:(b + 1) * T],
                                                    kz[:, hp, :, b * T:(b + 1) * T], start=True, stop=True)
                        last.then_inc(sa["s_ready"], 1)

                    pe.wait_ge(sa["exp_done"], PRIME + it * 8)
                    for b in range(2):
                        pe.wait_ge(sa["y_done"][b], PRIME + it)
                    scores(0)
                    scores(1)
                    wait_block(5, lay)
                    for b in range(2):
                        for n in range(2):
                            o = pj(8 + 2 * b + n)
                            for k in range(2):
                                w = wcol(4 + k, n * 512, 512)
                                tt = slice(b * T, (b + 1) * T)
                                last = three(o[0:T, :], hTh[:, k, tt], hTl[:, k, tt], WH[:, w], WL[:, w], k == 0, k == 1)
                            last.then_inc(sa["v_ready"], 1)

                    def turn_out(i, j):
                        o = pj(j)
                        pe.wait_ge(sa["o_done"][i % 2], PRIME + it * 2 + i // 2 + 1)
                        for c in range(4):
                            last = turn(o[:, c * T:(c + 1) * T], O[0:T, i % 2, c * 128:(c + 1) * 128], T)
                        last.then_inc(sa["ot_ready"], 1)

                    def project(b, cs):
                        for c in cs:
                            w = wcol(6, c * D, D)
                            last = three(SC[b][0:T, 0:D], OTh[:, 8 * b + c, :], OTl[:, 8 * b + c, :], WH[:, w], WL[:, w],
                                         c == 0, c == HP - 1)
                        return last

                    for s in range(2, 11):
                        g = s - 2
                        if 0 <= g < 8:
                            pe.wait_ge(sa["exp_done"], PRIME + it * 8 + g + 1)
                            pe.wait_ge(sa["pt_done"][g % 2], PRIME + it * 4 + g // 2)
                            for c in range(4):
                                last = turn(TR[g % 2][0:T, c * T:(c + 1) * T], P[:, g % 2, c * T:(c + 1) * T], T)
                            last.then_inc(sa["t_ready"], 1)
                        if s < 8:
                            scores(s)
                        if s == 2:
                            ln_turn(PJ, git0 + pair + 1, pj, 12)
                        g = s - 3
                        if 0 <= g < 8:
                            i = g // 2
                            pe.wait_ge(sa["pt_done"][g % 2], PRIME + it * 4 + g // 2 + 1)
                            if g % 2 == 0:
                                pe.wait_ge(sa["o_done"][i % 2], PRIME + it * 2 + i // 2)
                            if g % 4 == 0:
                                pj_out(8 + 2 * (g // 4))
                                pj_out(9 + 2 * (g // 4))
                            for c in range(4):
                                h = 4 * (g % 4) + c
                                oc = (4 * (g % 2) + c) * DH
                                last = nc.tensor.matmul(OA[i % 2][0:T, oc:oc + DH], PT[0:T, g % 2, c * T:(c + 1) * T],
                                                        V[0:T, g // 4, h * DH:(h + 1) * DH], start=True, stop=True)
                            if g % 2 == 1:
                                last.then_inc(sa["o_ready"], 1)
                        if s == 5:
                            turn_out(0, 14)
                        if s == 7:
                            turn_out(1, 15)
                        if s == 9:
                            turn_out(2, 16)
                    wait_block(7, lay)
                    pj_out(14)
                    pj_out(15)
                    project(0, range(0, 4))
                    turn_out(3, 17)
                    project(0, range(4, HP)).then_inc(sa["y_ready"], 1)
                    pj_out(16)
                    project(1, range(0, 4))
                    pj_out(17)
                    project(1, range(4, HP)).then_inc(sa["y_ready"], 1)

                with pe.Fori(0, PAIRS) as pair:
                    for i in range(2):
                        pe.wait_ge(sa["pj_done"][i], PRIME + (lay + 1) * (PAIRS * SA_J // 2))
                        pe.wait_ge(sa["pt_done"][i], PRIME + (lay + 1) * (PAIRS * 4))
                        pe.wait_ge(sa["y_done"][i], PRIME + (lay + 1) * PAIRS)
                        pe.wait_ge(sa["o_done"][i], PRIME + (lay + 1) * (PAIRS * 2))
                        wait_block(8 + i, lay)
                    pe.wait_ge(sa["exp_done"], PRIME + (lay + 1) * (PAIRS * 8))
                    it = lay * PAIRS + pair
                    pb = it * (CA_J // 2)

                    def pj(j):
                        pe.wait_ge(ca["pj_done"][j % 2], PRIME + pb + j // 2)
                        return PJ[j % 2]

                    def pj_out(j):
                        pe.wait_ge(ca["pj_done"][j % 2], PRIME + pb + j // 2 + 1)

                    pe.wait_ge(ln_low, git0 + PAIRS + pair + 1)
                    for q in range(4):
                        o = pj(q)
                        for a in range(2):
                            for k in range(2):
                                w = wcol(k, (2 * q + a) * 128, 128)
                                last = three(o[:, a * T2:(a + 1) * T2], WH[:, w], WL[:, w], hTh[:, k, :], hTl[:, k, :],
                                             k == 0, k == 1)
                        last.then_inc(ca["q_ready"], 1)

                    def values(b, n):
                        t, c = n // 2, n % 2
                        tt = slice(t * KC, (t + 1) * KC)
                        o = pj(CA_JOBS[("v", b, n)])
                        w, wl = wcol(3, c * 512, 512), wcol(5, c * 512, 512)
                        three(o[0:KC, :], CT[:, b, 0, tt], CT[:, b, 1, tt], WH[:, w], WL[:, w], True, False)
                        nc.tensor.matmul(o[0:KC, :], CT[:, b, 2, tt], WH[:, wl], start=False, stop=False)
                        nc.tensor.matmul(o[0:KC, :], CT[:, b, 2, tt], WL[:, wl], start=False, stop=True) \
                            .then_inc(ca["v_ready"], 1)

                    def keys(hp):
                        b, h2 = hp // HP, hp % HP
                        o = pj(CA_JOBS[("k", hp)])
                        w, wl = wcol(2, h2 * 128, 128), wcol(4, h2 * 128, 128)
                        three(o[:, 0:SP], WH[:, w], WL[:, w], CT[:, b, 0, :], CT[:, b, 1, :], True, False)
                        nc.tensor.matmul(o[:, 0:SP], WH[:, wl], CT[:, b, 2, :], start=False, stop=False)
                        nc.tensor.matmul(o[:, 0:SP], WL[:, wl], CT[:, b, 2, :], start=False, stop=True) \
                            .then_inc(ca["k_ready"][b], 1)

                    def turn_out(i):
                        o = pj(CA_JOBS[("ot", i)])
                        pe.wait_ge(ca["o_done"][i % 2], PRIME + it * 2 + i // 2 + 1)
                        for c in range(4):
                            last = turn(o[:, c * T:(c + 1) * T], O[0:T, i % 2, c * 128:(c + 1) * 128], T)
                        last.then_inc(ca["ot_ready"], 1)

                    def project(b, cs):
                        if cs[0] == 0:
                            pj_out(CA_JOBS[("ot", 2 * b)])
                        if cs[0] == 0 and b == 0:
                            pj_out(CA_JOBS[("ot", 1)])
                        if b == 1 and cs[0] == 4:
                            pj_out(CA_JOBS[("ot", 3)])
                        for c in cs:
                            w = wcol(6, c * D, D)
                            last = three(SC[b][0:T, 0:D], OTh[:, 8 * b + c, :], OTl[:, 8 * b + c, :], WH[:, w], WL[:, w],
                                         c == 0, c == HP - 1)
                        if cs[-1] == HP - 1:
                            last.then_inc(ca["y_ready"], 1)

                    def scores(h):
                        hp, a = h // 2, h % 2
                        if h < 2:
                            pe.wait_ge(ca["exp_done"], PRIME + it * (2 * H))
                            pe.wait_ge(ca["y_done"][h], PRIME + it)
                        if a == 0:
                            pe.wait_ge(ca["qz_done"], PRIME + it * (8 * HP) + 4 * hp + 4)
                            pj_out(CA_JOBS[("k", hp)])
                        three(SC[h % 2][0:T, 0:SP], qzh[:, hp % 2, a, :], qzl[:, hp % 2, a, :], Kh[:, hp % 2, :],
                              Kl[:, hp % 2, :], True, True).then_inc(ca["s_ready"], 1)

                    def turn_probs(h):
                        pe.wait_ge(ca["exp_done"], PRIME + it * (2 * H) + h + 1)
                        pe.wait_ge(ca["pt_done"][h % 2], PRIME + it * H + h // 2)
                        for t in range(KT):
                            last = turn(TR[h % 2][0:KC, t * T:(t + 1) * T], P[:, h % 2, t * KC:(t + 1) * KC], T)
                        last.then_inc(ca["t_ready"], 1)

                    def attend(h):
                        i, b = h // 8, h // H
                        pe.wait_ge(ca["pt_done"][h % 2], PRIME + it * H + h // 2 + 1)
                        if h % 8 == 0:
                            pe.wait_ge(ca["o_done"][i % 2], PRIME + it * 2 + i // 2)
                        if h % H == 0:
                            pj_out(CA_JOBS[("v", b, 4)])
                            pj_out(CA_JOBS[("v", b, 5)])
                        oc = (h % 8) * DH
                        for t in range(KT):
                            vc = t * INNER + (h % H) * DH
                            last = nc.tensor.matmul(OA[i % 2][0:T, oc:oc + DH], PT[0:KC, h % 2, t * T:(t + 1) * T],
                                                    V[0:KC, b, vc:vc + DH], start=t == 0, stop=t == KT - 1)
                        if h % 8 == 7:
                            last.then_inc(ca["o_ready"], 1)

                    for job in CA_ORDER:
                        if job[0] == "v":
                            if job[2] == 0:
                                pe.wait_ge(ctx_in[job[1]], PRIME + 16 * it)
                                wait_block(13, lay)
                            values(job[1], job[2])
                        elif job[0] == "k":
                            if job[1] == 0:
                                pe.wait_ge(ctx_in[0], PRIME + 16 * it)
                                wait_block(11, lay)
                            keys(job[1])
                        elif job[0] == "ln":
                            ln_turn([PJ[CA_JOBS[job] % 2], PJ[(CA_JOBS[job] + 1) % 2]], git0 + PAIRS + pair + 1,
                                    pj, CA_JOBS[job])
                        elif job[0] == "ot":
                            turn_out(job[1])
                        elif job[0] == "y":
                            if job[1:] == (0, (0, 1)):
                                wait_block(15, lay)
                            project(job[1], job[2])
                        elif job[0] == "s":
                            scores(job[1])
                        elif job[0] == "t":
                            turn_probs(job[1])
                        elif job[0] == "pv":
                            attend(job[1])

                with pe.Fori(0, PAIRS) as pair:
                    for i in range(2):
                        pe.wait_ge(ca["pj_done"][i], PRIME + (lay + 1) * (PAIRS * CA_J // 2))
                        pe.wait_ge(ca["y_done"][i], PRIME + (lay + 1) * PAIRS)
                        wait_block(16 + i, lay)
                    it = lay * PAIRS + pair
                    pb = it * (FF_J // 2)

                    def pj(j):
                        pe.wait_ge(ff["pj_done"][j % 2], PRIME + pb + j // 2)
                        return PJ[j % 2]

                    pe.wait_ge(ln_low, git0 + 2 * PAIRS + pair + 1)
                    for q in range(4):
                        o = pj(q)
                        for a in range(2):
                            for k in range(2):
                                w = wcol(k, (2 * q + a) * 128, 128)
                                last = three(o[:, a * T2:(a + 1) * T2], WH[:, w], WL[:, w], hTh[:, k, :], hTl[:, k, :],
                                             k == 0, k == 1)
                        last.then_inc(ff["f_ready"], 1)
                    ln_turn([SC[0], SC[1]], git0 + 2 * PAIRS + pair + 1)
                    for i in range(2):
                        wait_block(18 + i, lay)
                        pe.wait_ge(ff["y_done"][i], PRIME + it)
                    for f0, f1 in ((0, 6), (6, 8)):
                        for b in range(2):
                            for f in range(f0, f1):
                                if b == 0 and f % 2 == 0:
                                    pe.wait_ge(ff["g_split"], it * 4 + f // 2 + 1)
                                w = wcol(3 + 2 * (f // 4), (f % 4) * D, D)
                                tt = slice(b * T, (b + 1) * T)
                                last = three(OA[b][0:T, 0:D], Gh[:, f, tt], Gl[:, f, tt], WH[:, w], WL[:, w],
                                             f == 0, f == 7)
                            if f1 == 8:
                                last.then_inc(ff["y_ready"], 1)

            for i in range(2):
                pe.wait_ge(ff["pj_done"][i], PRIME + L * (PAIRS * FF_J // 2))
                pe.wait_ge(ff["y_done"][i], PRIME + L * PAIRS)
                wait_block(i, L)
            with pe.Fori(0, PAIRS) as pair:
                pb = pair * (L1_J // 2)

                def pj(j):
                    pe.wait_ge(l1["pj_done"][j % 2], PRIME + pb + j // 2)
                    return PJ[j % 2]

                def pj_out(j):
                    pe.wait_ge(l1["pj_done"][j % 2], PRIME + pb + j // 2 + 1)

                pe.wait_ge(l1["xs_done"], pair + 1)
                o = pj(0)
                for b in range(2):
                    for k in range(2):
                        last = turn(o[:, k * T2 + b * T:k * T2 + (b + 1) * T], xs[:, b, k * 128:(k + 1) * 128], T)
                last.then_inc(l1["x_ready"], 1)
                for b in range(2):
                    pe.wait_ge(ctx_in[b], PRIME + 16 * (pair + L * PAIRS))
                    for m in range(2):
                        o = pj(1 + 2 * b + m)
                        w, wl = wcol(7, m * 128, 128), wcol(0, m * 128, 128)
                        three(o[:, 0:SP], WH[:, w], WL[:, w], CT[:, b, 0, :], CT[:, b, 1, :], True, False)
                        nc.tensor.matmul(o[:, 0:SP], WH[:, wl], CT[:, b, 2, :], start=False, stop=False)
                        nc.tensor.matmul(o[:, 0:SP], WL[:, wl], CT[:, b, 2, :], start=False, stop=True) \
                            .then_inc(l1["tok_ready"], 1)
                pe.wait_ge(ln_low, L * (PHASES * PAIRS) + pair + 1)

                def tokens(b):
                    for n, ts in enumerate(((0, 1), (2,))):
                        o = pj(5 + 2 * b + n)
                        for c, t in enumerate(ts):
                            tt = slice(t * KC, (t + 1) * KC)
                            oc = o[0:KC, c * D:(c + 1) * D]
                            w, wl = wcol(7, 0, D), wcol(0, 0, D)
                            three(oc, CT[:, b, 0, tt], CT[:, b, 1, tt], WH[:, w], WL[:, w], True, False)
                            nc.tensor.matmul(oc, CT[:, b, 2, tt], WH[:, wl], start=False, stop=False)
                            last = nc.tensor.matmul(oc, CT[:, b, 2, tt], WL[:, wl], start=False, stop=True)
                        last.then_inc(l1["tok_ready"], 1)

                tokens(0)
                for b in range(2):
                    for k in range(2):
                        last = nc.tensor.matmul(SC[b][0:T, 0:SP], xT[:, k, b * T:(b + 1) * T], tokT[:, b, k, :],
                                                start=k == 0, stop=k == 1)
                    last.then_inc(l1["s_ready"], 1)
                tokens(1)
                for b in range(2):
                    pe.wait_ge(l1["exp_done"], pair * 2 + b + 1)
                    pe.wait_ge(l1["pt_done"][b], PRIME + pair)
                    for t in range(KT):
                        last = turn(TR[b][0:KC, t * T:(t + 1) * T], P[:, b, t * KC:(t + 1) * KC], T)
                    last.then_inc(l1["t_ready"], 1)

                pj_out(7)
                pj_out(8)
                wait_block(2, L)
                for b in range(2):
                    pe.wait_ge(l1["pt_done"][b], PRIME + pair + 1)
                    pe.wait_ge(l1["out_read"][b], PRIME + pair)
                    for t in range(KT):
                        last = nc.tensor.matmul(OA[b][0:T, 0:D], PT[0:KC, b, t * T:(t + 1) * T], tok[b][:, t, :],
                                                start=t == 0, stop=t == KT - 1)
                    last.then_inc(l1["o_ready"], 1)
                    if b == 0:
                        o_r = pj(9)
                o_u = pj(10)

                def gate_half(o, blk, m, h, l, rows):
                    for k in range(2):
                        w = wcol(blk, (rows + k) * D + m * 128, 128)
                        last = three(o[:, m * T2:(m + 1) * T2], WH[:, w], WL[:, w], h[:, k, :], l[:, k, :],
                                     rows == 0 and k == 0, rows == 2 and k == 1)
                    return last

                r_banks, u_banks = (o_r, SC[0]), (o_u, SC[1])
                for m in range(2):
                    gate_half(r_banks[m], 4, m, hTh, hTl, 0)
                wait_block(3, L)
                for m in range(2):
                    gate_half(u_banks[m], 2, m, hTh, hTl, 0)
                for b in range(2):
                    pe.wait_ge(l1["norm"], pair * 2 + b + 1)
                    for k in range(2):
                        last = turn(TR[b][:, k * T:(k + 1) * T], routed[:, b, k * 128:(k + 1) * 128], T)
                    last.then_inc(l1["in_ready"], 1)
                pe.wait_ge(l1["in_low"], pair + 1)

                for banks, blk in ((r_banks, 4), (u_banks, 2)):
                    for m in range(2):
                        last = gate_half(banks[m], blk, m, inTh, inTl, 2)
                    last.then_inc(l1["g_ready"], 1)
                ln_turn([TR[b][:, T2:2 * T2] for b in range(2)], L * (PHASES * PAIRS) + pair + 1)
                o = pj(11)
                wait_block(4, L)
                pe.wait_ge(l1["rp_split"], pair + 1)
                for m in range(2):
                    gate_half(o, 6, m, rph, rpl, 0)
                    last = gate_half(o, 6, m, inTh, inTl, 2)
                last.then_inc(l1["g_ready"], 1)
                pe.wait_ge(l1["ns_done"], pair + 1)
                for b in range(2):
                    for k in range(2):
                        last = turn(OA[b][0:T, k * 128:(k + 1) * 128], nsT[:, k, b * T:(b + 1) * T], 128)
                    last.then_inc(l1["out_ready"], 1)

        @block.scalar
        def _(act):
            def copy(o, i):
                return nc.scalar.activation(o, i, ACT.Copy)

            def affine_done(pj_done, base, j):
                for n in (j, j + 1):
                    act.wait_ge(pj_done[n % 2], PRIME + base + n // 2 + 1)

            def batch(i, u):
                return i * (-4) + (B - 4 + u)

            def load_raw(i, u):
                act.dma_start(craw[u], ctx_768[ds(batch(i, u), 1), :, :].rearrange("o (t p) c -> p (o t) c", p=KC)) \
                    .then_inc(ctx_raw_in[u], 16)

            def ctx_round(i, more):
                for u in range(4):
                    act.wait_ge(ctx_turned, 4 * i + u + 1)
                    act.wait_ge(ctx_stored[u], PRIME + 16 * i)
                    copy(ctx_slots[u][:, 0, 0:S], ctx_banks[u][0][:, 0:S])
                    copy(ctx_slots[u][0:CL, 2, 0:S], ctx_banks[u][1][0:CL, 0:S]).then_inc(ctx_high, 1)
                    if more:
                        load_raw(i + 1, u)
                for u in range(4):
                    act.wait_ge(ctx_split[u], PRIME + i + 1)
                    act.dma_start(ctxT[ds(batch(i, u), 1), :, :].rearrange("o p n -> p (o n)"),
                                  ctx_slots[u].rearrange("p a s -> p (a s)").bitcast(f32)).then_inc(ctx_stored[u], 16)

            for u in range(4):
                load_raw(0, u)
            act.wait_ge(first_affine, 2)
            copy(hTh[:, :, :], hTf[:, :, :]).then_inc(ln_high, 1)
            act.wait_ge(consts_set, 8)
            with act.Fori(0, ROUNDS - 1) as i:
                ctx_round(i, True)
            ctx_round(ROUNDS - 1, False)

            def split_high(blocks, lay):
                for n in blocks:
                    for s, v in last_use(n, lay):
                        act.wait_ge(s, PRIME + v)
                    act.wait_ge(stage_in[n % SLOTS], loads(n, lay))
                    act.wait_ge(w_high, highs(n - 1, lay))
                    copy(WH[:, wcol(LAYER_BLOCKS[n][0], 0, BLK)], stage[:, n % SLOTS, :]).then_inc(w_high, 2)

            with act.Fori(0, L) as lay:
                nc.scalar.activation(warm[:, :], mhalf[:, 0:1], ACT.Exp)
                split_high(SHARED["sa"], lay)
                with act.Fori(0, PAIRS) as pair:
                    it = lay * PAIRS + pair
                    pb = it * (SA_J // 2)
                    for hp in range(HP):
                        act.wait_ge(sa["qk_ready"], it * 8 + hp + 1)
                        o = PJ[hp % 2]
                        nc.scalar.activation(qT[:, hp, :], o[:, 0:T2], ACT.Copy, scale=-SCALE)
                        copy(kz[0:64, hp, 0, :], o[0:64, T2:2 * T2])
                        copy(kz[64:128, hp, 1, :], o[64:128, T2:2 * T2]).then_inc(sa["pj_done"][hp % 2], 1)

                    def out_high(i, j):
                        act.wait_ge(sa["ot_ready"], it * 4 + i + 1)
                        for u in (2, 3):
                            act.wait_ge(ctx_stored[u], PRIME + 16 * ROUNDS)
                        copy(OTh[:, 4 * i:4 * i + 4, :].rearrange("p c t -> p (c t)"), PJ[j % 2][:, 0:4 * T]) \
                            .then_inc(sa["ot_high"], 1)

                    for s in range(11):
                        if s < 8:
                            act.wait_ge(sa["nb_ready"], it * 8 + s + 1)
                            for c in range(4):
                                h = 4 * (s % 4) + c
                                last = nc.scalar.activation(P[:, s % 2, c * T:(c + 1) * T], SC[s % 2][0:T, c * T:(c + 1) * T],
                                                            ACT.Exp, bias=nb[:, s % 2, c:c + 1], scale=-1.0,
                                                            accum_out=rs[:, s // 4, h:h + 1])
                            last.then_inc(sa["exp_done"], 1)
                        if s == 3:
                            affine_done(sa["pj_done"], pb, 12)
                            copy(hTh[:, :, :], hTf[:, :, :]).then_inc(ln_high, 1)
                        if s == 5:
                            out_high(0, 14)
                        if s == 7:
                            out_high(1, 15)
                        if s == 9:
                            out_high(2, 16)
                        if s == 10:
                            out_high(3, 17)

                split_high(SHARED["ca"], lay)
                with act.Fori(0, PAIRS) as pair:
                    it = lay * PAIRS + pair
                    for q in range(4):
                        act.wait_ge(ca["q_ready"], PRIME + it * 4 + q + 1)
                        nc.scalar.activation(qT[:, 2 * q:2 * q + 2, :].rearrange("p a t -> p (a t)"),
                                             PJ[q % 2][:, 0:2 * T2], ACT.Copy, scale=-SCALE) \
                            .then_inc(ca["pj_done"][q % 2], 1)
                    for job in CA_ORDER:
                        if job[0] == "k":
                            hp = job[1]
                            b = hp // HP
                            act.wait_ge(ca["k_ready"][b], PRIME + it * HP + hp % HP + 1)
                            copy(Kh[:, hp % 2, :], PJ[CA_JOBS[job] % 2][:, 0:SP]).then_inc(ca["k_high"], 1)
                        elif job[0] == "ln":
                            affine_done(ca["pj_done"], it * (CA_J // 2), CA_JOBS[job])
                            copy(hTh[:, :, :], hTf[:, :, :]).then_inc(ln_high, 1)
                        elif job[0] == "ot":
                            i = job[1]
                            act.wait_ge(ca["ot_ready"], it * 4 + i + 1)
                            copy(OTh[:, 4 * i:4 * i + 4, :].rearrange("p c t -> p (c t)"),
                                 PJ[CA_JOBS[job] % 2][:, 0:4 * T]).then_inc(ca["ot_high"], 1)
                        elif job[0] == "s":
                            h = job[1]
                            act.wait_ge(ca["nb_ready"], it * (2 * H) + h + 1)
                            nc.scalar.activation(P[:, h % 2, 0:S], SC[h % 2][0:T, 0:S], ACT.Exp,
                                                 bias=nb[:, h % 2, 0:1], scale=-1.0,
                                                 accum_out=rs[:, h // H, h % H:h % H + 1]).then_inc(ca["exp_done"], 1)
                        elif job[0] == "t":
                            h = job[1]
                            act.wait_ge(ca["t_ready"], it * (2 * H) + h + 1)
                            copy(PT[0:KC, h % 2, 0:KT * T], TR[h % 2][0:KC, 0:KT * T]).then_inc(ca["pt_done"][h % 2], 1)

                nc.scalar.activation(warm[:, :], mhalf[:, 0:1], ACT.Gelu)
                split_high(SHARED["ff"], lay)
                with act.Fori(0, PAIRS) as pair:
                    it = lay * PAIRS + pair
                    for q in range(4):
                        act.wait_ge(ff["f_ready"], PRIME + it * 4 + q + 1)
                        for a in range(2):
                            f = 2 * q + a
                            last = nc.scalar.activation(Gf[:, f, :], PJ[q % 2][:, a * T2:(a + 1) * T2], ACT.Gelu,
                                                        bias=pcol[:, ds(FF_V + lay * 8 + f, 1)])
                        last.then_inc(ff["pj_done"][q % 2], 1)
                    act.wait_ge(ff["ln_done"], 2 * (it + 1))
                    copy(hTh[:, :, :], hTf[:, :, :]).then_inc(ln_high, 1)

            nc.scalar.activation(warm[:, :], mhalf[:, 0:1], ACT.Exp)
            with act.Fori(0, PAIRS) as pair:
                pb = pair * (L1_J // 2)
                act.wait_ge(ff["dve_step"], L * PAIRS * FF_STEPS)
                copy(xs[:, :, :], X[:, ds(2 * pair, 2), :]).then_inc(l1["xs_done"], 1)
                act.wait_ge(l1["x_ready"], pair + 1)
                copy(xT[:, :, :].rearrange("p k t -> p (k t)"), PJ[0][:, 0:2 * T2]).then_inc(l1["pj_done"][0], 1)
                for j in range(1, 5):
                    b, m = (j - 1) // 2, (j - 1) % 2
                    act.wait_ge(l1["tok_ready"], pair * 8 + j)
                    nc.scalar.activation(tokT[:, b, m, :], PJ[j % 2][:, 0:SP], ACT.Identity, bias=cols[:, 4 + m:5 + m]) \
                        .then_inc(l1["pj_done"][j % 2], 1)
                for b in range(2):
                    act.wait_ge(l1["nb_ready"], pair * 2 + b + 1)
                    nc.scalar.activation(P[:, b, 0:S], SC[b][0:T, 0:S], ACT.Exp, bias=nb[:, b, 0:1], scale=SCALE_OUT,
                                         accum_out=rs[:, b, 0:1]).then_inc(l1["exp_done"], 1)
                for b in range(2):
                    act.wait_ge(l1["t_ready"], pair * 2 + b + 1)
                    copy(PT[0:KC, b, 0:KT * T], TR[b][0:KC, 0:KT * T]).then_inc(l1["pt_done"][b], 1)
                act.wait_ge(l1["in_done"], 2 * (pair + 1))
                copy(inTh, inT).then_inc(l1["in_high"], 1)
                for n, (dst, j, c0) in enumerate(((rT, 9, 2), (uT, 10, 0))):
                    act.wait_ge(l1["g_ready"], pair * 3 + n + 1)
                    for m, bank in enumerate((PJ[j % 2], SC[n])):
                        last = nc.scalar.activation(dst[:, m, :], bank[:, m * T2:(m + 1) * T2], ACT.Tanh,
                                                    bias=hcols[:, c0 + m:c0 + m + 1], scale=0.5)
                    last.then_inc(l1["pj_done"][j % 2], 1)
                act.wait_ge(l1["ln_done"], 2 * (pair + 1))
                copy(hTh[:, :, :], hTf[:, :, :]).then_inc(ln_high, 1)
                act.wait_ge(l1["g_ready"], pair * 3 + 3)
                for m in range(2):
                    last = nc.scalar.activation(cT[:, m, :], PJ[1][:, m * T2:(m + 1) * T2], ACT.Tanh,
                                                bias=cols[:, 10 + m:11 + m])
                last.then_inc(l1["pj_done"][1], 1)

        @block.vector
        def _(dve):
            def ln_stats(step, nxt):
                for b in range(2):
                    last = nc.vector.bn_stats(bst[:, b, :], X[:, ds(2 * nxt + b, 1), :].rearrange("p o d -> p (o d)"))
                step(last, before_aggr=True)
                for b in range(2):
                    last = nc.vector.bn_aggr(mv[:, b, :], bst[:, b, :])
                step(last)
                nc.vector.tensor_scalar(vare[:, :], mv[:, :, 1], EPS, None, ALU.add).then_inc(ln_var, 1)

            def ln_norm(nxt, var_value):
                dve.wait_ge(ln_rstd, var_value)
                for b in range(2):
                    nc.vector.tensor_scalar(xn[:, b, :], X[:, ds(2 * nxt + b, 1), :].rearrange("p o d -> p (o d)"),
                                            mv[:, b, 0:1], rstd[:, b:b + 1], ALU.subtract, ALU.mult).then_inc(ln_xn, 1)

            def ln_affine_to(gcol, banks, done, event):
                for b in range(2):
                    dve.wait_ge(ln_turned, event * 2 + b + 1)
                    for k in range(2):
                        ins = nc.vector.tensor_scalar(hTf[:, k, b * T:(b + 1) * T], banks[b][:, k * T:(k + 1) * T],
                                                      pcol[:, ds(gcol + k, 1)], pcol[:, ds(gcol + LNV + k, 1)],
                                                      ALU.mult, ALU.add)
                    ins.then_inc(done[b], 1)

            def split_low(blocks, lay):
                for n in blocks:
                    c = wcol(LAYER_BLOCKS[n][0], 0, BLK)
                    dve.wait_ge(w_high, highs(n, lay))
                    nc.vector.tensor_tensor(WL[:, c], stage[:, n % SLOTS, :], WH[:, c].bitcast(f32), ALU.subtract) \
                        .then_inc(w_split[n % SLOTS], 1)

            def ln_low_part(event):
                dve.wait_ge(ln_high, event + 1)
                nc.vector.tensor_tensor(hTl[:, :, :], hTf[:, :, :], hTh[:, :, :].bitcast(f32), ALU.subtract) \
                    .then_inc(ln_low, 1)

            def least(h, src, n):
                return nc.vector.tensor_reduce(nb[:, h % 2, 0:n], src, AX.X, ALU.min)

            def negmax(step, h, src, n, scale):
                step(nc.vector.reduce_max(mx[:, h % 2, 0:n], src, AX.X))
                return nc.vector.tensor_scalar(nb[:, h % 2, 0:n], mx[:, h % 2, 0:n], -scale, None, ALU.mult)

            def normalise(step, i, done):
                step(nc.vector.reciprocal(rinv[:, i % 2, :], rs[:, i // 2, 8 * (i % 2):8 * (i % 2) + 8]))
                nc.vector.tensor_tensor(O[0:T, i % 2, :].rearrange("p (h d) -> p h d", h=8),
                                        OA[i % 2][0:T, :].rearrange("p (h d) -> p h d", h=8),
                                        rinv[:, i % 2, :].unsqueeze(2).broadcast_to([T, 8, DH]),
                                        ALU.mult).then_inc(done, 1)

            def out_low(i, bk, pj_done):
                nc.vector.tensor_tensor(OTl[:, 4 * i:4 * i + 4, :].rearrange("p c t -> p (c t)"),
                                        PJ[bk][:, 0:4 * T],
                                        OTh[:, 4 * i:4 * i + 4, :].rearrange("p c t -> p (c t)").bitcast(f32),
                                        ALU.subtract).then_inc(pj_done[bk], 1)

            def residual(step, bt, y, slot, read, added):
                xb = X[:, ds(bt, 1), :].rearrange("p o d -> p (o d)")
                nc.vector.tensor_tensor(xb, y[0:T, 0:D], xb, ALU.add).then_inc(read, 1)
                dve.wait_ge(read, PRIME + added)
                step(nc.vector.tensor_tensor(xb, xb, OB[:, ds(slot, 1), :].rearrange("p o d -> p (o d)"), ALU.add))

            dve.wait_ge(consts_set, 4)
            dve.wait_ge(params_in, 16 * PARAM_DMAS)
            dve.wait_ge(params_turned, 1)
            nc.vector.tensor_copy(pcol[:, :], OA[0][:, 0:128]).then_inc(first_step, 1)
            dve.wait_ge(first_step, 1)
            nc.vector.tensor_scalar(hcols[:, :], cols[:, 6:10], 0.5, None, ALU.mult)
            step = Steps(dve, first_step, 1, 2)
            ln_stats(step, 0)
            step.close()
            ln_norm(0, 1)
            ln_affine_to(0, PJ, [first_affine, first_affine], 0)
            ln_low_part(0)
            with dve.Fori(0, ROUNDS) as i:
                for u, c in enumerate(ctx_slots):
                    dve.wait_ge(ctx_high, 4 * i + u + 1)
                    nc.vector.tensor_tensor(c[:, 1, 0:S], ctx_banks[u][0][:, 0:S], c[:, 0, 0:S].bitcast(f32), ALU.subtract)
                    nc.vector.tensor_tensor(c[CL:2 * CL, 2, 0:S], ctx_banks[u][1][0:CL, 0:S],
                                            c[0:CL, 2, 0:S].bitcast(f32), ALU.subtract).then_inc(ctx_split[u], 1)

            with dve.Fori(0, L) as lay:
                split_low([n for n in SHARED["sa"] if n not in LOW_BY_POOL], lay)
                with dve.Fori(0, PAIRS) as pair:
                    it = lay * PAIRS + pair
                    event = lay * (PHASES * PAIRS) + pair + 1
                    nxt = (pair + 1) % PAIRS
                    gcol = 2 * lay + (pair + 1) // PAIRS * (2 * LNV)
                    step = Steps(dve, sa["dve_step"], it * SA_STEPS, SA_STEPS)

                    def sa_negmax(s):
                        dve.wait_ge(sa["s_ready"], it * 8 + s + 1)
                        least(s, SC[s % 2][0:T, 0:4 * T].rearrange("p (c t) -> p c t", c=4), 4) \
                            .then_inc(sa["nb_ready"], 1)

                    ln_stats(step, nxt)
                    ln_norm(nxt, event + 1)
                    for s in range(2):
                        sa_negmax(s)
                    for n in range(4):
                        j = 8 + n
                        dve.wait_ge(sa["v_ready"], PRIME + it * 4 + n + 1)
                        nc.vector.tensor_copy(V[0:T, n // 2, (n % 2) * 512:(n % 2) * 512 + 512], PJ[j % 2][0:T, :]) \
                            .then_inc(sa["pj_done"][j % 2], 1)
                    for s in range(2, 11):
                        if s < 8:
                            sa_negmax(s)
                        g = s - 2
                        if 0 <= g < 8:
                            dve.wait_ge(sa["t_ready"], it * 8 + g + 1)
                            nc.vector.tensor_copy(PT[0:T, g % 2, :], TR[g % 2][0:T, 0:4 * T]) \
                                .then_inc(sa["pt_done"][g % 2], 1)
                        if s == 2:
                            ln_affine_to(gcol, PJ, sa["pj_done"], event)
                        if s == 4:
                            ln_low_part(event)
                        for at, i, j in ((6, 0, 14), (8, 1, 15), (10, 2, 16)):
                            if s == at:
                                dve.wait_ge(sa["ot_high"], it * 4 + i + 1)
                                out_low(i, j % 2, sa["pj_done"])
                        if s in (4, 6, 8, 10):
                            i = (s - 4) // 2
                            dve.wait_ge(sa["o_ready"], it * 4 + i + 1)
                            normalise(step, i, sa["o_done"][i % 2])
                    dve.wait_ge(sa["ot_high"], it * 4 + 4)
                    out_low(3, 1, sa["pj_done"])
                    for b in range(2):
                        dve.wait_ge(sa["y_ready"], PRIME + it * 2 + b + 1)
                        residual(step, 2 * pair + b, SC[b], lay * PHASES, sa["y_done"][b], it + 1)
                    step.close()

                split_low(SHARED["ca"], lay)
                with dve.Fori(0, PAIRS) as pair:
                    it = lay * PAIRS + pair
                    event = lay * (PHASES * PAIRS) + PAIRS + pair + 1
                    nxt = (pair + 1) % PAIRS
                    gcol = 2 * LNV + 2 * lay + (pair + 1) // PAIRS * (2 * LNV)
                    step = Steps(dve, ca["dve_step"], it * CA_STEPS_DVE, CA_STEPS_DVE)
                    ln_stats(step, nxt)
                    ln_norm(nxt, event + 1)
                    for job in CA_ORDER:
                        bk = CA_JOBS.get(job, 0) % 2
                        if job[0] == "v":
                            b, n = job[1], job[2]
                            dve.wait_ge(ca["v_ready"], PRIME + it * 12 + 6 * b + n + 1)
                            vc = (n // 2) * INNER + (n % 2) * 512
                            nc.vector.tensor_copy(V[0:KC, b, vc:vc + 512], PJ[bk][0:KC, :]).then_inc(ca["pj_done"][bk], 1)
                        elif job[0] == "k":
                            hp = job[1]
                            dve.wait_ge(ca["k_high"], it * (2 * HP) + hp + 1)
                            nc.vector.tensor_tensor(Kl[:, hp % 2, :], PJ[bk][:, 0:SP], Kh[:, hp % 2, :].bitcast(f32),
                                                    ALU.subtract).then_inc(ca["pj_done"][bk], 1)
                        elif job[0] == "s":
                            h = job[1]
                            dve.wait_ge(ca["s_ready"], it * (2 * H) + h + 1)
                            least(h, SC[h % 2][0:T, 0:S], 1).then_inc(ca["nb_ready"], 1)
                        elif job[0] == "ln":
                            b0 = CA_JOBS[job] % 2
                            ln_affine_to(gcol, (PJ[b0], PJ[1 - b0]), (ca["pj_done"][b0], ca["pj_done"][1 - b0]), event)
                        elif job[0] == "lnlow":
                            ln_low_part(event)
                        elif job[0] == "pv" and job[1] % 8 == 7:
                            i = job[1] // 8
                            dve.wait_ge(ca["o_ready"], it * 4 + i + 1)
                            normalise(step, i, ca["o_done"][i % 2])
                        elif job[0] == "otlow":
                            dve.wait_ge(ca["ot_high"], it * 4 + job[1] + 1)
                            out_low(job[1], CA_JOBS[("ot", job[1])] % 2, ca["pj_done"])
                        elif job[0] == "y" and job[2][-1] == HP - 1:
                            dve.wait_ge(ca["y_ready"], PRIME + it * 2 + job[1] + 1)
                            residual(step, 2 * pair + job[1], SC[job[1]], lay * PHASES + 1, ca["y_done"][job[1]], it + 1)
                    step.close()

                split_low(SHARED["ff"], lay)
                with dve.Fori(0, PAIRS) as pair:
                    it = lay * PAIRS + pair
                    event = lay * (PHASES * PAIRS) + 2 * PAIRS + pair + 1
                    nxt = (pair + 1) % PAIRS
                    gcol = 4 * LNV + 2 * lay - (pair + 1) // PAIRS * (4 * LNV - 2)
                    step = Steps(dve, ff["dve_step"], it * FF_STEPS, FF_STEPS)
                    ln_stats(step, nxt)
                    for q in range(4):
                        dve.wait_ge(ff["pj_done"][q % 2], PRIME + it * (FF_J // 2) + q // 2 + 1)
                        step(nc.vector.tensor_copy(Gh[:, 2 * q:2 * q + 2, :], Gf[:, 2 * q:2 * q + 2, :]))
                        nc.vector.tensor_tensor(Gl[:, 2 * q:2 * q + 2, :], Gf[:, 2 * q:2 * q + 2, :],
                                                Gh[:, 2 * q:2 * q + 2, :].bitcast(f32), ALU.subtract).then_inc(ff["g_split"], 1)
                        if q == 0:
                            ln_norm(nxt, event + 1)
                    ln_affine_to(gcol, SC, (ff["ln_done"], ff["ln_done"]), event)
                    ln_low_part(event)
                    for b in range(2):
                        dve.wait_ge(ff["y_ready"], PRIME + it * 2 + b + 1)
                        residual(step, 2 * pair + b, OA[b], lay * PHASES + 2, ff["y_done"][b], it + 1)
                    step.close()

            with dve.Fori(0, PAIRS) as pair:
                event = L * (PHASES * PAIRS) + pair + 1
                step = Steps(dve, l1["dve_step"], pair * L1_STEPS, L1_STEPS)
                dve.wait_ge(l1["vectors_in"], 48)
                for b in range(2):
                    for n, ts in enumerate(((0, 1), (2,))):
                        j = 5 + 2 * b + n
                        dve.wait_ge(l1["tok_ready"], pair * 8 + j)
                        for c, t in enumerate(ts):
                            last = nc.vector.tensor_tensor(tok[b][:, t, :], PJ[j % 2][0:KC, c * D:(c + 1) * D], BP[:, :], ALU.add)
                        last.then_inc(l1["pj_done"][j % 2], 1)
                    if b == 0:
                        for h in range(2):
                            dve.wait_ge(l1["s_ready"], pair * 2 + h + 1)
                            negmax(step, h, SC[h][0:T, 0:S], 1, SCALE_OUT).then_inc(l1["nb_ready"], 1)
                ln_stats(step, (pair + 1) % PAIRS)
                ln_norm((pair + 1) % PAIRS, event + 1)
                for b in range(2):
                    dve.wait_ge(l1["o_ready"], pair * 2 + b + 1)
                    step(nc.vector.reciprocal(rinv[:, b, 0:1], rs[:, b, 0:1]))
                    step(nc.vector.tensor_scalar(routed[:, b, :], OA[b][0:T, 0:D], rinv[:, b, 0:1], None, ALU.mult))
                    step(nc.vector.bn_stats(bst[:, b, :], routed[:, b, :]), before_aggr=True)
                    step(nc.vector.bn_aggr(mv[:, b, :], bst[:, b, :]))
                nc.vector.tensor_scalar(vare[:, :], mv[:, :, 1], EPS, None, ALU.add).then_inc(l1["var"], 1)
                dve.wait_ge(l1["rstd"], pair * 2 + 1)
                for b in range(2):
                    nc.vector.tensor_scalar(routed[:, b, :], routed[:, b, :], mv[:, b, 0:1], rstd[:, b:b + 1],
                                            ALU.subtract, ALU.mult).then_inc(l1["norm"], 1)
                for b in range(2):
                    dve.wait_ge(l1["in_ready"], pair * 2 + b + 1)
                    for k in range(2):
                        ins = nc.vector.tensor_scalar(inT[:, k, b * T:(b + 1) * T], TR[b][:, k * T:(k + 1) * T],
                                                      cols[:, k:k + 1], cols[:, 2 + k:3 + k], ALU.mult, ALU.add)
                    ins.then_inc(l1["in_done"], 1)
                dve.wait_ge(l1["in_high"], pair + 1)
                nc.vector.tensor_tensor(inTl, inT, inTh.bitcast(f32), ALU.subtract).then_inc(l1["in_low"], 1)
                pb = pair * (L1_J // 2)
                dve.wait_ge(l1["pj_done"][1], PRIME + pb + 9 // 2 + 1)
                step(nc.vector.tensor_scalar(rT, rT, 0.5, 0.5, ALU.mult, ALU.add))
                step(nc.vector.tensor_tensor(rp, rT, hTf[:, :, :], ALU.mult))
                step(nc.vector.tensor_copy(rph, rp))
                nc.vector.tensor_tensor(rpl, rp, rph.bitcast(f32), ALU.subtract).then_inc(l1["rp_split"], 1)
                dve.wait_ge(l1["pj_done"][0], PRIME + pb + 10 // 2 + 1)
                step(nc.vector.tensor_scalar(uT, uT, 0.5, 0.5, ALU.mult, ALU.add))
                ln_affine_to(2 * L, [TR[b][:, T2:2 * T2] for b in range(2)], (l1["ln_done"], l1["ln_done"]), event)
                ln_low_part(event)
                dve.wait_ge(l1["pj_done"][1], PRIME + pb + 11 // 2 + 1)
                step(nc.vector.tensor_tensor(cT, cT, xT, ALU.subtract))
                step(nc.vector.tensor_tensor(cT, cT, uT, ALU.mult))
                nc.vector.tensor_tensor(nsT, cT, xT, ALU.add).then_inc(l1["ns_done"], 1)
                for b in range(2):
                    dve.wait_ge(l1["out_ready"], pair * 2 + b + 1)
                    nc.vector.tensor_copy(yn[:, b, :], OA[b][0:T, 0:D]).then_inc(l1["out_read"][b], 1)
                    dve.wait_ge(l1["out_read"][b], PRIME + pair + 1)
                    step(nc.vector.bn_stats(bst[:, b, :], yn[:, b, :]), before_aggr=True)
                    step(nc.vector.bn_aggr(mv[:, b, :], bst[:, b, :]))
                nc.vector.tensor_scalar(vare[:, :], mv[:, :, 1], EPS, None, ALU.add).then_inc(l1["var"], 1)
                dve.wait_ge(l1["rstd"], pair * 2 + 2)
                for b in range(2):
                    step(nc.vector.tensor_scalar(yn[:, b, :], yn[:, b, :], mv[:, b, 0:1], rstd[:, b:b + 1],
                                                 ALU.subtract, ALU.mult))
                    step(nc.vector.tensor_tensor(yn[:, b, :], yn[:, b, :], GO[:, 0, :], ALU.mult))
                    dve.wait_ge(l1["y_stored"], PRIME + pair * 32)
                    nc.vector.tensor_tensor(y[:, b, :], yn[:, b, :], GO[:, 1, :], ALU.add).then_inc(l1["y_done"], 1)
                step.close()


def _ca_order():
    order = [("k", 0), ("v", 0, 0), ("v", 0, 1), ("k", 1), ("s", 0), ("s", 1)] + [("v", 0, n) for n in range(2, 6)]
    for s in range(2, 35):
        if s % 2 == 0 and s // 2 + 1 < 16:
            order.append(("k", s // 2 + 1))
        if s - 2 < 32:
            order.append(("t", s - 2))
        if s < 32:
            order.append(("s", s))
        if 0 <= s - 3:
            order.append(("pv", s - 3))
        if 4 <= s < 10:
            order.append(("v", 1, s - 4))
        order += {12: [("ot", 0)], 13: [("otlow", 0)], 20: [("ot", 1)], 21: [("otlow", 1)], 22: [("ln",)],
                  24: [("lnlow",)], 28: [("ot", 2)], 29: [("otlow", 2)], 32: [("y", 0, (0, 1))]}.get(s, [])
    return order + [("y", 0, (2, 3)), ("ot", 3), ("otlow", 3), ("y", 0, (4, 5, 6, 7)), ("y", 1, (0, 1, 2, 3)),
                    ("y", 1, (4, 5, 6, 7))]


def _ca_jobs(order):
    at, n = {}, 4
    for job in order:
        if job[0] in ("v", "k", "ot"):
            at[job] = n
            n += 1
        if job[0] == "ln":
            at[job] = n
            n += 2
    assert n == 38, n
    return at


CA_ORDER = _ca_order()
CA_JOBS = _ca_jobs(CA_ORDER)
SA_STEPS, CA_STEPS_DVE, FF_STEPS, L1_STEPS = 8, 8, 8, 26
PARAM_DMAS = 1 + 6 + 2 + 1 + 6 + 3


def kernel(**inputs):
    import numpy as np
    import concourse.bacc as bacc
    from concourse.bass_utils import run_bass_kernel_spmd

    nc = bacc.Bacc("TRN2", target_bir_lowering=False, num_devices=1)
    arrays, args = {}, []
    for name in INPUTS:
        a = np.ascontiguousarray(inputs[name])
        arrays[name] = a
        args.append(nc.dram_tensor(name, a.shape, mybir.dt.from_np(a.dtype), kind="ExternalInput").ap())
    shape = inputs['x'].shape
    args.append(nc.dram_tensor("out", shape, mybir.dt.float32, kind="ExternalOutput").ap())
    xattn_stack_kernel(nc, *args)
    r = run_bass_kernel_spmd(nc, [arrays], core_ids=[0])
    return r.results[0]["out"]
```
